# Optimizing a Trainium2 kernel written in Bass

```python
import numpy as np
import jax
import jax.numpy as jnp

def _softmax(x, axis=-1):
    return jax.nn.softmax(x, axis=axis)

def _gelu(x):
    return jax.nn.gelu(x, approximate=True)

def _silu(x):
    return jax.nn.silu(x)

def _sigmoid(x):
    return jax.nn.sigmoid(x)

def _layernorm(x, axis=-1, eps=1e-05):
    m = jnp.mean(x, axis=axis, keepdims=True)
    v = jnp.var(x, axis=axis, keepdims=True)
    return (x - m) / jnp.sqrt(v + eps)

def _scatter_add(tgt, idx, src, axis=0):
    return tgt.at[idx].add(src)

def _segment_sum(src, seg, n):
    return jax.ops.segment_sum(src, seg, n)
kernel_name = 'mk_cond_seq_d2_seqx_r2_9f001e'

def setup_inputs(seed: int=0):
    np.random.seed(seed)
    _w = jnp.asarray

    def _rec_inputs():
        import jax
        import jax.numpy as jnp
        _rk = jax.random.key(seed)
        x = 1.648e-05 + 1 * jax.random.normal(jax.random.fold_in(_rk, 1), (8, 512, 512), jnp.float32)
        _lenS = 512 - jax.random.randint(jax.random.fold_in(_rk, 7), (8,), 0, max(1, 512 // 4) + 1, jnp.int32)
        _lenS2 = 512 - jax.random.randint(jax.random.fold_in(_rk, 8), (8,), 0, max(1, 512 // 4) + 1, jnp.int32)
        cond_1024 = 0.00191187 + 0.999416 * jax.random.normal(jax.random.fold_in(_rk, 11), (8, 512), jnp.float32)
        _validS = jnp.arange(512)[None, :] < _lenS[:, None]
        _validS2 = jnp.arange(512)[None, :] < _lenS2[:, None]
        _causal = jnp.tril(jnp.ones((512, 512), dtype=bool))
        mask_BxSxSx11_ik0 = jnp.where(jnp.ones((8, 512, 512, 11), dtype=bool), 0, 1).astype(jnp.int32)
        return (x, cond_1024, mask_BxSxSx11_ik0)
    x, cond_1024, mask_BxSxSx11_ik0 = _rec_inputs()

    def _L0_cond_setup():
        import jax, jax.numpy as jnp
        import numpy as np
        NONGT = 20
        H = 16
        NEG = -9000000000000000.0

        def _gat_attention(self_feat, cond_adj, label_bias, Wq, bq, Wk, bk, Wout, bout):
            B, N, F = self_feat.shape
            ng = min(NONGT, N)
            dh = F // H
            kv = self_feat[:, :ng]
            qh = (self_feat @ Wq.T + bq).reshape(B, N, H, dh)
            kh = (kv @ Wk.T + bk).reshape(B, ng, H, dh)
            aff = jnp.einsum('bnhd,bmhd->bnhm', qh, kh) * (1.0 / np.sqrt(dh))
            mask = cond_adj[:, :, None, :] > 0
            aff = jnp.where(mask, aff, NEG) + label_bias[:, :, None, :]
            w = jax.nn.softmax(aff, axis=-1)
            out_t = jnp.einsum('bnhm,bmf->bnhf', w, kv)
            out = jnp.einsum('bnhf,hgf->bnhg', out_t, Wout) + bout.reshape(H, F // H)
            return out.reshape(B, N, F)

        def _forward(v, q, adj, W_self, b_self, w_bias, b_bias, Wq, bq, Wk, bk, Wout, bout):
            adj_f = adj.astype(jnp.float32)
            exp_v = v
            row_zero = exp_v.sum(-1) == 0
            q_exp = jnp.where(row_zero[..., None], 0.0, q[:, None, :])
            vcq = jnp.concatenate([exp_v, q_exp], axis=-1)
            self_feat = vcq @ W_self.T + b_self
            output = self_feat
            for d in range(2):
                A = adj_f if d == 0 else jnp.swapaxes(adj_f, 1, 2)
                A = A[:, :, :NONGT, :]
                cond = A.sum(-1)
                vb = A @ w_bias + b_bias
                output = output + _gat_attention(self_feat, cond, vb, Wq[d], bq[d], Wk[d], bk[d], Wout[d], bout[d])
            rel = jax.nn.relu(output)
            return exp_v + rel
        key = jax.random.key(seed)
        ks = jax.random.split(key, 8)
        B, N, L, F, Q = (128, 36, 11, 512, 512)
        IN = F + Q
        s = 0.02
        return {'v': jax.random.normal(ks[0], (B, N, F), jnp.float32), 'q': jax.random.normal(ks[1], (B, Q), jnp.float32), 'adj': jax.random.randint(ks[2], (B, N, N, L), 0, 2, jnp.int32), 'W_self': jax.random.normal(ks[3], (F, IN), jnp.float32) * s, 'b_self': jnp.zeros((F,), jnp.float32), 'w_bias': jax.random.normal(ks[4], (L,), jnp.float32) * s, 'b_bias': jnp.zeros((), jnp.float32), 'Wq': jax.random.normal(ks[5], (2, F, F), jnp.float32) * s, 'bq': jnp.zeros((2, F), jnp.float32), 'Wk': jax.random.normal(ks[6], (2, F, F), jnp.float32) * s, 'bk': jnp.zeros((2, F), jnp.float32), 'Wout': jax.random.normal(ks[7], (2, H, F // H, F), jnp.float32) * s, 'bout': jnp.zeros((2, F), jnp.float32)}
    _L0_cond_all = _L0_cond_setup()
    _L0_cond_in = {k: v for k, v in _L0_cond_all.items() if k in ('W_self', 'b_self', 'w_bias', 'b_bias', 'Wq', 'bq', 'Wk', 'bk', 'Wout', 'bout')}
    del _L0_cond_all

    def _L1_cond_setup():
        import jax, jax.numpy as jnp
        import numpy as np
        EPS = 1e-05

        def _sln(h, w, ln_g, ln_b, Wg, bg, Wb, bb):
            mu = jnp.mean(h, axis=-1, keepdims=True)
            var = jnp.mean((h - mu) ** 2, axis=-1, keepdims=True)
            ln = (h - mu) / jnp.sqrt(var + EPS) * ln_g + ln_b
            gamma = (w @ Wg.T + bg)[:, None, :]
            beta = (w @ Wb.T + bb)[:, None, :]
            return gamma * ln + beta
        key = jax.random.key(seed)
        ks = jax.random.split(key, 20)
        B, N, D = (4, 512, 512)
        F = 4 * D
        s = lambda fan: 1.0 / np.sqrt(fan)
        inp = {'hidden': jax.random.normal(ks[0], (B, N, D), jnp.float32), 'w': jax.random.normal(ks[1], (B, D), jnp.float32), 'ln_g': jnp.ones((D,), jnp.float32), 'ln_b': jnp.zeros((D,), jnp.float32), 'Wg': jax.random.normal(ks[2], (D, D), jnp.float32) * s(D), 'bg': jnp.zeros((D,), jnp.float32), 'Wb': jax.random.normal(ks[3], (D, D), jnp.float32) * s(D), 'bb': jnp.zeros((D,), jnp.float32), 'Wqkv': jax.random.normal(ks[4], (3 * D, D), jnp.float32) * s(D), 'bqkv': jnp.zeros((3 * D,), jnp.float32), 'Wp': jax.random.normal(ks[5], (D, D), jnp.float32) * s(D), 'bp': jnp.zeros((D,), jnp.float32), 'W1': jax.random.normal(ks[6], (F, D), jnp.float32) * s(D), 'b1': jnp.zeros((F,), jnp.float32), 'W2': jax.random.normal(ks[7], (D, F), jnp.float32) * s(F), 'b2': jnp.zeros((D,), jnp.float32), 'num_heads': 16}
        return inp
    _L1_cond_all = _L1_cond_setup()
    _L1_cond_in = {k: v for k, v in _L1_cond_all.items() if k in ('ln_g', 'ln_b', 'Wg', 'bg', 'Wb', 'bb', 'Wqkv', 'bqkv', 'Wp', 'bp', 'W1', 'b1', 'W2', 'b2')}
    del _L1_cond_all
    return {'x': x, 'cond_1024': cond_1024, 'mask_BxSxSx11_ik0': mask_BxSxSx11_ik0, 'L0_cond_W_self': _L0_cond_in['W_self'], 'L0_cond_b_self': _L0_cond_in['b_self'], 'L0_cond_w_bias': _L0_cond_in['w_bias'], 'L0_cond_b_bias': _L0_cond_in['b_bias'], 'L0_cond_Wq': _L0_cond_in['Wq'], 'L0_cond_bq': _L0_cond_in['bq'], 'L0_cond_Wk': _L0_cond_in['Wk'], 'L0_cond_bk': _L0_cond_in['bk'], 'L0_cond_Wout': _L0_cond_in['Wout'], 'L0_cond_bout': _L0_cond_in['bout'], 'L1_cond_ln_g': _L1_cond_in['ln_g'], 'L1_cond_ln_b': _L1_cond_in['ln_b'], 'L1_cond_Wg': _L1_cond_in['Wg'], 'L1_cond_bg': _L1_cond_in['bg'], 'L1_cond_Wb': _L1_cond_in['Wb'], 'L1_cond_bb': _L1_cond_in['bb'], 'L1_cond_Wqkv': _L1_cond_in['Wqkv'], 'L1_cond_bqkv': _L1_cond_in['bqkv'], 'L1_cond_Wp': _L1_cond_in['Wp'], 'L1_cond_bp': _L1_cond_in['bp'], 'L1_cond_W1': _L1_cond_in['W1'], 'L1_cond_b1': _L1_cond_in['b1'], 'L1_cond_W2': _L1_cond_in['W2'], 'L1_cond_b2': _L1_cond_in['b2']}

def reference(x, cond_1024, mask_BxSxSx11_ik0, L0_cond_W_self, L0_cond_b_self, L0_cond_w_bias, L0_cond_b_bias, L0_cond_Wq, L0_cond_bq, L0_cond_Wk, L0_cond_bk, L0_cond_Wout, L0_cond_bout, L1_cond_ln_g, L1_cond_ln_b, L1_cond_Wg, L1_cond_bg, L1_cond_Wb, L1_cond_bb, L1_cond_Wqkv, L1_cond_bqkv, L1_cond_Wp, L1_cond_bp, L1_cond_W1, L1_cond_b1, L1_cond_W2, L1_cond_b2):
    import jax
    import jax.numpy as jnp

    def _L0_cond_ref(v, q, adj, W_self, b_self, w_bias, b_bias, Wq, bq, Wk, bk, Wout, bout):
        import jax, jax.numpy as jnp
        import numpy as np
        NONGT = 20
        H = 16
        NEG = -9000000000000000.0

        def _gat_attention(self_feat, cond_adj, label_bias, Wq, bq, Wk, bk, Wout, bout):
            B, N, F = self_feat.shape
            ng = min(NONGT, N)
            dh = F // H
            kv = self_feat[:, :ng]
            qh = (self_feat @ Wq.T + bq).reshape(B, N, H, dh)
            kh = (kv @ Wk.T + bk).reshape(B, ng, H, dh)
            aff = jnp.einsum('bnhd,bmhd->bnhm', qh, kh) * (1.0 / np.sqrt(dh))
            mask = cond_adj[:, :, None, :] > 0
            aff = jnp.where(mask, aff, NEG) + label_bias[:, :, None, :]
            w = jax.nn.softmax(aff, axis=-1)
            out_t = jnp.einsum('bnhm,bmf->bnhf', w, kv)
            out = jnp.einsum('bnhf,hgf->bnhg', out_t, Wout) + bout.reshape(H, F // H)
            return out.reshape(B, N, F)

        def _forward(v, q, adj, W_self, b_self, w_bias, b_bias, Wq, bq, Wk, bk, Wout, bout):
            adj_f = adj.astype(jnp.float32)
            exp_v = v
            row_zero = exp_v.sum(-1) == 0
            q_exp = jnp.where(row_zero[..., None], 0.0, q[:, None, :])
            vcq = jnp.concatenate([exp_v, q_exp], axis=-1)
            self_feat = vcq @ W_self.T + b_self
            output = self_feat
            for d in range(2):
                A = adj_f if d == 0 else jnp.swapaxes(adj_f, 1, 2)
                A = A[:, :, :NONGT, :]
                cond = A.sum(-1)
                vb = A @ w_bias + b_bias
                output = output + _gat_attention(self_feat, cond, vb, Wq[d], bq[d], Wk[d], bk[d], Wout[d], bout[d])
            rel = jax.nn.relu(output)
            return exp_v + rel
        return _forward(v, q, adj, W_self, b_self, w_bias, b_bias, Wq, bq, Wk, bk, Wout, bout)

    def _L1_cond_ref(hidden, w, ln_g, ln_b, Wg, bg, Wb, bb, Wqkv, bqkv, Wp, bp, W1, b1, W2, b2, num_heads):
        import jax, jax.numpy as jnp
        import numpy as np
        EPS = 1e-05

        def _sln(h, w, ln_g, ln_b, Wg, bg, Wb, bb):
            mu = jnp.mean(h, axis=-1, keepdims=True)
            var = jnp.mean((h - mu) ** 2, axis=-1, keepdims=True)
            ln = (h - mu) / jnp.sqrt(var + EPS) * ln_g + ln_b
            gamma = (w @ Wg.T + bg)[:, None, :]
            beta = (w @ Wb.T + bb)[:, None, :]
            return gamma * ln + beta
        B, N, D = hidden.shape
        hd = D // num_heads
        h = _sln(hidden, w, ln_g, ln_b, Wg, bg, Wb, bb)
        qkv = (h @ Wqkv.T + bqkv).reshape(B, N, num_heads, hd, 3)
        q = jnp.moveaxis(qkv[..., 0], 2, 1)
        k = jnp.moveaxis(qkv[..., 1], 2, 1)
        v = jnp.moveaxis(qkv[..., 2], 2, 1)
        energy = jnp.einsum('bhqd,bhkd->bhqk', q, k)
        att = jax.nn.softmax(energy, axis=-1) / D ** 0.5
        out = jnp.einsum('bhqk,bhkd->bhqd', att, v)
        out = jnp.moveaxis(out, 1, 2).reshape(B, N, D)
        out = out @ Wp.T + bp
        h1 = out + hidden
        h2 = _sln(h1, w, ln_g, ln_b, Wg, bg, Wb, bb)
        return h2 + h1
    x = _L0_cond_ref(x, cond_1024, mask_BxSxSx11_ik0, L0_cond_W_self, L0_cond_b_self, L0_cond_w_bias, L0_cond_b_bias, L0_cond_Wq, L0_cond_bq, L0_cond_Wk, L0_cond_bk, L0_cond_Wout, L0_cond_bout)
    x = _L1_cond_ref(x, cond_1024, L1_cond_ln_g, L1_cond_ln_b, L1_cond_Wg, L1_cond_bg, L1_cond_Wb, L1_cond_bb, L1_cond_Wqkv, L1_cond_bqkv, L1_cond_Wp, L1_cond_bp, L1_cond_W1, L1_cond_b1, L1_cond_W2, L1_cond_b2, 16)
    return x

_drawn_inputs = setup_inputs


def setup_inputs(seed=0):
    import zlib

    import numpy as np

    out = dict(_drawn_inputs(seed))
    spreads = {'L0_cond_b_self': (0.0, 0.1),
     'L0_cond_bq': (0.0, 0.1),
     'L0_cond_bk': (0.0, 0.1),
     'L0_cond_bout': (0.0, 0.1),
     'L1_cond_ln_g': (1.0, 0.2),
     'L1_cond_ln_b': (0.0, 0.1),
     'L1_cond_bg': (0.0, 0.1),
     'L1_cond_bb': (0.0, 0.1),
     'L1_cond_bqkv': (0.0, 0.8),
     'L1_cond_bp': (0.0, 0.1),
     'L1_cond_b1': (0.0, 0.1),
     'L1_cond_b2': (0.0, 0.1)}
    factors = {}
    for name, (base, spread) in spreads.items():
        noise = np.random.default_rng([zlib.crc32(name.encode()), seed]).standard_normal(out[name].shape)
        drawn = base * np.exp(spread * noise) if base else spread * noise
        out[name] = jnp.asarray(drawn.astype(out[name].dtype))
    for name, factor in factors.items():
        out[name] = (out[name] * factor).astype(out[name].dtype)
    return out
```

```python
from contextlib import ExitStack

import concourse.bass as bass
from concourse import mybir

F32 = mybir.dt.float32
F32R = mybir.dt.float32r
I32 = mybir.dt.int32
ALU = mybir.AluOpType
ACT = mybir.ActivationFunctionType
AX = mybir.AxisListType.X

P = 128
B, N, D = 8, 512, 512
H = 16
DH = D // H
L = 11
NK = 20
MP = 32
FC = D // P
NT = N // P
HC = P // DH
HK = H * NK
CK = HC * NK
NEG = -9000000000000000.0
EPS = 1e-5
ds = bass.ds


def sems(nc, ctx, names):
    return {n: ctx.enter_context(nc.semaphore(n)) for n in names.split()}


def mm3(nc, out, ah, al, bh, bl, start, stop):
    nc.tensor.matmul(out, ah, bh, start=start, stop=False)
    nc.tensor.matmul(out, ah, bl, start=False, stop=False)
    return nc.tensor.matmul(out, al, bh, start=False, stop=stop)


def prologue(nc, t, d):
    with ExitStack() as ctx:
        def sb(name, shape, dt=F32):
            return ctx.enter_context(nc.sbuf_tensor(name, shape, dt))

        cond64 = sb("cond64", [P, FC, 64])
        wself_raw = sb("wself_raw", [P, 2 * FC, D])
        wg = sb("wg", [P, FC, D])
        wb = sb("wb", [P, FC, D])
        x20 = sb("x20", [P, FC, B * MP])
        bg8, bb8, lng8, lnb8 = (sb(n, [B, D]) for n in ("bg8", "bb8", "lng8", "lnb8"))
        gam8, gs8, bt8, bs8 = (sb(n, [B, D]) for n in ("gam8", "gs8", "bt8", "bs8"))
        wk = sb("wk", [P, 2, FC, D])
        wq = sb("wq", [P, 2, FC, D])
        wout = sb("wout", [P, 2, FC, D])
        bk = sb("bk", [P, 2, FC])
        bout2 = sb("bout2", [P, 2, FC])
        bq64 = sb("bq64", [P, 2, FC, 64])
        hot20 = sb("hot20", [64, B * MP])
        ones64 = sb("ones64", [P, 64])
        z20 = sb("z20", [64, B * MP], F32R)
        sf20 = sb("sf20", [P, FC, B * MP])
        kdiag = sb("kdiag", [P, FC, B, CK])
        mout = sb("mout", [P, 2, B, HK])
        vparts = sb("vparts", [P, 2, 2, D], F32R)
        lo_tmp = sb("lo_tmp", [64, 2, 4 * CK], F32R)
        bank = ctx.enter_context(nc.psum_tensor("p_bank", [P, 8, 512], F32))

        s = sems(nc, ctx, "ld_small ld_const bout_done ld_wself ld_x20 ld_gb ld_wk ld_wq ld_wout ld_hot zeroed cond_in bq_in "
                          "sq_ready sq_hi sq_split rs_ready z_ready gb_ready gb_step sf_ready sf_done "
                          "kh_ready kdiag_done v_ready v_hi v_done m_ready m_done_dve m_done_act "
                          "bias_ready bias_hi bias_done w1_hi w1_split st_gb st_v st_m0 st_m1")
        block = ctx.enter_context(nc.Block())

        @block.sync
        def _(sp):
            sp.wait_ge(s["zeroed"], 1)
            sp.dma_start(cond64[:, :, :], d["cond64"]).then_inc(s["cond_in"], 16)
            sp.dma_start(wself_raw[:, :, :], d["wself_t"].rearrange("(c p) o -> p c o", p=P)).then_inc(s["ld_wself"], 16)
            for c in range(FC):
                sp.dma_start(x20[:, c, :].rearrange("p (b m) -> p b m", b=B)[:, :, 0:NK],
                             d["x_t"][:, :, c, 0:NK].rearrange("b p m -> p b m")).then_inc(s["ld_x20"], 16)
            sp.dma_start(hot20[:, :], d["hot20"]).then_inc(s["ld_hot"], 16)
            sp.dma_start(wk[:, :, :, :], d["wk_t"].rearrange("e (c p) o -> p e c o", p=P)).then_inc(s["ld_wk"], 16)
            sp.dma_start(wq[:, :, :, :], d["wq"].rearrange("e (c p) o -> p e c o", p=P)).then_inc(s["ld_wq"], 16)
            sp.dma_start(wout[:, :, :, :], d["wout_t"].rearrange("e (c p) o -> p e c o", p=P)).then_inc(s["ld_wout"], 16)
            sp.dma_start(wg[:, :, :], d["wg_t"].rearrange("(c p) o -> p c o", p=P)).then_inc(s["ld_gb"], 16)
            sp.dma_start(wb[:, :, :], d["wb_t"].rearrange("(c p) o -> p c o", p=P)).then_inc(s["ld_gb"], 16)
            for e in range(2):
                for g in range(2):
                    sp.wait_ge(s["v_done"], 2 * e + g + 1)
                    for part in range(2):
                        sp.dma_start(d["v_rows"][part, e, g * P:(g + 1) * P, :],
                                     vparts[:, g, part, :].bitcast(F32)).then_inc(s["st_v"], 16)
                for f in range(FC):
                    i = FC * e + f
                    sp.wait_ge(s["m_done_dve"], FC * (i + 1))
                    sp.wait_ge(s["m_done_act"], FC * (i + 1))
                    sp.dma_start(d["m_rows"][:, :, f, e, :].rearrange("b p k -> p b k"),
                                 mout[:, i % 2, :, :]).then_inc((s["st_m0"], s["st_m1"])[i % 2], 16)
            sp.wait_ge(s["gb_step"], 6)
            sp.dma_start(d["gb_rows"][:, 0, :], gs8[:, :]).then_inc(s["st_gb"], 16)
            sp.dma_start(d["gb_rows"][:, 1, :], bs8[:, :]).then_inc(s["st_gb"], 16)
            sp.wait_ge(s["st_gb"], 32)
            sp.wait_ge(s["st_v"], 16 * 8)
            sp.wait_ge(s["st_m0"], 16 * FC)
            sp.wait_ge(s["st_m1"], 16 * FC)

        @block.gpsimd
        def _(pool):
            nc.gpsimd.memset(x20[:, :, :], 0.0).then_inc(s["zeroed"], 1)
            nc.gpsimd.memset(ones64[:, :], 1.0).then_inc(s["zeroed"], 1)
            nc.gpsimd.memset(kdiag[:, :, :, :], 0.0).then_inc(s["zeroed"], 1)
            pool.wait_ge(s["w1_hi"], 1)
            nc.gpsimd.tensor_tensor(t["w1l"][:, :, :], wself_raw[:, 0:FC, :], t["w1h"][:, :, :].bitcast(F32),
                                    ALU.subtract).then_inc(s["w1_split"], 1)

        @block.scalar
        def _(act):
            act.dma_start(bq64[:, :, :, :], d["bq64"]).then_inc(s["bq_in"], 16)
            act.dma_start(t["bself"][:, :], d["b_self"]).then_inc(s["ld_const"], 16)
            act.dma_start(bout2[:, :, :], d["bout"]).then_inc(s["ld_const"], 16)
            act.dma_start(t["ident"][:, :], d["ident"]).then_inc(s["ld_const"], 16)
            act.dma_start(t["hot"][:, :], d["hot"]).then_inc(s["ld_const"], 16)
            act.dma_start(t["wbias"][:, :], d["w_bias"].partition_broadcast(P)).then_inc(s["ld_const"], 16)
            act.dma_start(t["bbias"][:, :], d["b_bias"].partition_broadcast(P)).then_inc(s["ld_const"], 16)
            act.dma_start(bk[:, :, :], d["bk"]).then_inc(s["ld_small"], 16)
            for row, src in ((bg8, d["bg"]), (bb8, d["bb"]), (lng8, d["ln_g"]), (lnb8, d["ln_b"])):
                act.dma_start(row[:, :], src.partition_broadcast(B)).then_inc(s["ld_small"], 16)
            act.wait_ge(s["ld_const"], 16 * 6)
            for o in range(FC):
                act.wait_ge(s["sf_ready"], o + 1)
                nc.scalar.activation(sf20[:, o, :], bank[:, 4 + o, 0:B * MP], ACT.Identity,
                                     bias=t["bself"][:, o:o + 1]).then_inc(s["sf_done"], 1)
            for i in range(2 * FC):
                if i >= 2:
                    act.wait_ge((s["st_m0"], s["st_m1"])[i % 2], 16 * (i // 2))
                for h in range(FC):
                    act.wait_ge(s["m_ready"], 2 * (FC * i + h) + 2)
                    nc.scalar.activation(mout[:, i % 2, 4:8, h * CK:(h + 1) * CK],
                                         bank[:, 2 * (h % 2) + 1, 0:4 * CK].rearrange("p (b k) -> p b k", b=4),
                                         ACT.Copy).then_inc(s["m_done_act"], 1)

        @block.vector
        def _(dve):
            dve.wait_ge(s["sq_ready"], 1)
            nc.vector.tensor_copy(t["sq"][:, :], bank[0:64, 0, :]).then_inc(s["sq_hi"], 1)
            dve.wait_ge(s["sq_hi"], 1)
            nc.vector.tensor_tensor(t["sq"][32:64, :], bank[32:64, 0, :], t["sq"][32:64, :].bitcast(F32),
                                    ALU.subtract).then_inc(s["sq_split"], 1)
            dve.wait_ge(s["rs_ready"], 1)
            dve.wait_ge(s["ld_hot"], 16)
            nc.vector.scalar_tensor_tensor(z20[:, :], bank[0:64, 1, 0:B * MP], 0.0, hot20[:, :],
                                           ALU.not_equal, ALU.mult).then_inc(s["z_ready"], 1)
            dve.wait_ge(s["ld_wself"], 16)
            nc.vector.tensor_copy(t["w1h"][:, :, :], wself_raw[:, 0:FC, :]).then_inc(s["w1_hi"], 1)
            dve.wait_ge(s["ld_const"], 16 * 6)
            nc.vector.tensor_tensor(t["boutc"][:, :], bout2[:, 0, :], bout2[:, 1, :], ALU.add).then_inc(s["bout_done"], 1)
            dve.wait_ge(s["ld_small"], 16 * 5)
            for e in range(2):
                if e == 1:
                    dve.wait_ge(s["bias_ready"], 2 * FC)
                for h in range(FC):
                    dve.wait_ge(s["kh_ready"], FC * e + h + 1)
                    dve.wait_ge(s["zeroed"], 3)
                    src = bank[:, h % 2 + 4, 0:B * MP].rearrange("p (b m) -> p b m", b=B)
                    for j in range(HC):
                        r = slice(DH * j, DH * j + DH)
                        nc.vector.tensor_scalar(kdiag[r, h, :, NK * j:NK * j + NK], src[r, :, 0:NK],
                                                bk[r, e, h:h + 1], float(DH) ** -0.5,
                                                ALU.add, ALU.mult).then_inc(s["kdiag_done"], 1)
                for g in range(2):
                    n = 2 * e + g
                    dve.wait_ge(s["v_ready"], n + 1)
                    if e == 1:
                        dve.wait_ge(s["st_v"], 16 * 2 * 2)
                    nc.vector.tensor_copy(vparts[:, g, 0, :], bank[:, 6 + g, :]).then_inc(s["v_hi"], 1)
                    dve.wait_ge(s["v_hi"], n + 1)
                    nc.vector.tensor_tensor(vparts[:, g, 1, :], bank[:, 6 + g, :],
                                            vparts[:, g, 0, :].bitcast(F32), ALU.subtract).then_inc(s["v_done"], 1)
                for f in range(FC):
                    i = FC * e + f
                    if i >= 2:
                        dve.wait_ge((s["st_m0"], s["st_m1"])[i % 2], 16 * (i // 2))
                    for h in range(FC):
                        dve.wait_ge(s["m_ready"], 2 * (FC * i + h) + 1)
                        nc.vector.tensor_copy(mout[:, i % 2, 0:4, h * CK:(h + 1) * CK],
                                              bank[:, 2 * (h % 2), 0:4 * CK].rearrange("p (b k) -> p b k", b=4)
                                              ).then_inc(s["m_done_dve"], 1)
                for h in range(FC):
                    for half in range(2):
                        n = 2 * (FC * e + h) + half
                        dve.wait_ge(s["bias_ready"], n + 1)
                        src = bank[:, 4 + n % 2, 0:4 * CK].rearrange("p (b k) -> p b k", b=4)
                        dst = t["bias_rows"][:, 4 * half:4 * half + 4, e, h * CK:(h + 1) * CK]
                        nc.vector.tensor_copy(dst[0:64], src[0:64]).then_inc(s["bias_hi"], 1)
                        dve.wait_ge(s["bias_hi"], n + 1)
                        nc.vector.tensor_tensor(dst[32:64], src[32:64], dst[32:64].bitcast(F32),
                                                ALU.subtract).then_inc(s["bias_done"], 1)
            dve.wait_ge(s["gb_ready"], 2)
            nc.vector.tensor_tensor(gam8[:, :], bank[0:B, 2, :], bg8[:, :], ALU.add).then_inc(s["gb_step"], 1)
            nc.vector.tensor_tensor(bt8[:, :], bank[0:B, 3, :], bb8[:, :], ALU.add).then_inc(s["gb_step"], 1)
            dve.wait_ge(s["gb_step"], 2)
            nc.vector.tensor_tensor(gs8[:, :], gam8[:, :], lng8[:, :], ALU.mult).then_inc(s["gb_step"], 1)
            dve.wait_ge(s["gb_step"], 3)
            nc.vector.tensor_tensor(gam8[:, :], gam8[:, :], lnb8[:, :], ALU.mult).then_inc(s["gb_step"], 1)
            dve.wait_ge(s["gb_step"], 4)
            nc.vector.tensor_tensor(bs8[:, :], gam8[:, :], bt8[:, :], ALU.add).then_inc(s["gb_step"], 2)

        @block.tensor
        def _(pe):
            pe.wait_ge(s["cond_in"], 16)
            pe.wait_ge(s["ld_wself"], 16)
            for f in range(FC):
                last = nc.tensor.matmul(bank[0:64, 0, :], cond64[:, f, :], wself_raw[:, FC + f, :],
                                        start=f == 0, stop=f == FC - 1)
            last.then_inc(s["sq_ready"], 1)
            pe.wait_ge(s["ld_x20"], 16 * FC)
            pe.wait_ge(s["zeroed"], 2)
            for f in range(FC):
                last = nc.tensor.matmul(bank[0:64, 1, 0:B * MP], ones64[:, :], x20[:, f, :],
                                        start=f == 0, stop=f == FC - 1)
            last.then_inc(s["rs_ready"], 1)
            pe.wait_ge(s["z_ready"], 1)
            pe.wait_ge(s["sq_split"], 1)
            for o in range(FC):
                out = bank[:, 4 + o, 0:B * MP]
                nc.tensor.matmul(out, t["sq"][:, o * P:(o + 1) * P], z20[:, :], start=True, stop=False)
                for f in range(FC):
                    last = nc.tensor.matmul(out, wself_raw[:, f, o * P:(o + 1) * P], x20[:, f, :],
                                            start=False, stop=f == FC - 1)
                last.then_inc(s["sf_ready"], 1)
            pe.wait_ge(s["ld_wk"], 16)
            pe.wait_ge(s["ld_wout"], 16)
            pe.wait_ge(s["ld_wq"], 16)
            pe.wait_ge(s["bq_in"], 16)
            pe.wait_ge(s["sf_done"], FC)
            for e in range(2):
                if e == 1:
                    pe.wait_ge(s["bias_done"], 2 * FC)
                for h in range(FC):
                    if h >= 2:
                        pe.wait_ge(s["kdiag_done"], HC * (FC * e + h - 1))
                    for f in range(FC):
                        last = nc.tensor.matmul(bank[:, 4 + h % 2, 0:B * MP], wk[:, e, f, h * P:(h + 1) * P],
                                                sf20[:, f, :], start=f == 0, stop=f == FC - 1)
                    last.then_inc(s["kh_ready"], 1)
                for g in range(2):
                    if e == 1:
                        pe.wait_ge(s["v_done"], g + 1)
                    for f in range(FC):
                        last = nc.tensor.matmul(bank[:, 6 + g, :], sf20[:, f, g * P:(g + 1) * P], wout[:, e, f, :],
                                                start=f == 0, stop=f == FC - 1)
                    last.then_inc(s["v_ready"], 1)
                pe.wait_ge(s["kdiag_done"], HC * FC * (e + 1))
                for f in range(FC):
                    for h in range(FC):
                        k = FC * (FC * e + f) + h
                        if k == 0:
                            pe.wait_ge(s["z_ready"], 1)
                        if k >= 2:
                            pe.wait_ge(s["m_done_dve"], k - 1)
                            pe.wait_ge(s["m_done_act"], k - 1)
                        for half in range(2):
                            nc.tensor.matmul(bank[:, 2 * (h % 2) + half, 0:4 * CK], wq[:, e, h, f * P:(f + 1) * P],
                                             kdiag[:, h, 4 * half:4 * half + 4, :], start=True, stop=True
                                             ).then_inc(s["m_ready"], 1)
                for h in range(FC):
                    for half in range(2):
                        n = 2 * (FC * e + h) + half
                        if n % 8 >= 2:
                            pe.wait_ge(s["bias_done"], n - 1)
                        last = nc.tensor.matmul(bank[0:64, 4 + n % 2, 0:4 * CK], bq64[:, e, h, :],
                                                kdiag[:, h, 4 * half:4 * half + 4, :], start=True, stop=True)
                        last.then_inc(s["bias_ready"], 1)
            pe.wait_ge(s["m_done_dve"], 2 * FC * FC)
            pe.wait_ge(s["m_done_act"], 2 * FC * FC)
            pe.wait_ge(s["ld_gb"], 32)
            for k, w in enumerate((wg, wb)):
                for f in range(FC):
                    last = nc.tensor.matmul(bank[0:B, 2 + k, :], cond64[:, f, 0:B], w[:, f, :],
                                            start=f == 0, stop=f == FC - 1)
                last.then_inc(s["gb_ready"], 1)


def graph(nc, t, d):
    with ExitStack() as ctx:
        def sb(name, shape, dt=F32):
            return ctx.enter_context(nc.sbuf_tensor(name, shape, dt))

        xraw = sb("xraw", [P, FC, N])
        xh, xl = sb("xh", [P, FC, N], F32R), sb("xl", [P, FC, N], F32R)
        xn = sb("xn", [P, NT, D])
        adj = sb("adj", [P, NT * 2 * NK, L], I32)
        adjw = sb("adjw", [P, NT * 2 * NK, L])
        cnt, vb, mask, blocked, cadd = (sb(n, [P, NT, 2, NK]) for n in ("cnt", "vb", "mask", "blocked", "cadd"))
        m = sb("m", [P, FC, 2, HK])
        vdiag = sb("vdiag", [CK, 2, 2, FC, P], F32R)
        z = sb("z", [64, N], F32R)
        sf = sb("sf", [P, FC, N])
        ot = sb("ot", [P, FC, N])
        e = sb("e", [P, NT, 2, H, NK])
        mx, sm, rc = (sb(n, [P, NT, 2 * H]) for n in ("mx", "sm", "rc"))
        wth, wtl = sb("wth", [CK, 2, N], F32R), sb("wtl", [CK, 2, N], F32R)
        st = sb("st", [P, NT, 6])
        mv = sb("mv", [P, NT, 2])
        ve, rstd, mhalf = sb("ve", [P, NT]), sb("rstd", [P, NT]), sb("mhalf", [P, NT])
        ln = sb("ln", [P, NT, D])
        hout = sb("hout", [P, FC, N])
        gcol, bcol = sb("gcol", [P, FC, B]), sb("bcol", [P, FC, B])
        onesr = sb("onesr", [64, P], F32R)
        ones64 = sb("g_ones64", [P, 64])
        bank = ctx.enter_context(nc.psum_tensor("g_bank", [P, 8, 512], F32))

        s = sems(nc, ctx, "x_t_in x_in adj_in m_in v_in gb_in set_up xh_done xl_done rs_ready z_done sf_ready "
                          "sf_done adj_step sc_ready mult_done add_done mx_done sub_done exp_done sum_done "
                          "rc_done w_done wtr_ready wh_done wl_done att_mm att_done back_ready h_done "
                          "st_done mv_done ve_done rstd_done ln_done lnt_ready lnt_done h_stored t_stored")
        block = ctx.enter_context(nc.Block())

        def heads(x):
            return x.unsqueeze(2).broadcast_to([P, 2, H, NK])

        def keys(x):
            return x.unsqueeze(2).broadcast_to([P, 2 * H, NK])

        @block.sync
        def _(sp):
            for c in range(FC):
                for k, dst in enumerate((gcol, bcol)):
                    sp.dma_start(dst[:, c, :], d["gb_rows"][:, k, c * P:(c + 1) * P].rearrange("b p -> p b"),
                                 allow_slow_non_contiguous=True).then_inc(s["gb_in"], 16)
            sp.wait_ge(s["set_up"], 2)

            def load_first(b):
                sp.dma_start(xraw[:, :, :], d["x_t"][ds(b, 1)].rearrange("o p c n -> (o p) c n")).then_inc(s["x_t_in"], 16)

            def load_adj(b):
                sp.dma_start(adj[:, :, :], d["adj"][ds(b, 1)].rearrange("o p k l -> (o p) k l")).then_inc(s["adj_in"], 16)

            def load_m(b):
                sp.dma_start(m[:, :, :, :], d["m_rows"][ds(b, 1)].rearrange("o p c e k -> (o p) c e k")).then_inc(s["m_in"], 16)

            def load_v(b):
                for part in range(2):
                    for dr in range(2):
                        for j in range(HC):
                            sp.dma_start(
                                vdiag[NK * j:NK * j + NK, part, dr, :, DH * j:DH * j + DH].bitcast(F32),
                                d["v_rows"][part, dr, ds(b * MP, NK), :].rearrange(
                                    "m (c j g) -> m c j g", c=FC, j=HC)[:, :, j, :]).then_inc(s["v_in"], 16)

            def load_x(b):
                sp.dma_start(xn[:, :, :], d["x"][ds(b, 1)].rearrange("o (t p) f -> (o p) t f", p=P)).then_inc(s["x_in"], 16)

            def stores(b, at):
                sp.wait_ge(s["h_done"], at[0])
                sp.dma_start(d["h_rows"][ds(b, 1)].rearrange("o p t f -> (o p) t f"), xn[:, :, :]).then_inc(s["h_stored"], 16)
                sp.wait_ge(s["lnt_done"], at[0])
                sp.dma_start(d["t_rows"][ds(b, 1)].rearrange("o p c n -> (o p) c n"), hout[:, :, :]).then_inc(s["t_stored"], 16)

            load_first(0)
            load_adj(0)
            load_m(0)
            load_v(0)
            load_x(0)
            def step(b):
                const = isinstance(b, int)
                four, one16, eight = (b * k if const else sp.snap(b * k) for k in (4, 16, 8))
                prev = b - 1 if const else sp.snap(b - 1)
                sp.wait_ge(s["rs_ready"], b)
                sp.wait_ge(s["xl_done"], b)
                load_first(b)
                sp.wait_ge(s["adj_step"], 6 * b)
                load_adj(b)
                sp.wait_ge(s["sc_ready"], four)
                load_m(b)
                sp.wait_ge(s["att_mm"], eight)
                load_v(b)
                stores(prev, (four,))
                sp.wait_ge(s["h_stored"], one16)
                sp.wait_ge(s["ln_done"], four)
                load_x(b)

            step(1)
            with sp.Fori(2, B) as b:
                step(b)
            stores(B - 1, (4 * B,))
            sp.wait_ge(s["h_stored"], 16 * B)
            sp.wait_ge(s["t_stored"], 16 * B)

        @block.gpsimd
        def _(pool):
            nc.gpsimd.memset(vdiag[:, :, :, :, :].bitcast(F32), 0.0).then_inc(s["set_up"], 1)
            nc.gpsimd.memset(onesr[:, :].bitcast(F32), 1.0).then_inc(s["set_up"], 1)
            nc.gpsimd.memset(ones64[:, :], 1.0).then_inc(s["set_up"], 1)
            nc.gpsimd.memset(mhalf[:, :], -0.5).then_inc(s["set_up"], 1)

            def front(b):
                pool.wait_ge(s["xh_done"], b + 1)
                pool.wait_ge(s["sf_ready"], 4 * b)
                nc.gpsimd.tensor_tensor(xl[:, :, :], xraw[:, :, :], xh[:, :, :].bitcast(F32),
                                        ALU.subtract).then_inc(s["xl_done"], 1)

            def softmax(b):
                for i in range(NT + 2):
                    if i < NT:
                        pool.wait_ge(s["mult_done"], 4 * b + i + 1)
                        nc.gpsimd.tensor_tensor(e[:, i], e[:, i], heads(cadd[:, i]), ALU.add).then_inc(s["add_done"], 1)
                    if i >= 2:
                        pool.wait_ge(s["rc_done"], 4 * b + i - 1)
                        pool.wait_ge(s["exp_done"], 4 * b + i - 1)
                        v = e[:, i - 2].rearrange("p e h k -> p (e h) k")
                        nc.gpsimd.tensor_tensor(v, v, keys(rc[:, i - 2]), ALU.mult).then_inc(s["w_done"], 1)

            def back(b):
                pool.wait_ge(s["ve_done"], 2 * b + 2)
                nc.gpsimd.tensor_tensor(rstd[:, :], ve[:, :], mhalf[:, :], ALU.pow).then_inc(s["rstd_done"], 1)

            pool.wait_ge(s["set_up"], 4)
            front(0)
            softmax(0)
            def step(b):
                front(b)
                back(b - 1)
                softmax(b)

            step(1)
            with pool.Fori(2, B) as b:
                step(b)
            back(B - 1)

        @block.scalar
        def _(act):
            act.wait_ge(s["gb_in"], 16 * 2 * FC)

            def self_features(b):
                for o in range(FC):
                    act.wait_ge(s["sf_ready"], 4 * b + o + 1)
                    act.wait_ge(s["att_done"], 4 * b)
                    nc.scalar.activation(sf[:, o, :], bank[:, (o + 1) % 2, :], ACT.Identity,
                                         bias=t["bself"][:, o:o + 1]).then_inc(s["sf_done"], 1)

            def exps(b):
                for i in range(NT):
                    act.wait_ge(s["sub_done"], 4 * b + i + 1)
                    nc.scalar.activation(e[:, i], e[:, i], ACT.Exp).then_inc(s["exp_done"], 1)

            def weights_t(b):
                for i in range(2 * FC):
                    act.wait_ge(s["wtr_ready"], 8 * b + i + 1)
                    act.wait_ge(s["att_mm"], 8 * b + max(i - 1, 0))
                    nc.scalar.activation(wth[:, i % 2, :], bank[0:CK, 6 + i % 2, :], ACT.Copy).then_inc(s["wh_done"], 1)

            def scale_ln(b, prev16):
                act.wait_ge(s["t_stored"], prev16)
                for f in range(FC):
                    act.wait_ge(s["lnt_ready"], 4 * b + f + 1)
                    nc.scalar.activation(hout[:, f, :], bank[:, 6 + f % 2, :], ACT.Identity,
                                         bias=bcol[:, f, ds(b, 1)], scale=gcol[:, f, ds(b, 1)]).then_inc(s["lnt_done"], 1)

            self_features(0)
            exps(0)
            def step(b):
                weights_t(b - 1)
                self_features(b)
                scale_ln(b - 1, 16 * b - 16)
                exps(b)

            step(1)
            with act.Fori(2, B) as b:
                step(b)
            weights_t(B - 1)
            scale_ln(B - 1, 16 * B - 16)

        @block.vector
        def _(dve):
            def front(b):
                dve.wait_ge(s["x_t_in"], 16 * b + 16)
                dve.wait_ge(s["sf_ready"], 4 * b)
                nc.vector.tensor_copy(xh[:, :, :], xraw[:, :, :]).then_inc(s["xh_done"], 1)

            def nonzero_rows(b):
                dve.wait_ge(s["rs_ready"], b + 1)
                dve.wait_ge(s["sf_ready"], 4 * b)
                nc.vector.tensor_scalar(z[:, :], bank[0:64, 0, :], 0.0, t["hot"][:, ds(b, 1)],
                                        ALU.not_equal, ALU.mult).then_inc(s["z_done"], 1)

            def labels(b):
                dve.wait_ge(s["adj_in"], 16 * b + 16)
                dve.wait_ge(s["w_done"], 4 * b)
                flat = "p t e k -> p (t e k)"
                wl = t["wbias"][:, :].unsqueeze(1).broadcast_to([P, NT * 2 * NK, L])
                nc.vector.tensor_tensor(adjw[:, :, :], adj[:, :, :], wl, ALU.mult).then_inc(s["adj_step"], 1)
                nc.vector.tensor_reduce(cnt[:].rearrange(flat), adj[:, :, :], AX, ALU.add).then_inc(s["adj_step"], 1)
                dve.wait_ge(s["adj_step"], 6 * b + 1)
                nc.vector.tensor_reduce(vb[:].rearrange(flat), adjw[:, :, :], AX, ALU.add).then_inc(s["adj_step"], 1)
                dve.wait_ge(s["adj_step"], 6 * b + 2)
                nc.vector.tensor_scalar(mask[:].rearrange(flat), cnt[:].rearrange(flat), 0.0, None,
                                        ALU.is_gt).then_inc(s["adj_step"], 1)
                nc.vector.tensor_scalar(blocked[:].rearrange(flat), cnt[:].rearrange(flat), 0.0, NEG,
                                        ALU.is_le, ALU.mult).then_inc(s["adj_step"], 1)
                dve.wait_ge(s["adj_step"], 6 * b + 5)
                nc.vector.scalar_tensor_tensor(cadd[:].rearrange(flat), vb[:].rearrange(flat), t["bbias"][:, 0:1],
                                               blocked[:].rearrange(flat), ALU.add, ALU.add).then_inc(s["adj_step"], 1)

            def softmax(b):
                dve.wait_ge(s["adj_step"], 6 * b + 6)
                dve.wait_ge(s["wtr_ready"], 8 * b)
                for i in range(NT + 2):
                    if i < NT:
                        dve.wait_ge(s["sc_ready"], 4 * b + i + 1)
                        sc = bank[:, 2 + 2 * (i % 2):4 + 2 * (i % 2), 0:HK].rearrange("p e (h k) -> p e h k", h=H)
                        nc.vector.tensor_tensor(e[:, i], sc, heads(mask[:, i]), ALU.mult).then_inc(s["mult_done"], 1)
                    if 1 <= i <= NT:
                        v = e[:, i - 1].rearrange("p e h k -> p (e h) k")
                        dve.wait_ge(s["add_done"], 4 * b + i)
                        nc.vector.tensor_reduce(mx[:, i - 1], v, AX, ALU.max).then_inc(s["mx_done"], 1)
                        dve.wait_ge(s["mx_done"], 4 * b + i)
                        nc.vector.tensor_tensor(v, v, keys(mx[:, i - 1]), ALU.subtract).then_inc(s["sub_done"], 1)
                    if i >= 2:
                        v = e[:, i - 2].rearrange("p e h k -> p (e h) k")
                        dve.wait_ge(s["exp_done"], 4 * b + i - 1)
                        nc.vector.tensor_reduce(sm[:, i - 2], v, AX, ALU.add).then_inc(s["sum_done"], 1)
                        dve.wait_ge(s["sum_done"], 4 * b + i - 1)
                        nc.vector.reciprocal(rc[:, i - 2], sm[:, i - 2]).then_inc(s["rc_done"], 1)

            def attention(b):
                dve.wait_ge(s["sf_done"], 4 * b + 4)
                dve.wait_ge(s["back_ready"], 4 * b)
                for i in range(2 * FC + 1):
                    if i < 2 * FC:
                        dve.wait_ge(s["wh_done"], 8 * b + i + 1)
                        nc.vector.tensor_tensor(wtl[:, i % 2, :], bank[0:CK, 6 + i % 2, :],
                                                wth[:, i % 2, :].bitcast(F32), ALU.subtract).then_inc(s["wl_done"], 1)
                    if i >= 2 and i % 2 == 0:
                        c = i // 2 - 1
                        dve.wait_ge(s["att_mm"], 8 * b + 2 * c + 2)
                        nc.vector.scalar_tensor_tensor(ot[:, c, :], bank[:, (c + 1) % 2, :], t["boutc"][:, c:c + 1],
                                                       sf[:, c, :], ALU.add, ALU.add).then_inc(s["att_done"], 1)

            def residual_ln(b):
                dve.wait_ge(s["x_in"], 16 * b + 16)
                dve.wait_ge(s["lnt_ready"], 4 * b)
                for i in range(NT):
                    dve.wait_ge(s["back_ready"], 4 * b + i + 1)
                    nc.vector.scalar_tensor_tensor(xn[:, i, :], bank[:, 6 + i % 2, :], 0.0, xn[:, i, :],
                                                   ALU.max, ALU.add).then_inc(s["h_done"], 1)
                for i in range(NT):
                    dve.wait_ge(s["h_done"], 4 * b + i + 1)
                    if i:
                        dve.wait_ge(s["st_done"], 4 * b + i)
                    nc.vector.bn_stats(st[:, i, :], xn[:, i, :]).then_inc(s["st_done"], 1)
                    if i:
                        nc.vector.bn_aggr(mv[:, i - 1, :], st[:, i - 1, :]).then_inc(s["mv_done"], 1)
                dve.wait_ge(s["st_done"], 4 * b + NT)
                dve.wait_ge(s["mv_done"], 4 * b + NT - 1)
                nc.vector.tensor_scalar(ve[:, 0:NT - 1], mv[:, 0:NT - 1, 1], EPS, None, ALU.add).then_inc(s["ve_done"], 1)
                nc.vector.bn_aggr(mv[:, NT - 1, :], st[:, NT - 1, :]).then_inc(s["mv_done"], 1)
                dve.wait_ge(s["mv_done"], 4 * b + NT)
                nc.vector.tensor_scalar(ve[:, NT - 1:NT], mv[:, NT - 1:NT, 1], EPS, None, ALU.add).then_inc(s["ve_done"], 1)
                dve.wait_ge(s["rstd_done"], b + 1)
                for i in range(NT):
                    nc.vector.tensor_scalar(ln[:, i, :], xn[:, i, :], mv[:, i, 0:1], rstd[:, i:i + 1],
                                            ALU.subtract, ALU.mult).then_inc(s["ln_done"], 1)

            front(0)
            nonzero_rows(0)
            labels(0)
            softmax(0)
            def step(b):
                front(b)
                attention(b - 1)
                nonzero_rows(b)
                labels(b)
                residual_ln(b - 1)
                softmax(b)

            step(1)
            with dve.Fori(2, B) as b:
                step(b)
            attention(B - 1)
            residual_ln(B - 1)

        @block.tensor
        def _(pe):
            def self_features(b):
                pe.wait_ge(s["x_t_in"], 16 * b + 16)
                pe.wait_ge(s["att_done"], 4 * b)
                for f in range(FC):
                    last = nc.tensor.matmul(bank[0:64, 0, :], ones64[:, :], xraw[:, f, :],
                                            start=f == 0, stop=f == FC - 1)
                last.then_inc(s["rs_ready"], 1)
                pe.wait_ge(s["xh_done"], b + 1)
                pe.wait_ge(s["xl_done"], b + 1)
                for o in range(FC):
                    if o == 1:
                        pe.wait_ge(s["z_done"], b + 1)
                    if o >= 2:
                        pe.wait_ge(s["sf_done"], 4 * b + o - 1)
                    out, col = bank[:, (o + 1) % 2, :], slice(o * P, (o + 1) * P)
                    for f in range(FC):
                        mm3(nc, out, t["w1h"][:, f, col], t["w1l"][:, f, col], xh[:, f, :], xl[:, f, :], f == 0, False)
                    if o == 0:
                        pe.wait_ge(s["z_done"], b + 1)
                    nc.tensor.matmul(out, t["sq"][:, col], z[:, :], start=False, stop=True).then_inc(s["sf_ready"], 1)

            def scores(b):
                pe.wait_ge(s["m_in"], 16 * b + 16)
                pe.wait_ge(s["sf_done"], 4 * b + 4)
                for i in range(NT):
                    pe.wait_ge(s["mult_done"], 4 * b + max(i - 1, 0))
                    for dr in range(2):
                        out = bank[:, 2 + 2 * (i % 2) + dr, 0:HK]
                        for f in range(FC):
                            nc.tensor.matmul(out, sf[:, f, i * P:(i + 1) * P], m[:, f, dr, :],
                                             start=f == 0, stop=False)
                        last = nc.tensor.matmul(out, onesr[:, :],
                                                t["bias_rows"][:, ds(b, 1), dr, :].rearrange("p o k -> p (o k)"),
                                                start=False, stop=True)
                    last.then_inc(s["sc_ready"], 1)

            def attention(b):
                pe.wait_ge(s["w_done"], 4 * b + 4)
                pe.wait_ge(s["v_in"], 16 * 16 * b + 16 * 16)
                pe.wait_ge(s["sf_done"], 4 * b + 4)
                pe.wait_ge(s["lnt_done"], 4 * b)
                for i in range(2 * FC + 1):
                    if i < 2 * FC:
                        c, dr = divmod(i, 2)
                        if i >= 2:
                            pe.wait_ge(s["wl_done"], 8 * b + i - 1)
                        for n in range(NT):
                            last = nc.tensor.transpose(
                                bank[0:CK, 6 + i % 2, n * P:(n + 1) * P],
                                e[:, n, dr, HC * c:HC * c + HC, :].rearrange("p h k -> p (h k)"), t["ident"][:, :])
                        last.then_inc(s["wtr_ready"], 1)
                    if i >= 1:
                        k = i - 1
                        c, dr = divmod(k, 2)
                        pe.wait_ge(s["wl_done"], 8 * b + k + 1)
                        if dr == 0 and c >= 2:
                            pe.wait_ge(s["att_done"], 4 * b + c - 1)
                        last = mm3(nc, bank[:, (c + 1) % 2, :], vdiag[:, 0, dr, c, :], vdiag[:, 1, dr, c, :],
                                   wth[:, k % 2, :], wtl[:, k % 2, :], dr == 0, dr == 1)
                        last.then_inc(s["att_mm"], 1)

            def back(b):
                pe.wait_ge(s["att_done"], 4 * b + 4)
                pe.wait_ge(s["wl_done"], 8 * b + 8)
                for i in range(NT):
                    if i >= 2:
                        pe.wait_ge(s["h_done"], 4 * b + i - 1)
                    for f in range(FC):
                        last = nc.tensor.transpose(bank[:, 6 + i % 2, f * P:(f + 1) * P],
                                                   ot[:, f, i * P:(i + 1) * P], t["ident"][:, :])
                    last.then_inc(s["back_ready"], 1)

            def ln_t(b):
                pe.wait_ge(s["ln_done"], 4 * b + 4)
                pe.wait_ge(s["h_done"], 4 * b + 4)
                for f in range(FC):
                    if f >= 2:
                        pe.wait_ge(s["lnt_done"], 4 * b + f - 1)
                    for i in range(NT):
                        last = nc.tensor.transpose(bank[:, 6 + f % 2, i * P:(i + 1) * P],
                                                   ln[:, i, f * P:(f + 1) * P], t["ident"][:, :])
                    last.then_inc(s["lnt_ready"], 1)

            pe.wait_ge(s["set_up"], 4)
            self_features(0)
            scores(0)
            def step(b):
                attention(b - 1)
                self_features(b)
                back(b - 1)
                ln_t(b - 1)
                scores(b)

            step(1)
            with pe.Fori(2, B) as b:
                step(b)
            attention(B - 1)
            back(B - 1)
            ln_t(B - 1)


def split_weights(nc, t, d):
    with ExitStack() as ctx:
        raw = ctx.enter_context(nc.sbuf_tensor("w_raw", [P, 4, FC, D], F32))
        s = sems(nc, ctx, "w_in0 w_in1 w_in2 w_in3 w_hi w_lo")
        w_in = (s["w_in0"], s["w_in1"], s["w_in2"], s["w_in3"])
        block = ctx.enter_context(nc.Block())
        dst = [(t["wqkh"][:, :, 0:D], t["wqkl"][:, :, 0:D]), (t["wqkh"][:, :, D:2 * D], t["wqkl"][:, :, D:2 * D]),
               (t["wvh"][:, :, :], t["wvl"][:, :, :]), (t["wph"][:, :, :], t["wpl"][:, :, :])]

        @block.sync
        def _(sp):
            for k in range(4):
                src = d["wqkv_t"][:, k, :] if k < 3 else d["wp_t"]
                sp.dma_start(raw[:, k], src.rearrange("(c p) o -> p c o", p=P)).then_inc(w_in[k], 16)

        @block.vector
        def _(dve):
            for k in range(4):
                dve.wait_ge(w_in[k], 16)
                nc.vector.tensor_copy(dst[k][0], raw[:, k]).then_inc(s["w_hi"], 1)
                dve.wait_ge(s["w_hi"], k + 1)
                nc.vector.tensor_tensor(dst[k][1], raw[:, k], dst[k][0].bitcast(F32), ALU.subtract).then_inc(s["w_lo"], 1)


def attention(nc, t, d):
    with ExitStack() as ctx:
        def sb(name, shape, dt=F32):
            return ctx.enter_context(nc.sbuf_tensor(name, shape, dt))

        traw = sb("traw", [P, FC, N])
        hh, hl = sb("hh", [P, FC, N], F32R), sb("hl", [P, FC, N], F32R)
        h = sb("h", [P, NT, D])
        qh, ql, kh, kl = (sb(n, [P, N], F32R) for n in ("qh", "ql", "kh", "kl"))
        sq, sk = sb("sq_stack", [P, 2, HC, N], F32R), sb("sk_stack", [P, 2, HC, N], F32R)
        v = sb("v", [P, NT, D])
        pt = sb("pt", [P, 4, 2, N])
        rden, o = sb("rden", [P, N]), sb("o", [P, N])
        oh, ol = sb("oh", [P, FC, N], F32R), sb("ol", [P, FC, N], F32R)
        shrow = sb("shrow", [2 * HC, N])
        rows = sb("rows", [P, 2, D])
        bv, bp = sb("bv", [P, D]), sb("bp", [P, D])
        bqc, bkc = sb("bqc", [P, FC]), sb("bkc", [P, FC])
        ln = sb("ln2", [P, NT, D])
        ones32 = sb("ones32", [P, DH])
        mx = sb("mx2", [P, 2, NT, HC])
        shift = sb("shift", [P, NT, 2 * HC], F32R)
        st, mv = sb("st2", [P, NT, 6]), sb("mv2", [P, NT, 2])
        ve, rstd, mhalf = sb("ve2", [P, NT]), sb("rstd2", [P, NT]), sb("mhalf2", [P, NT])
        bank = ctx.enter_context(nc.psum_tensor("a_bank", [P, 8, 512], F32))
        O, DEN = 4, 5

        s = sems(nc, ctx, "ld_c t_in h_in rows_in stk0 stk1 shf0 shf1 set_up hh_done hl_done q_ready k_ready "
                          "qh_done ql_done kh_done kl_done e_ready emax_done sh_hi sh_lo sh_ready shrow_done "
                          "et_ready exp_done pv_done rden_done o_done oh_done ol_done v_ready v_done pj_ready "
                          "hb_done h1_done st_done mv_done ve_done rstd_done ln_done mulg_done addb_done y_done y_out")
        stk, shf = (s["stk0"], s["stk1"]), (s["shf0"], s["shf1"])
        STK = 16 * 24
        block = ctx.enter_context(nc.Block())

        def ahead(b, c, k):
            return (b, c + k) if c + k < FC else (b + 1, c + k - FC)

        def use(b, c):
            return 2 * b + c // 2

        @block.sync
        def _(sp):
            sp.dma_start(bqc[:, :], d["bqkc"][:, 0, :]).then_inc(s["ld_c"], 16)
            sp.dma_start(bkc[:, :], d["bqkc"][:, 1, :]).then_inc(s["ld_c"], 16)
            sp.dma_start(bv[:, :], d["bv"].partition_broadcast(P)).then_inc(s["ld_c"], 16)
            sp.dma_start(bp[:, :], d["bp"].partition_broadcast(P)).then_inc(s["ld_c"], 16)

            def load_t(b):
                sp.dma_start(traw[:, :, :], d["t_rows"][ds(b, 1)].rearrange("o p c n -> (o p) c n")).then_inc(s["t_in"], 16)

            def load_h(b):
                sp.dma_start(h[:, :, :], d["h_rows"][ds(b, 1)].rearrange("o p t f -> (o p) t f")).then_inc(s["h_in"], 16)
                sp.dma_start(rows[:, :, :], d["gb_rows"][ds(b, 1)].rearrange("o k f -> (o k f)").partition_broadcast(P)
                             .rearrange("p (k f) -> p k f", k=2)).then_inc(s["rows_in"], 16)

            def store_y(b):
                sp.dma_start(d["out"][ds(b, 1)].rearrange("o (t p) f -> (o p) t f", p=P), ln[:, :, :]).then_inc(s["y_out"], 16)

            def stacks(c, hi_ready, lo_ready, hi, lo, dst, hi_rows, lo_rows):
                par = c % 2
                sp.wait_ge(*hi_ready)
                for r in hi_rows:
                    for j in range(HC):
                        sp.dma_start(dst[r:r + DH, par, j, :].bitcast(F32), hi[DH * j:DH * j + DH, :].bitcast(F32)).then_inc(stk[par], 16)
                sp.wait_ge(*lo_ready)
                for r in lo_rows:
                    for j in range(HC):
                        sp.dma_start(dst[r:r + DH, par, j, :].bitcast(F32), lo[DH * j:DH * j + DH, :].bitcast(F32)).then_inc(stk[par], 16)

            def q_stack(c, n):
                stacks(c, (s["qh_done"], n), (s["ql_done"], n), qh, ql, sq, (0, 2 * DH), (DH,))

            def k_stack(c, n):
                stacks(c, (s["kh_done"], n), (s["kl_done"], n), kh, kl, sk, (0, DH), (2 * DH,))

            def shifts(c, n):
                sp.wait_ge(s["shrow_done"], n)
                par = c % 2
                for part in range(2):
                    sp.dma_start(sq[3 * DH + part:3 * DH + part + 1, par, :, :].bitcast(F32),
                                 shrow[HC * part:HC * part + HC, :]).then_inc(shf[par], 16)

            load_t(0)
            load_h(0)
            sp.wait_ge(s["set_up"], 4)
            for c in range(2):
                q_stack(c, c + 1)
                k_stack(c, c + 1)

            def chunks(b, more):
                num = [sp.snap(4 * b + k) if not isinstance(b, int) else 4 * b + k for k in range(8)]
                one = sp.snap(b + 1) if not isinstance(b, int) else b + 1
                nxt = sp.snap(b + 1) if not isinstance(b, int) else b + 1
                prev = (sp.snap(b - 1) if not isinstance(b, int) else b - 1)
                b16 = (sp.snap(16 * b) if not isinstance(b, int) else 16 * b)
                for c in range(FC):
                    shifts(c, num[c + 1])
                    if c < 2 or more:
                        q_stack(c, num[c + 3])
                        k_stack(c, num[c + 3])
                    if c == 0:
                        if more:
                            sp.wait_ge(s["hl_done"], one)
                            load_t(nxt)
                    if c == 1 and not (isinstance(b, int) and b == 0):
                        sp.wait_ge(s["y_done"], num[0])
                        store_y(prev)
                        load_h(b)

            chunks(0, True)
            with sp.Fori(1, B - 1) as b:
                chunks(b, True)
            chunks(B - 1, False)
            sp.wait_ge(s["y_done"], 4 * B)
            store_y(B - 1)
            sp.wait_ge(s["y_out"], 16 * B)

        @block.gpsimd
        def _(pool):
            nc.gpsimd.memset(sk[3 * DH:, :, :, :].bitcast(F32), 1.0).then_inc(s["set_up"], 1)
            pool.wait_ge(s["set_up"], 1)
            nc.gpsimd.memset(sq[3 * DH:, :, :, :].bitcast(F32), 0.0).then_inc(s["set_up"], 1)
            pool.wait_ge(s["set_up"], 2)
            nc.gpsimd.memset(ones32[:, :], 1.0).then_inc(s["set_up"], 1)
            nc.gpsimd.memset(mhalf[:, :], -0.5).then_inc(s["set_up"], 1)

            def split_h(b):
                pool.wait_ge(s["hh_done"], b + 1)
                nc.gpsimd.tensor_tensor(hl[:, :, :], traw[:, :, :], hh[:, :, :].bitcast(F32),
                                        ALU.subtract).then_inc(s["hl_done"], 1)

            def add_bp(b):
                pool.wait_ge(s["h_in"], 16 * b + 16)
                nc.gpsimd.tensor_tensor(h[:, :, :], h[:, :, :], bp[:, :].unsqueeze(1).broadcast_to([P, NT, D]),
                                        ALU.add).then_inc(s["hb_done"], 1)

            def tail(b):
                pool.wait_ge(s["ve_done"], 2 * b + 2)
                nc.gpsimd.tensor_tensor(rstd[:, :], ve[:, :], mhalf[:, :], ALU.pow).then_inc(s["rstd_done"], 1)
                pool.wait_ge(s["rows_in"], 16 * b + 16)
                for i in range(NT):
                    pool.wait_ge(s["ln_done"], 4 * b + i + 1)
                    nc.gpsimd.tensor_tensor(ln[:, i, :], ln[:, i, :], rows[:, 0, :], ALU.mult).then_inc(s["mulg_done"], 1)
                    nc.gpsimd.tensor_tensor(h[:, i, :], h[:, i, :], rows[:, 1, :], ALU.add).then_inc(s["addb_done"], 1)

            def batch(b, more):
                if more:
                    split_h(b + 1)
                add_bp(b)
                tail(b)

            pool.wait_ge(s["set_up"], 4)
            pool.wait_ge(s["ld_c"], 64)
            split_h(0)
            batch(0, True)
            with pool.Fori(1, B - 1) as b:
                batch(b, True)
            batch(B - 1, False)

        @block.scalar
        def _(act):
            act.wait_ge(s["ld_c"], 64)

            def project(b, c):
                g = 4 * b + c
                if not (isinstance(b, int) and g == 0):
                    prev = (b, c - 1) if c else (b - 1, FC - 1)
                    act.wait_ge(stk[prev[1] % 2], STK * (use(*prev) + 1))
                act.wait_ge(s["q_ready"], g + 1)
                nc.scalar.activation(qh[:, :], bank[:, 6, :], ACT.Identity, bias=bqc[:, c:c + 1]).then_inc(s["qh_done"], 1)
                act.wait_ge(s["k_ready"], g + 1)
                nc.scalar.activation(kh[:, :], bank[:, 7, :], ACT.Identity, bias=bkc[:, c:c + 1]).then_inc(s["kh_done"], 1)

            def shift_rows(b, c):
                g = 4 * b + c
                if not (isinstance(b, int) and g == 0):
                    prev = (b, c - 1) if c else (b - 1, FC - 1)
                    act.wait_ge(shf[prev[1] % 2], 32 * (use(*prev) + 1))
                act.wait_ge(s["sh_ready"], g + 1)
                nc.scalar.activation(shrow[:, :], bank[0:2 * HC, 2, :], ACT.Copy).then_inc(s["shrow_done"], 1)

            def exps(b, c):
                g = 4 * b + c
                for i in range(8):
                    if not (isinstance(b, int) and 8 * g + i - 3 <= 0):
                        act.wait_ge(s["pv_done"], 8 * g + i - 3)
                    for k in range(2):
                        act.wait_ge(s["et_ready"], 16 * g + 2 * i + k + 1)
                        nc.scalar.activation(pt[:, i % 4, k, :], bank[:, k, :], ACT.Exp).then_inc(s["exp_done"], 1)

            def batch(b, more):
                for c in range(FC):
                    shift_rows(b, c)
                    exps(b, c)
                    if c < 2 or more:
                        project(*ahead(b, c, 2))

            project(0, 0)
            project(0, 1)
            batch(0, True)
            with act.Fori(1, B - 1) as b:
                batch(b, True)
            batch(B - 1, False)

        @block.vector
        def _(dve):
            def split_h(b):
                dve.wait_ge(s["t_in"], 16 * b + 16)
                dve.wait_ge(s["k_ready"], 4 * b)
                dve.wait_ge(s["v_ready"], 4 * b)
                nc.vector.tensor_copy(hh[:, :, :], traw[:, :, :]).then_inc(s["hh_done"], 1)

            def lo_part(b, c, src, bias, hi, lo, hi_done, lo_done):
                dve.wait_ge(hi_done, 4 * b + c + 1)
                nc.vector.scalar_tensor_tensor(lo[:, :], src, bias[:, c:c + 1], hi[:, :].bitcast(F32),
                                               ALU.add, ALU.subtract).then_inc(lo_done, 1)

            def ql_part(b, c):
                lo_part(b, c, bank[:, 6, :], bqc, qh, ql, s["qh_done"], s["ql_done"])

            def kl_part(b, c):
                lo_part(b, c, bank[:, 7, :], bkc, kh, kl, s["kh_done"], s["kl_done"])

            def maxima(b, c):
                g = 4 * b + c
                for i in range(16):
                    dve.wait_ge(s["e_ready"], 16 * g + i + 1)
                    j, n = divmod(i, NT)
                    nc.vector.reduce_max(mx[:, c % 2, n, j:j + 1], bank[:, 2 + i % 2, :], AX).then_inc(s["emax_done"], 1)

            def shift_parts(b, c):
                g = 4 * b + c
                dve.wait_ge(s["emax_done"], 16 * g + 16)
                dve.wait_ge(s["sh_ready"], g)
                nc.vector.tensor_scalar(shift[:, :, 0:HC], mx[:, c % 2], -1.0, None, ALU.mult).then_inc(s["sh_hi"], 1)
                dve.wait_ge(s["sh_hi"], g + 1)
                nc.vector.scalar_tensor_tensor(shift[:, :, HC:2 * HC], mx[:, c % 2], -1.0,
                                               shift[:, :, 0:HC].bitcast(F32), ALU.mult, ALU.subtract).then_inc(s["sh_lo"], 1)

            def row_sums(b, c):
                g = 4 * b + c
                dve.wait_ge(s["pv_done"], 8 * g + 8)
                nc.vector.reciprocal(rden[:, :], bank[:, DEN, :]).then_inc(s["rden_done"], 1)

            def outputs(b, c):
                g = 4 * b + c
                dve.wait_ge(s["rden_done"], g + 1)
                for k in range(2):
                    a, r = slice(64 * k, 64 * k + 64), slice(64 - 64 * k, 128 - 64 * k)
                    nc.vector.scalar_tensor_tensor(o[a, :], bank[a, O, :], float(D) ** -0.5, rden[r, :],
                                                   ALU.mult, ALU.mult).then_inc(s["o_done"], 1)
                dve.wait_ge(s["o_done"], 2 * g + 2)
                dve.wait_ge(s["pj_ready"], 4 * b)
                nc.vector.tensor_copy(oh[:, c, :], o[:, :]).then_inc(s["oh_done"], 1)
                dve.wait_ge(s["oh_done"], g + 1)
                nc.vector.tensor_tensor(ol[:, c, :], o[:, :], oh[:, c, :].bitcast(F32), ALU.subtract).then_inc(s["ol_done"], 1)

            def values(b):
                dve.wait_ge(s["pv_done"], 32 * b)
                for i in range(NT):
                    dve.wait_ge(s["v_ready"], 4 * b + i + 1)
                    nc.vector.tensor_tensor(v[:, i, :], bank[:, 6 + i % 2, :], bv[:, :], ALU.add).then_inc(s["v_done"], 1)

            def tail(b):
                dve.wait_ge(s["hb_done"], b + 1)
                for i in range(NT):
                    dve.wait_ge(s["pj_ready"], 4 * b + i + 1)
                    nc.vector.tensor_tensor(h[:, i, :], bank[:, 6 + i % 2, :], h[:, i, :], ALU.add).then_inc(s["h1_done"], 1)
                for i in range(NT):
                    dve.wait_ge(s["h1_done"], 4 * b + i + 1)
                    if i:
                        dve.wait_ge(s["st_done"], 4 * b + i)
                    nc.vector.bn_stats(st[:, i, :], h[:, i, :]).then_inc(s["st_done"], 1)
                    if i:
                        nc.vector.bn_aggr(mv[:, i - 1, :], st[:, i - 1, :]).then_inc(s["mv_done"], 1)
                dve.wait_ge(s["st_done"], 4 * b + NT)
                dve.wait_ge(s["mv_done"], 4 * b + NT - 1)
                nc.vector.tensor_scalar(ve[:, 0:NT - 1], mv[:, 0:NT - 1, 1], EPS, None, ALU.add).then_inc(s["ve_done"], 1)
                nc.vector.bn_aggr(mv[:, NT - 1, :], st[:, NT - 1, :]).then_inc(s["mv_done"], 1)
                dve.wait_ge(s["mv_done"], 4 * b + NT)
                nc.vector.tensor_scalar(ve[:, NT - 1:NT], mv[:, NT - 1:NT, 1], EPS, None, ALU.add).then_inc(s["ve_done"], 1)
                dve.wait_ge(s["y_out"], 16 * b)
                dve.wait_ge(s["rstd_done"], b + 1)
                for i in range(NT):
                    nc.vector.tensor_scalar(ln[:, i, :], h[:, i, :], mv[:, i, 0:1], rstd[:, i:i + 1],
                                            ALU.subtract, ALU.mult).then_inc(s["ln_done"], 1)

            def result(b):
                for i in range(NT):
                    dve.wait_ge(s["mulg_done"], 4 * b + i + 1)
                    dve.wait_ge(s["addb_done"], 4 * b + i + 1)
                    nc.vector.tensor_tensor(ln[:, i, :], ln[:, i, :], h[:, i, :], ALU.add).then_inc(s["y_done"], 1)

            def batch(b, more):
                for c in range(FC):
                    if c == 1 and not (isinstance(b, int) and b == 0):
                        result(b - 1)
                    if c == 2 and more:
                        split_h(b + 1)
                    nxt, tgt = c < 3 or more, c < 2 or more
                    if nxt:
                        maxima(*ahead(b, c, 1))
                    if tgt:
                        ql_part(*ahead(b, c, 2))
                    if nxt:
                        shift_parts(*ahead(b, c, 1))
                    row_sums(b, c)
                    if tgt:
                        kl_part(*ahead(b, c, 2))
                    outputs(b, c)
                if more:
                    values(b + 1)
                tail(b)

            dve.wait_ge(s["ld_c"], 64)
            split_h(0)
            for c in range(2):
                ql_part(0, c)
                kl_part(0, c)
            maxima(0, 0)
            shift_parts(0, 0)
            values(0)
            batch(0, True)
            with dve.Fori(1, B - 1) as b:
                batch(b, True)
            batch(B - 1, False)
            result(B - 1)

        @block.tensor
        def _(pe):
            def project(b, c, which):
                g = 4 * b + c
                if which == 0:
                    pe.wait_ge(s["hh_done"], b + 1)
                    pe.wait_ge(s["hl_done"], b + 1)
                pe.wait_ge((s["ql_done"], s["kl_done"])[which], g)
                if c == 2:
                    pe.wait_ge(s["h1_done"], 4 * b)
                col = slice(which * D + c * P, which * D + (c + 1) * P)
                for f in range(FC):
                    last = mm3(nc, bank[:, 6 + which, :], t["wqkh"][:, f, col], t["wqkl"][:, f, col],
                               hh[:, f, :], hl[:, f, :], f == 0, f == FC - 1)
                last.then_inc((s["q_ready"], s["k_ready"])[which], 1)

            def values(b):
                pe.wait_ge(s["ql_done"], 4 * b + 2)
                pe.wait_ge(s["kl_done"], 4 * b + 2)
                for i in range(NT):
                    if i >= 2:
                        pe.wait_ge(s["v_done"], 4 * b + i - 1)
                    r = slice(i * P, (i + 1) * P)
                    for f in range(FC):
                        last = mm3(nc, bank[:, 6 + i % 2, :], hh[:, f, r], hl[:, f, r],
                                   t["wvh"][:, f, :], t["wvl"][:, f, :], f == 0, f == FC - 1)
                    last.then_inc(s["v_ready"], 1)

            def scores(b, c, i):
                g = 4 * b + c
                if i == 0:
                    pe.wait_ge(stk[c % 2], STK * (use(b, c) + 1))
                    pe.wait_ge(s["shrow_done"], g)
                if i < 2:
                    pe.wait_ge(s["emax_done"], 16 * g)
                else:
                    pe.wait_ge(s["emax_done"], 16 * g + i - 1)
                j, n = divmod(i, NT)
                nc.tensor.matmul(bank[:, 2 + i % 2, :], sq[0:3 * DH, c % 2, j, n * P:(n + 1) * P],
                                 sk[0:3 * DH, c % 2, j, :], start=True, stop=True).then_inc(s["e_ready"], 1)

            def shift_t(b, c):
                g = 4 * b + c
                pe.wait_ge(s["sh_lo"], g + 1)
                for n in range(NT):
                    last = nc.tensor.matmul(bank[0:2 * HC, 2, n * P:(n + 1) * P], shift[:, n, :].bitcast(F32),
                                            t["ident"][:, :], start=True, stop=True)
                last.then_inc(s["sh_ready"], 1)

            def scores_t(b, c, i):
                g = 4 * b + c
                if i == 0:
                    pe.wait_ge(stk[c % 2], STK * (use(b, c) + 1))
                    pe.wait_ge(shf[c % 2], 32 * (use(b, c) + 1))
                for k in range(2):
                    if i == 0:
                        pe.wait_ge(s["exp_done"], 16 * g)
                    else:
                        pe.wait_ge(s["exp_done"], 16 * g + 2 * i + k - 1)
                    j, n = 2 * (i // 4) + k, i % 4
                    nc.tensor.matmul(bank[:, k, :], sk[0:3 * DH + 2, c % 2, j, n * P:(n + 1) * P],
                                     sq[0:3 * DH + 2, c % 2, j, :], start=True, stop=True).then_inc(s["et_ready"], 1)

            def weighted(b, c, i):
                g = 4 * b + c
                if i == 0:
                    pe.wait_ge(s["o_done"], 2 * g)
                    pe.wait_ge(s["v_done"], 4 * b + 4)
                pe.wait_ge(s["exp_done"], 16 * g + 2 * i + 2)
                n = i % 4
                for k in range(2):
                    j = 2 * (i // 4) + k
                    w = pt[:, n, k, :]
                    nc.tensor.matmul(bank[DH * j:DH * j + DH, O, :], v[:, n, (HC * c + j) * DH:(HC * c + j + 1) * DH],
                                     w, start=n == 0, stop=n == 3)
                    r = DH * ((j + 2) % 4)
                    last = nc.tensor.matmul(bank[r:r + DH, DEN, :], ones32[:, :], w, start=n == 0, stop=n == 3)
                last.then_inc(s["pv_done"], 1)

            def output_projection(b, more):
                pe.wait_ge(s["ol_done"], 4 * b + 4)
                if more:
                    pe.wait_ge(s["v_done"], 4 * b + 8)
                else:
                    pe.wait_ge(s["ql_done"], 4 * b + 4)
                    pe.wait_ge(s["kl_done"], 4 * b + 4)
                for i in range(NT):
                    if i >= 2:
                        pe.wait_ge(s["h1_done"], 4 * b + i - 1)
                    r = slice(i * P, (i + 1) * P)
                    for c in range(FC):
                        last = mm3(nc, bank[:, 6 + i % 2, :], oh[:, c, r], ol[:, c, r],
                                   t["wph"][:, c, :], t["wpl"][:, c, :], c == 0, c == FC - 1)
                    last.then_inc(s["pj_ready"], 1)

            E_AT = [0, 3, 3, 3, 3, 2, 2, 0]

            def batch(b, more):
                for c in range(FC):
                    shift_t(b, c)
                    scores_t(b, c, 0)
                    e = 0
                    for i in range(8):
                        if c < 3 or more:
                            for _ in range(E_AT[i]):
                                scores(*ahead(b, c, 1), e)
                                e += 1
                        if i < 7:
                            scores_t(b, c, i + 1)
                        weighted(b, c, i)
                        if i >= 6 and (c < 2 or more):
                            project(*ahead(b, c, 2), i - 6)
                if more:
                    values(b + 1)
                output_projection(b, more)

            pe.wait_ge(s["set_up"], 4)
            for c in range(2):
                project(0, c, 0)
                project(0, c, 1)
            for i in range(16):
                scores(0, 0, i)
            values(0)
            batch(0, True)
            with pe.Fori(1, B - 1) as b:
                batch(b, True)
            batch(B - 1, False)


def program(nc, d):
    d["gb_rows"] = nc.dram_tensor("gb_rows", [B, 2, D], F32, kind="Internal").ap()
    d["v_rows"] = nc.dram_tensor("v_rows", [2, 2, B * MP, D], F32, kind="Internal").ap()
    d["m_rows"] = nc.dram_tensor("m_rows", [B, P, FC, 2, HK], F32, kind="Internal").ap()
    d["h_rows"] = nc.dram_tensor("h_rows", [B, P, NT, D], F32, kind="Internal").ap()
    d["t_rows"] = nc.dram_tensor("t_rows", [B, P, FC, N], F32, kind="Internal").ap()
    t = {}
    with ExitStack() as outer:
        t["ident"] = outer.enter_context(nc.sbuf_tensor("ident", [P, P], F32))
        with ExitStack() as ctx:
            def sb(name, shape, dt=F32):
                return ctx.enter_context(nc.sbuf_tensor(name, shape, dt))

            t["w1h"], t["w1l"] = sb("w1h", [P, FC, D], F32R), sb("w1l", [P, FC, D], F32R)
            t["sq"] = sb("sq", [64, D], F32R)
            t["hot"] = sb("hot", [64, B])
            t["bself"], t["boutc"] = sb("bself", [P, FC]), sb("boutc", [P, FC])
            t["wbias"], t["bbias"] = sb("wbias", [P, L]), sb("bbias", [P, 1])
            t["bias_rows"] = sb("bias_rows", [64, B, 2, HK], F32R)
            prologue(nc, t, d)
            graph(nc, t, d)
        with ExitStack() as ctx:
            def wt(name, width):
                return ctx.enter_context(nc.sbuf_tensor(name, [P, FC, width], F32R))

            t["wqkh"], t["wqkl"] = wt("wqkh", 2 * D), wt("wqkl", 2 * D)
            t["wvh"], t["wvl"], t["wph"], t["wpl"] = wt("wvh", D), wt("wvl", D), wt("wph", D), wt("wpl", D)
            split_weights(nc, t, d)
            attention(nc, t, d)


def kernel(**inputs):
    import numpy as np
    import concourse.bacc as bacc
    from concourse import mybir as mb
    from concourse.bass_utils import run_bass_kernel_spmd

    a = {k: np.asarray(v) for k, v in inputs.items()}

    def g(k):
        return a["L0_cond_" + k]

    def f(k):
        return a["L1_cond_" + k]

    adj = a["mask_BxSxSx11_ik0"]
    x = a["x"]
    bqkv = f("bqkv").reshape(D, 3).T

    def columns(v):
        v = v.reshape(v.shape[:-1] + (FC, P))
        return np.moveaxis(v, -1, 0)

    def twice(v):
        out = np.zeros(v.shape[:-1] + (64,), v.dtype)
        out[..., 0:v.shape[-1]] = v
        out[..., 32:32 + v.shape[-1]] = v
        return out

    adj2 = np.stack([adj[:, :, :NK, :], adj[:, :NK, :, :].transpose(0, 2, 1, 3)], axis=2)
    hot = np.zeros((64, B), np.float32)
    for b in range(B):
        hot[b, b] = hot[32 + b, b] = 1.0
    hot20 = np.repeat(hot[:, :, None], MP, axis=2).reshape(64, B * MP)
    wqkv = f("Wqkv").reshape(D, 3, D)
    arrays = {
        "x": x,
        "x_t": x.transpose(0, 2, 1).reshape(B, FC, P, N).transpose(0, 2, 1, 3),
        "adj": adj2.reshape(B, NT, P, 2 * NK, L).transpose(0, 2, 1, 3, 4).reshape(B, P, NT * 2 * NK, L),
        "cond64": twice(a["cond_1024"].T.reshape(FC, P, B).transpose(1, 0, 2)),
        "wself_t": g("W_self").T,
        "b_self": columns(g("b_self")),
        "w_bias": g("w_bias"),
        "b_bias": g("b_bias").reshape(1),
        "wq": g("Wq"),
        "bq64": twice(columns(g("bq"))[..., None]),
        "wk_t": g("Wk").transpose(0, 2, 1),
        "bk": columns(g("bk")),
        "wout_t": g("Wout").reshape(2, D, D).transpose(0, 2, 1),
        "bout": columns(g("bout")),
        "ln_g": f("ln_g"), "ln_b": f("ln_b"), "bg": f("bg"), "bb": f("bb"),
        "wg_t": f("Wg").T, "wb_t": f("Wb").T,
        "wqkv_t": wqkv.transpose(2, 1, 0),
        "bqkc": columns(bqkv[0:2]),
        "bv": bqkv[2],
        "wp_t": f("Wp").T,
        "bp": f("bp"),
        "ident": np.eye(P, dtype=np.float32),
        "hot": hot,
        "hot20": hot20,
    }
    nc = bacc.Bacc("TRN2", target_bir_lowering=False, num_devices=1)
    feed, drams = {}, {}
    for name, v in arrays.items():
        v = np.ascontiguousarray(v)
        feed["in_" + name] = v
        drams[name] = nc.dram_tensor("in_" + name, v.shape, mb.dt.from_np(v.dtype), kind="ExternalInput").ap()
    d = dict(drams)
    d["out"] = nc.dram_tensor("out_y", (B, N, D), mb.dt.float32, kind="ExternalOutput").ap()
    program(nc, d)
    r = run_bass_kernel_spmd(nc, [feed], core_ids=[0])
    return r.results[0]["out_y"]
```

```python
from contextlib import ExitStack

import concourse.bass as bass
from concourse import mybir

F32 = mybir.dt.float32
F32R = mybir.dt.float32r
I32 = mybir.dt.int32
ALU = mybir.AluOpType
ACT = mybir.ActivationFunctionType
AX = mybir.AxisListType.X

P = 128
B, N, D = 8, 512, 512
H = 16
DH = D // H
L = 11
NK = 20
MP = 32
FC = D // P
NT = N // P
HC = P // DH
HK = H * NK
CK = HC * NK
NEG = -9000000000000000.0
EPS = 1e-5
ds = bass.ds


def sems(nc, ctx, names):
    return {n: ctx.enter_context(nc.semaphore(n)) for n in names.split()}


def mm3(nc, out, ah, al, bh, bl, start, stop):
    nc.tensor.matmul(out, ah, bh, start=start, stop=False)
    nc.tensor.matmul(out, ah, bl, start=False, stop=False)
    return nc.tensor.matmul(out, al, bh, start=False, stop=stop)


def prologue(nc, t, d):
    with ExitStack() as ctx:
        def sb(name, shape, dt=F32):
            return ctx.enter_context(nc.sbuf_tensor(name, shape, dt))

        cond64 = sb("cond64", [P, FC, 64])
        wself_raw = sb("wself_raw", [P, 2 * FC, D])
        wg = sb("wg", [P, FC, D])
        wb = sb("wb", [P, FC, D])
        x20 = sb("x20", [P, FC, B * MP])
        bg8, bb8, lng8, lnb8 = (sb(n, [B, D]) for n in ("bg8", "bb8", "lng8", "lnb8"))
        gam8, gs8, bt8, bs8 = (sb(n, [B, D]) for n in ("gam8", "gs8", "bt8", "bs8"))
        wk = sb("wk", [P, 2, FC, D])
        wq = sb("wq", [P, 2, FC, D])
        wout = sb("wout", [P, 2, FC, D])
        bk = sb("bk", [P, 2, FC])
        bout2 = sb("bout2", [P, 2, FC])
        bq64 = sb("bq64", [P, 2, FC, 64])
        hot20 = sb("hot20", [64, B * MP])
        ones64 = sb("ones64", [P, 64])
        z20 = sb("z20", [64, B * MP], F32R)
        sf20 = sb("sf20", [P, FC, B * MP])
        kdiag = sb("kdiag", [P, FC, B, CK])
        mout = sb("mout", [P, 2, B, HK])
        vparts = sb("vparts", [P, 2, 2, D], F32R)
        lo_tmp = sb("lo_tmp", [64, 2, 4 * CK], F32R)
        bank = ctx.enter_context(nc.psum_tensor("p_bank", [P, 8, 512], F32))

        s = sems(nc, ctx, "ld_small ld_const bout_done ld_wself ld_x20 ld_gb ld_wk ld_wq ld_wout ld_hot zeroed cond_in bq_in "
                          "sq_ready sq_hi sq_split rs_ready z_ready gb_ready gb_step sf_ready sf_done "
                          "kh_ready kdiag_done v_ready v_hi v_done m_ready m_done_dve m_done_act "
                          "bias_ready bias_hi bias_done w1_hi w1_split st_gb st_v st_m0 st_m1")
        block = ctx.enter_context(nc.Block())

        @block.sync
        def _(sp):
            sp.wait_ge(s["zeroed"], 1)
            sp.dma_start(cond64[:, :, :], d["cond64"]).then_inc(s["cond_in"], 16)
            sp.dma_start(wself_raw[:, :, :], d["wself_t"].rearrange("(c p) o -> p c o", p=P)).then_inc(s["ld_wself"], 16)
            for c in range(FC):
                sp.dma_start(x20[:, c, :].rearrange("p (b m) -> p b m", b=B)[:, :, 0:NK],
                             d["x_t"][:, :, c, 0:NK].rearrange("b p m -> p b m")).then_inc(s["ld_x20"], 16)
            sp.dma_start(hot20[:, :], d["hot20"]).then_inc(s["ld_hot"], 16)
            sp.dma_start(wk[:, :, :, :], d["wk_t"].rearrange("e (c p) o -> p e c o", p=P)).then_inc(s["ld_wk"], 16)
            sp.dma_start(wq[:, :, :, :], d["wq"].rearrange("e (c p) o -> p e c o", p=P)).then_inc(s["ld_wq"], 16)
            sp.dma_start(wout[:, :, :, :], d["wout_t"].rearrange("e (c p) o -> p e c o", p=P)).then_inc(s["ld_wout"], 16)
            sp.dma_start(wg[:, :, :], d["wg_t"].rearrange("(c p) o -> p c o", p=P)).then_inc(s["ld_gb"], 16)
            sp.dma_start(wb[:, :, :], d["wb_t"].rearrange("(c p) o -> p c o", p=P)).then_inc(s["ld_gb"], 16)
            for e in range(2):
                for g in range(2):
                    sp.wait_ge(s["v_done"], 2 * e + g + 1)
                    for part in range(2):
                        sp.dma_start(d["v_rows"][part, e, g * P:(g + 1) * P, :],
                                     vparts[:, g, part, :].bitcast(F32)).then_inc(s["st_v"], 16)
                for f in range(FC):
                    i = FC * e + f
                    sp.wait_ge(s["m_done_dve"], FC * (i + 1))
                    sp.wait_ge(s["m_done_act"], FC * (i + 1))
                    sp.dma_start(d["m_rows"][:, :, f, e, :].rearrange("b p k -> p b k"),
                                 mout[:, i % 2, :, :]).then_inc((s["st_m0"], s["st_m1"])[i % 2], 16)
            sp.wait_ge(s["gb_step"], 6)
            sp.dma_start(d["gb_rows"][:, 0, :], gs8[:, :]).then_inc(s["st_gb"], 16)
            sp.dma_start(d["gb_rows"][:, 1, :], bs8[:, :]).then_inc(s["st_gb"], 16)
            sp.wait_ge(s["st_gb"], 32)
            sp.wait_ge(s["st_v"], 16 * 8)
            sp.wait_ge(s["st_m0"], 16 * FC)
            sp.wait_ge(s["st_m1"], 16 * FC)

        @block.gpsimd
        def _(pool):
            nc.gpsimd.memset(x20[:, :, :], 0.0).then_inc(s["zeroed"], 1)
            nc.gpsimd.memset(ones64[:, :], 1.0).then_inc(s["zeroed"], 1)
            nc.gpsimd.memset(kdiag[:, :, :, :], 0.0).then_inc(s["zeroed"], 1)
            pool.wait_ge(s["w1_hi"], 1)
            nc.gpsimd.tensor_tensor(t["w1l"][:, :, :], wself_raw[:, 0:FC, :], t["w1h"][:, :, :].bitcast(F32),
                                    ALU.subtract).then_inc(s["w1_split"], 1)

        @block.scalar
        def _(act):
            act.dma_start(bq64[:, :, :, :], d["bq64"]).then_inc(s["bq_in"], 16)
            act.dma_start(t["bself"][:, :], d["b_self"]).then_inc(s["ld_const"], 16)
            act.dma_start(bout2[:, :, :], d["bout"]).then_inc(s["ld_const"], 16)
            act.dma_start(t["ident"][:, :], d["ident"]).then_inc(s["ld_const"], 16)
            act.dma_start(t["hot"][:, :], d["hot"]).then_inc(s["ld_const"], 16)
            act.dma_start(t["wbias"][:, :], d["w_bias"].partition_broadcast(P)).then_inc(s["ld_const"], 16)
            act.dma_start(t["bbias"][:, :], d["b_bias"].partition_broadcast(P)).then_inc(s["ld_const"], 16)
            act.dma_start(bk[:, :, :], d["bk"]).then_inc(s["ld_small"], 16)
            for row, src in ((bg8, d["bg"]), (bb8, d["bb"]), (lng8, d["ln_g"]), (lnb8, d["ln_b"])):
                act.dma_start(row[:, :], src.partition_broadcast(B)).then_inc(s["ld_small"], 16)
            act.wait_ge(s["ld_const"], 16 * 6)
            for o in range(FC):
                act.wait_ge(s["sf_ready"], o + 1)
                nc.scalar.activation(sf20[:, o, :], bank[:, 4 + o, 0:B * MP], ACT.Identity,
                                     bias=t["bself"][:, o:o + 1]).then_inc(s["sf_done"], 1)
            for i in range(2 * FC):
                if i >= 2:
                    act.wait_ge((s["st_m0"], s["st_m1"])[i % 2], 16 * (i // 2))
                for h in range(FC):
                    act.wait_ge(s["m_ready"], 2 * (FC * i + h) + 2)
                    nc.scalar.activation(mout[:, i % 2, 4:8, h * CK:(h + 1) * CK],
                                         bank[:, 2 * (h % 2) + 1, 0:4 * CK].rearrange("p (b k) -> p b k", b=4),
                                         ACT.Copy).then_inc(s["m_done_act"], 1)

        @block.vector
        def _(dve):
            dve.wait_ge(s["sq_ready"], 1)
            nc.vector.tensor_copy(t["sq"][:, :], bank[0:64, 0, :]).then_inc(s["sq_hi"], 1)
            dve.wait_ge(s["sq_hi"], 1)
            nc.vector.tensor_tensor(t["sq"][32:64, :], bank[32:64, 0, :], t["sq"][32:64, :].bitcast(F32),
                                    ALU.subtract).then_inc(s["sq_split"], 1)
            dve.wait_ge(s["rs_ready"], 1)
            dve.wait_ge(s["ld_hot"], 16)
            nc.vector.scalar_tensor_tensor(z20[:, :], bank[0:64, 1, 0:B * MP], 0.0, hot20[:, :],
                                           ALU.not_equal, ALU.mult).then_inc(s["z_ready"], 1)
            dve.wait_ge(s["ld_wself"], 16)
            nc.vector.tensor_copy(t["w1h"][:, :, :], wself_raw[:, 0:FC, :]).then_inc(s["w1_hi"], 1)
            dve.wait_ge(s["ld_const"], 16 * 6)
            nc.vector.tensor_tensor(t["boutc"][:, :], bout2[:, 0, :], bout2[:, 1, :], ALU.add).then_inc(s["bout_done"], 1)
            dve.wait_ge(s["ld_small"], 16 * 5)
            for e in range(2):
                if e == 1:
                    dve.wait_ge(s["bias_ready"], 2 * FC)
                for h in range(FC):
                    dve.wait_ge(s["kh_ready"], FC * e + h + 1)
                    dve.wait_ge(s["zeroed"], 3)
                    src = bank[:, h % 2 + 4, 0:B * MP].rearrange("p (b m) -> p b m", b=B)
                    for j in range(HC):
                        r = slice(DH * j, DH * j + DH)
                        nc.vector.tensor_scalar(kdiag[r, h, :, NK * j:NK * j + NK], src[r, :, 0:NK],
                                                bk[r, e, h:h + 1], float(DH) ** -0.5,
                                                ALU.add, ALU.mult).then_inc(s["kdiag_done"], 1)
                for g in range(2):
                    n = 2 * e + g
                    dve.wait_ge(s["v_ready"], n + 1)
                    if e == 1:
                        dve.wait_ge(s["st_v"], 16 * 2 * 2)
                    nc.vector.tensor_copy(vparts[:, g, 0, :], bank[:, 6 + g, :]).then_inc(s["v_hi"], 1)
                    dve.wait_ge(s["v_hi"], n + 1)
                    nc.vector.tensor_tensor(vparts[:, g, 1, :], bank[:, 6 + g, :],
                                            vparts[:, g, 0, :].bitcast(F32), ALU.subtract).then_inc(s["v_done"], 1)
                for f in range(FC):
                    i = FC * e + f
                    if i >= 2:
                        dve.wait_ge((s["st_m0"], s["st_m1"])[i % 2], 16 * (i // 2))
                    for h in range(FC):
                        dve.wait_ge(s["m_ready"], 2 * (FC * i + h) + 1)
                        nc.vector.tensor_copy(mout[:, i % 2, 0:4, h * CK:(h + 1) * CK],
                                              bank[:, 2 * (h % 2), 0:4 * CK].rearrange("p (b k) -> p b k", b=4)
                                              ).then_inc(s["m_done_dve"], 1)
                for h in range(FC):
                    for half in range(2):
                        n = 2 * (FC * e + h) + half
                        dve.wait_ge(s["bias_ready"], n + 1)
                        src = bank[:, 4 + n % 2, 0:4 * CK].rearrange("p (b k) -> p b k", b=4)
                        dst = t["bias_rows"][:, 4 * half:4 * half + 4, e, h * CK:(h + 1) * CK]
                        nc.vector.tensor_copy(dst[0:64], src[0:64]).then_inc(s["bias_hi"], 1)
                        dve.wait_ge(s["bias_hi"], n + 1)
                        nc.vector.tensor_tensor(dst[32:64], src[32:64], dst[32:64].bitcast(F32),
                                                ALU.subtract).then_inc(s["bias_done"], 1)
            dve.wait_ge(s["gb_ready"], 2)
            nc.vector.tensor_tensor(gam8[:, :], bank[0:B, 2, :], bg8[:, :], ALU.add).then_inc(s["gb_step"], 1)
            nc.vector.tensor_tensor(bt8[:, :], bank[0:B, 3, :], bb8[:, :], ALU.add).then_inc(s["gb_step"], 1)
            dve.wait_ge(s["gb_step"], 2)
            nc.vector.tensor_tensor(gs8[:, :], gam8[:, :], lng8[:, :], ALU.mult).then_inc(s["gb_step"], 1)
            dve.wait_ge(s["gb_step"], 3)
            nc.vector.tensor_tensor(gam8[:, :], gam8[:, :], lnb8[:, :], ALU.mult).then_inc(s["gb_step"], 1)
            dve.wait_ge(s["gb_step"], 4)
            nc.vector.tensor_tensor(bs8[:, :], gam8[:, :], bt8[:, :], ALU.add).then_inc(s["gb_step"], 2)

        @block.tensor
        def _(pe):
            pe.wait_ge(s["cond_in"], 16)
            pe.wait_ge(s["ld_wself"], 16)
            for f in range(FC):
                last = nc.tensor.matmul(bank[0:64, 0, :], cond64[:, f, :], wself_raw[:, FC + f, :],
                                        start=f == 0, stop=f == FC - 1)
            last.then_inc(s["sq_ready"], 1)
            pe.wait_ge(s["ld_x20"], 16 * FC)
            pe.wait_ge(s["zeroed"], 2)
            for f in range(FC):
                last = nc.tensor.matmul(bank[0:64, 1, 0:B * MP], ones64[:, :], x20[:, f, :],
                                        start=f == 0, stop=f == FC - 1)
            last.then_inc(s["rs_ready"], 1)
            pe.wait_ge(s["z_ready"], 1)
            pe.wait_ge(s["sq_split"], 1)
            for o in range(FC):
                out = bank[:, 4 + o, 0:B * MP]
                nc.tensor.matmul(out, t["sq"][:, o * P:(o + 1) * P], z20[:, :], start=True, stop=False)
                for f in range(FC):
                    last = nc.tensor.matmul(out, wself_raw[:, f, o * P:(o + 1) * P], x20[:, f, :],
                                            start=False, stop=f == FC - 1)
                last.then_inc(s["sf_ready"], 1)
            pe.wait_ge(s["ld_wk"], 16)
            pe.wait_ge(s["ld_wout"], 16)
            pe.wait_ge(s["ld_wq"], 16)
            pe.wait_ge(s["bq_in"], 16)
            pe.wait_ge(s["sf_done"], FC)
            for e in range(2):
                if e == 1:
                    pe.wait_ge(s["bias_done"], 2 * FC)
                for h in range(FC):
                    if h >= 2:
                        pe.wait_ge(s["kdiag_done"], HC * (FC * e + h - 1))
                    for f in range(FC):
                        last = nc.tensor.matmul(bank[:, 4 + h % 2, 0:B * MP], wk[:, e, f, h * P:(h + 1) * P],
                                                sf20[:, f, :], start=f == 0, stop=f == FC - 1)
                    last.then_inc(s["kh_ready"], 1)
                for g in range(2):
                    if e == 1:
                        pe.wait_ge(s["v_done"], g + 1)
                    for f in range(FC):
                        last = nc.tensor.matmul(bank[:, 6 + g, :], sf20[:, f, g * P:(g + 1) * P], wout[:, e, f, :],
                                                start=f == 0, stop=f == FC - 1)
                    last.then_inc(s["v_ready"], 1)
                pe.wait_ge(s["kdiag_done"], HC * FC * (e + 1))
                for f in range(FC):
                    for h in range(FC):
                        k = FC * (FC * e + f) + h
                        if k == 0:
                            pe.wait_ge(s["z_ready"], 1)
                        if k >= 2:
                            pe.wait_ge(s["m_done_dve"], k - 1)
                            pe.wait_ge(s["m_done_act"], k - 1)
                        for half in range(2):
                            nc.tensor.matmul(bank[:, 2 * (h % 2) + half, 0:4 * CK], wq[:, e, h, f * P:(f + 1) * P],
                                             kdiag[:, h, 4 * half:4 * half + 4, :], start=True, stop=True
                                             ).then_inc(s["m_ready"], 1)
                for h in range(FC):
                    for half in range(2):
                        n = 2 * (FC * e + h) + half
                        if n % 8 >= 2:
                            pe.wait_ge(s["bias_done"], n - 1)
                        last = nc.tensor.matmul(bank[0:64, 4 + n % 2, 0:4 * CK], bq64[:, e, h, :],
                                                kdiag[:, h, 4 * half:4 * half + 4, :], start=True, stop=True)
                        last.then_inc(s["bias_ready"], 1)
            pe.wait_ge(s["m_done_dve"], 2 * FC * FC)
            pe.wait_ge(s["m_done_act"], 2 * FC * FC)
            pe.wait_ge(s["ld_gb"], 32)
            for k, w in enumerate((wg, wb)):
                for f in range(FC):
                    last = nc.tensor.matmul(bank[0:B, 2 + k, :], cond64[:, f, 0:B], w[:, f, :],
                                            start=f == 0, stop=f == FC - 1)
                last.then_inc(s["gb_ready"], 1)


def graph(nc, t, d):
    with ExitStack() as ctx:
        def sb(name, shape, dt=F32):
            return ctx.enter_context(nc.sbuf_tensor(name, shape, dt))

        xraw = sb("xraw", [P, FC, N])
        xh, xl = sb("xh", [P, FC, N], F32R), sb("xl", [P, FC, N], F32R)
        xn = sb("xn", [P, NT, D])
        adj = sb("adj", [P, NT * 2 * NK, L], I32)
        adjw = sb("adjw", [P, NT * 2 * NK, L])
        cnt, vb, mask, blocked, cadd = (sb(n, [P, NT, 2, NK]) for n in ("cnt", "vb", "mask", "blocked", "cadd"))
        m = sb("m", [P, FC, 2, HK])
        vdiag = sb("vdiag", [CK, 2, 2, FC, P], F32R)
        z = sb("z", [64, N], F32R)
        sf2 = sb("sf", [P, 2, FC, N])
        ot = sb("ot", [P, FC, N])
        e = sb("e", [P, NT, 2, H, NK])
        mx, sm, rc = (sb(n, [P, NT, 2 * H]) for n in ("mx", "sm", "rc"))
        wth, wtl = sb("wth", [CK, 2, N], F32R), sb("wtl", [CK, 2, N], F32R)
        st = sb("st", [P, NT, 6])
        mv = sb("mv", [P, NT, 2])
        ve, rstd, nmr, mhalf = (sb(n, [P, NT]) for n in ("ve", "rstd", "nmr", "mhalf"))
        ln = sb("ln", [P, NT, D])
        hout = sb("hout", [P, FC, N])
        gcol, bcol = sb("gcol", [P, FC, B]), sb("bcol", [P, FC, B])
        onesr = sb("onesr", [64, P], F32R)
        ones64 = sb("g_ones64", [P, 64], F32R)
        bank = ctx.enter_context(nc.psum_tensor("g_bank", [P, 8, 512], F32))

        SFB = (0, 6, 7, 1)

        s = sems(nc, ctx, "x_t_in x_in adj_in m_in v_in gb_in set_up xh_done xl_done rs_ready z_done adjf_done adjw_done nmr_done sf_ready "
                          "sf_done adj_step sc_ready mult_done add_done mx_done sub_done exp_done sum_done "
                          "rc_done w_done wtr_ready wh_done wl_done att_mm att_done back_ready h_done "
                          "st_done mv_done ve_done rstd_done ln_done lnt_ready lnt_done h_stored t_stored")
        block = ctx.enter_context(nc.Block())

        def steps(eng, step):
            step(1, 1, False)
            step(2, 0, False)
            with eng.Fori(1, B // 2 - 1) as k:
                step(2 * k + 1, 1, False)
                step(2 * k + 2, 0, False)
            step(B - 1, 1, True)

        def heads(x):
            return x.unsqueeze(2).broadcast_to([P, 2, H, NK])

        def keys(x):
            return x.unsqueeze(2).broadcast_to([P, 2 * H, NK])

        @block.sync
        def _(sp):
            for c in range(FC):
                for k, dst in enumerate((gcol, bcol)):
                    sp.dma_start(dst[:, c, :], d["gb_rows"][:, k, c * P:(c + 1) * P].rearrange("b p -> p b"),
                                 allow_slow_non_contiguous=True).then_inc(s["gb_in"], 16)
            sp.wait_ge(s["set_up"], 2)

            def load_first(b):
                sp.dma_start(xraw[:, :, :], d["x_t"][ds(b, 1)].rearrange("o p c n -> (o p) c n")).then_inc(s["x_t_in"], 16)

            def load_adj(b):
                sp.dma_start(adj[:, :, :], d["adj"][ds(b, 1)].rearrange("o p k l -> (o p) k l")).then_inc(s["adj_in"], 16)

            def load_m(b):
                sp.dma_start(m[:, :, :, :], d["m_rows"][ds(b, 1)].rearrange("o p c e k -> (o p) c e k")).then_inc(s["m_in"], 16)

            def load_v(b):
                for part in range(2):
                    for dr in range(2):
                        for j in range(HC):
                            sp.dma_start(
                                vdiag[NK * j:NK * j + NK, part, dr, :, DH * j:DH * j + DH].bitcast(F32),
                                d["v_rows"][part, dr, ds(b * MP, NK), :].rearrange(
                                    "m (c j g) -> m c j g", c=FC, j=HC)[:, :, j, :]).then_inc(s["v_in"], 16)

            def load_x(b):
                sp.dma_start(xn[:, :, :], d["x"][ds(b, 1)].rearrange("o (t p) f -> (o p) t f", p=P)).then_inc(s["x_in"], 16)

            def store_h(b, four):
                sp.wait_ge(s["h_done"], four)
                sp.dma_start(d["h_rows"][ds(b, 1)].rearrange("o p t f -> (o p) t f"), xn[:, :, :]).then_inc(s["h_stored"], 16)

            def store_t(b, four):
                sp.wait_ge(s["lnt_done"], four)
                sp.dma_start(d["t_rows"][ds(b, 1)].rearrange("o p c n -> (o p) c n"), hout[:, :, :]).then_inc(s["t_stored"], 16)

            def step(b, par, last):
                if not last:
                    sp.wait_ge(s["xl_done"], 4 * b + 4)
                    load_first(b + 1)
                    sp.wait_ge(s["adj_step"], 5 * b + 5)
                    load_adj(b + 1)
                if not (isinstance(b, int) and b == 1):
                    store_t(b - 2, 4 * b - 4)
                sp.wait_ge(s["att_mm"], 8 * b)
                load_v(b)
                store_h(b - 1, 4 * b)
                sp.wait_ge(s["h_stored"], 16 * b)
                sp.wait_ge(s["ln_done"], 4 * b)
                load_x(b)
                if not last:
                    sp.wait_ge(s["sc_ready"], 4 * b + 4)
                    load_m(b + 1)

            load_first(0)
            load_adj(0)
            load_m(0)
            load_v(0)
            load_x(0)
            sp.wait_ge(s["xl_done"], 4)
            load_first(1)
            sp.wait_ge(s["adj_step"], 5)
            load_adj(1)
            sp.wait_ge(s["sc_ready"], 4)
            load_m(1)
            steps(sp, step)
            store_t(B - 2, 4 * B - 4)
            store_h(B - 1, 4 * B)
            store_t(B - 1, 4 * B)
            sp.wait_ge(s["h_stored"], 16 * B)
            sp.wait_ge(s["t_stored"], 16 * B)

        @block.gpsimd
        def _(pool):
            nc.gpsimd.memset(vdiag[:, :, :, :, :].bitcast(F32), 0.0).then_inc(s["set_up"], 1)
            nc.gpsimd.memset(onesr[:, :].bitcast(F32), 1.0).then_inc(s["set_up"], 1)
            nc.gpsimd.memset(ones64[:, :].bitcast(F32), 1.0).then_inc(s["set_up"], 1)
            nc.gpsimd.memset(mhalf[:, :], -0.5).then_inc(s["set_up"], 1)

            def front(b):
                pool.wait_ge(s["sf_ready"], 4 * b)
                for f in range(FC):
                    pool.wait_ge(s["xh_done"], 4 * b + f + 1)
                    nc.gpsimd.tensor_tensor(xl[:, f, :], xraw[:, f, :], xh[:, f, :].bitcast(F32),
                                            ALU.subtract).then_inc(s["xl_done"], 1)

            def label_products(b):
                pool.wait_ge(s["adjf_done"], b + 1)
                nc.gpsimd.tensor_tensor(adjw[:, :, :], adjw[:, :, :], t["wbias"][:, :].unsqueeze(1).broadcast_to(
                    [P, NT * 2 * NK, L]), ALU.mult).then_inc(s["adjw_done"], 1)

            def softmax(b):
                for i in range(NT + 2):
                    if i < NT:
                        pool.wait_ge(s["mult_done"], 4 * b + i + 1)
                        nc.gpsimd.tensor_tensor(e[:, i], e[:, i], heads(cadd[:, i]), ALU.add).then_inc(s["add_done"], 1)
                    if i >= 2:
                        pool.wait_ge(s["rc_done"], 4 * b + i - 1)
                        pool.wait_ge(s["exp_done"], 4 * b + i - 1)
                        v = e[:, i - 2].rearrange("p e h k -> p (e h) k")
                        nc.gpsimd.tensor_tensor(v, v, keys(rc[:, i - 2]), ALU.mult).then_inc(s["w_done"], 1)

            def back(b):
                pool.wait_ge(s["ve_done"], 2 * b + 2)
                nc.gpsimd.tensor_tensor(rstd[:, :], ve[:, :], mhalf[:, :], ALU.pow).then_inc(s["rstd_done"], 1)

            def step(b, par, last):
                if not last:
                    front(b + 1)
                back(b - 1)
                softmax(b)
                if not last:
                    label_products(b + 1)

            pool.wait_ge(s["set_up"], 4)
            front(0)
            label_products(0)
            front(1)
            softmax(0)
            label_products(1)
            steps(pool, step)
            back(B - 1)

        @block.scalar
        def _(act):
            act.wait_ge(s["gb_in"], 16 * 2 * FC)

            def hi_chunk(b, f):
                if f == 0:
                    act.wait_ge(s["x_t_in"], 16 * b + 16)
                    act.wait_ge(s["sf_ready"], 4 * b)
                nc.scalar.activation(xh[:, f, :], xraw[:, f, :], ACT.Copy).then_inc(s["xh_done"], 1)

            def self_features(b, par):
                act.wait_ge(s["att_done"], 4 * b - 4 if not isinstance(b, int) else max(4 * b - 4, 0))
                for o in range(FC):
                    act.wait_ge(s["sf_ready"], 4 * b + o + 1)
                    nc.scalar.activation(sf2[:, par, o, :], bank[:, SFB[o], :], ACT.Identity,
                                         bias=t["bself"][:, o:o + 1]).then_inc(s["sf_done"], 1)

            def normalise(b):
                act.wait_ge(s["lnt_ready"], 4 * b)
                act.wait_ge(s["rstd_done"], b + 1)
                act.wait_ge(s["nmr_done"], b + 1)
                for i in range(NT):
                    nc.scalar.activation(ln[:, i, :], xn[:, i, :], ACT.Identity, bias=nmr[:, i:i + 1],
                                         scale=rstd[:, i:i + 1]).then_inc(s["ln_done"], 1)

            def labels_float(b):
                act.wait_ge(s["adj_in"], 16 * b + 16)
                act.wait_ge(s["adj_step"], 5 * b)
                nc.scalar.activation(adjw[:, :, :], adj[:, :, :], ACT.Copy).then_inc(s["adjf_done"], 1)

            def exps(b):
                for i in range(NT):
                    act.wait_ge(s["sub_done"], 4 * b + i + 1)
                    nc.scalar.activation(e[:, i], e[:, i], ACT.Exp).then_inc(s["exp_done"], 1)

            def hi_weights(b, i):
                act.wait_ge(s["wtr_ready"], 8 * b + i + 1)
                if i >= 1:
                    act.wait_ge(s["att_mm"], 8 * b + i - 1)
                nc.scalar.activation(wth[:, i % 2, :], bank[0:CK, 6 + i % 2, :], ACT.Copy).then_inc(s["wh_done"], 1)

            def scale_ln(b, f):
                if f == 0:
                    act.wait_ge(s["t_stored"], 16 * b)
                act.wait_ge(s["lnt_ready"], 4 * b + f + 1)
                nc.scalar.activation(hout[:, f, :], bank[:, 2 + f, :], ACT.Identity,
                                     bias=bcol[:, f, ds(b, 1)], scale=gcol[:, f, ds(b, 1)]).then_inc(s["lnt_done"], 1)

            def step(b, par, last):
                self_features(b, par)
                for i in range(2 * FC):
                    hi_weights(b - 1, i)
                    if i < FC:
                        if not last:
                            hi_chunk(b + 1, i)
                    elif not (isinstance(b, int) and b == 1):
                        scale_ln(b - 2, i - FC)
                normalise(b - 1)
                exps(b)
                if not last:
                    labels_float(b + 1)

            for f in range(FC):
                hi_chunk(0, f)
            labels_float(0)
            self_features(0, 0)
            for f in range(FC):
                hi_chunk(1, f)
            exps(0)
            labels_float(1)
            steps(act, step)
            for i in range(2 * FC):
                hi_weights(B - 1, i)
                if i >= FC:
                    scale_ln(B - 2, i - FC)
            normalise(B - 1)
            for f in range(FC):
                scale_ln(B - 1, f)

        @block.vector
        def _(dve):
            def nonzero_rows(b):
                dve.wait_ge(s["rs_ready"], b + 1)
                dve.wait_ge(s["sf_ready"], 4 * b)
                nc.vector.tensor_scalar(z[:, :], bank[0:64, 1, :], 0.0, t["hot"][:, ds(b, 1)],
                                        ALU.not_equal, ALU.mult).then_inc(s["z_done"], 1)

            def labels(b):
                dve.wait_ge(s["adj_in"], 16 * b + 16)
                dve.wait_ge(s["w_done"], 4 * b)
                flat = "p t e k -> p (t e k)"
                nc.vector.tensor_reduce(cnt[:].rearrange(flat), adj[:, :, :], AX, ALU.add).then_inc(s["adj_step"], 1)
                dve.wait_ge(s["adjw_done"], b + 1)
                nc.vector.tensor_reduce(vb[:].rearrange(flat), adjw[:, :, :], AX, ALU.add).then_inc(s["adj_step"], 1)
                dve.wait_ge(s["adj_step"], 5 * b + 1)
                nc.vector.tensor_scalar(mask[:].rearrange(flat), cnt[:].rearrange(flat), 0.0, None,
                                        ALU.is_gt).then_inc(s["adj_step"], 1)
                nc.vector.tensor_scalar(blocked[:].rearrange(flat), cnt[:].rearrange(flat), 0.0, NEG,
                                        ALU.is_le, ALU.mult).then_inc(s["adj_step"], 1)
                dve.wait_ge(s["adj_step"], 5 * b + 4)
                nc.vector.scalar_tensor_tensor(cadd[:].rearrange(flat), vb[:].rearrange(flat), t["bbias"][:, 0:1],
                                               blocked[:].rearrange(flat), ALU.add, ALU.add).then_inc(s["adj_step"], 1)

            def softmax(b):
                dve.wait_ge(s["adj_step"], 5 * b + 5)
                dve.wait_ge(s["wtr_ready"], 8 * b)
                for i in range(NT + 2):
                    if i < NT:
                        dve.wait_ge(s["sc_ready"], 4 * b + i + 1)
                        sc = bank[:, 2 + 2 * (i % 2):4 + 2 * (i % 2), 0:HK].rearrange("p e (h k) -> p e h k", h=H)
                        nc.vector.tensor_tensor(e[:, i], sc, heads(mask[:, i]), ALU.mult).then_inc(s["mult_done"], 1)
                    if 1 <= i <= NT:
                        v = e[:, i - 1].rearrange("p e h k -> p (e h) k")
                        dve.wait_ge(s["add_done"], 4 * b + i)
                        nc.vector.tensor_reduce(mx[:, i - 1], v, AX, ALU.max).then_inc(s["mx_done"], 1)
                        dve.wait_ge(s["mx_done"], 4 * b + i)
                        nc.vector.tensor_tensor(v, v, keys(mx[:, i - 1]), ALU.subtract).then_inc(s["sub_done"], 1)
                    if i >= 2:
                        v = e[:, i - 2].rearrange("p e h k -> p (e h) k")
                        dve.wait_ge(s["exp_done"], 4 * b + i - 1)
                        nc.vector.tensor_reduce(sm[:, i - 2], v, AX, ALU.add).then_inc(s["sum_done"], 1)
                        dve.wait_ge(s["sum_done"], 4 * b + i - 1)
                        nc.vector.reciprocal(rc[:, i - 2], sm[:, i - 2]).then_inc(s["rc_done"], 1)

            def attention(b, par):
                dve.wait_ge(s["sf_done"], 4 * b + 4)
                dve.wait_ge(s["back_ready"], 4 * b)
                for i in range(2 * FC + 1):
                    if i < 2 * FC:
                        dve.wait_ge(s["wh_done"], 8 * b + i + 1)
                        nc.vector.tensor_tensor(wtl[:, i % 2, :], bank[0:CK, 6 + i % 2, :],
                                                wth[:, i % 2, :].bitcast(F32), ALU.subtract).then_inc(s["wl_done"], 1)
                    if i >= 2 and i % 2 == 0:
                        c = i // 2 - 1
                        dve.wait_ge(s["att_mm"], 8 * b + 2 * c + 2)
                        nc.vector.scalar_tensor_tensor(ot[:, c, :], bank[:, (c + 1) % 2, :], t["boutc"][:, c:c + 1],
                                                       sf2[:, par, c, :], ALU.add, ALU.add).then_inc(s["att_done"], 1)

            def residual_ln(b):
                dve.wait_ge(s["x_in"], 16 * b + 16)
                for i in range(NT):
                    dve.wait_ge(s["back_ready"], 4 * b + i + 1)
                    nc.vector.scalar_tensor_tensor(xn[:, i, :], bank[:, 6 + i % 2, :], 0.0, xn[:, i, :],
                                                   ALU.max, ALU.add).then_inc(s["h_done"], 1)
                for i in range(NT):
                    dve.wait_ge(s["h_done"], 4 * b + i + 1)
                    if i:
                        dve.wait_ge(s["st_done"], 4 * b + i)
                    nc.vector.bn_stats(st[:, i, :], xn[:, i, :]).then_inc(s["st_done"], 1)
                    if i:
                        nc.vector.bn_aggr(mv[:, i - 1, :], st[:, i - 1, :]).then_inc(s["mv_done"], 1)
                dve.wait_ge(s["st_done"], 4 * b + NT)
                dve.wait_ge(s["mv_done"], 4 * b + NT - 1)
                nc.vector.tensor_scalar(ve[:, 0:NT - 1], mv[:, 0:NT - 1, 1], EPS, None, ALU.add).then_inc(s["ve_done"], 1)
                nc.vector.bn_aggr(mv[:, NT - 1, :], st[:, NT - 1, :]).then_inc(s["mv_done"], 1)
                dve.wait_ge(s["mv_done"], 4 * b + NT)
                nc.vector.tensor_scalar(ve[:, NT - 1:NT], mv[:, NT - 1:NT, 1], EPS, None, ALU.add).then_inc(s["ve_done"], 1)
                dve.wait_ge(s["rstd_done"], b + 1)
                nc.vector.scalar_tensor_tensor(nmr[:, :], mv[:, :, 0], -1.0, rstd[:, :],
                                               ALU.mult, ALU.mult).then_inc(s["nmr_done"], 1)

            def step(b, par, last):
                attention(b - 1, 1 - par)
                residual_ln(b - 1)
                softmax(b)
                if not last:
                    nonzero_rows(b + 1)
                    labels(b + 1)

            nonzero_rows(0)
            labels(0)
            softmax(0)
            nonzero_rows(1)
            labels(1)
            steps(dve, step)
            attention(B - 1, 1)
            residual_ln(B - 1)

        @block.tensor
        def _(pe):
            def self_features(b):
                if not (isinstance(b, int) and b == 0):
                    pe.wait_ge(s["att_done"], 4 * b - 4)
                    pe.wait_ge(s["h_done"], 4 * b - 4)
                pe.wait_ge(s["xh_done"], 4 * b + 4)
                pe.wait_ge(s["xl_done"], 4 * b + 4)
                for f in range(FC):
                    nc.tensor.matmul(bank[0:64, 1, :], ones64[:, :], xh[:, f, :], start=f == 0, stop=False)
                    last = nc.tensor.matmul(bank[0:64, 1, :], ones64[:, :], xl[:, f, :],
                                            start=False, stop=f == FC - 1)
                last.then_inc(s["rs_ready"], 1)
                for o in range(FC):
                    if o == FC - 1:
                        pe.wait_ge(s["z_done"], b + 1)
                    out, col = bank[:, SFB[o], :], slice(o * P, (o + 1) * P)
                    for f in range(FC):
                        mm3(nc, out, t["w1h"][:, f, col], t["w1l"][:, f, col], xh[:, f, :], xl[:, f, :], f == 0, False)
                for o in range(FC):
                    nc.tensor.matmul(bank[:, SFB[o], :], t["sq"][:, o * P:(o + 1) * P], z[:, :],
                                     start=False, stop=True).then_inc(s["sf_ready"], 1)

            def scores(b, par, first, end):
                if first == 0:
                    pe.wait_ge(s["m_in"], 16 * b + 16)
                    pe.wait_ge(s["sf_done"], 4 * b + 4)
                    if not isinstance(b, int) or b >= 2:
                        pe.wait_ge(s["lnt_done"], 4 * b - 4)
                for i in range(first, end):
                    pe.wait_ge(s["mult_done"], 4 * b + max(i - 1, 0))
                    for dr in range(2):
                        out = bank[:, 2 + 2 * (i % 2) + dr, 0:HK]
                        for f in range(FC):
                            nc.tensor.matmul(out, sf2[:, par, f, i * P:(i + 1) * P], m[:, f, dr, :],
                                             start=f == 0, stop=False)
                        last = nc.tensor.matmul(out, onesr[:, :],
                                                t["bias_rows"][:, ds(b, 1), dr, :].rearrange("p o k -> p (o k)"),
                                                start=False, stop=True)
                    last.then_inc(s["sc_ready"], 1)

            def attention(b):
                pe.wait_ge(s["w_done"], 4 * b + 4)
                pe.wait_ge(s["v_in"], 16 * 16 * b + 16 * 16)
                pe.wait_ge(s["sf_done"], (4 * b + 8) if not isinstance(b, int) else min(4 * b + 8, 4 * B))
                for i in range(2 * FC + 1):
                    if i < 2 * FC:
                        c, dr = divmod(i, 2)
                        if i >= 2:
                            pe.wait_ge(s["wl_done"], 8 * b + i - 1)
                        for n in range(NT):
                            last = nc.tensor.transpose(
                                bank[0:CK, 6 + i % 2, n * P:(n + 1) * P],
                                e[:, n, dr, HC * c:HC * c + HC, :].rearrange("p h k -> p (h k)"), t["ident"][:, :])
                        last.then_inc(s["wtr_ready"], 1)
                    if i >= 1:
                        k = i - 1
                        c, dr = divmod(k, 2)
                        pe.wait_ge(s["wl_done"], 8 * b + k + 1)
                        if dr == 0 and c >= 2:
                            pe.wait_ge(s["att_done"], 4 * b + c - 1)
                        last = mm3(nc, bank[:, (c + 1) % 2, :], vdiag[:, 0, dr, c, :], vdiag[:, 1, dr, c, :],
                                   wth[:, k % 2, :], wtl[:, k % 2, :], dr == 0, dr == 1)
                        last.then_inc(s["att_mm"], 1)

            def back(b):
                pe.wait_ge(s["att_done"], 4 * b + 4)
                pe.wait_ge(s["wl_done"], 8 * b + 8)
                for i in range(NT):
                    if i >= 2:
                        pe.wait_ge(s["h_done"], 4 * b + i - 1)
                    for f in range(FC):
                        last = nc.tensor.transpose(bank[:, 6 + i % 2, f * P:(f + 1) * P],
                                                   ot[:, f, i * P:(i + 1) * P], t["ident"][:, :])
                    last.then_inc(s["back_ready"], 1)

            def ln_t(b, after):
                pe.wait_ge(s["ln_done"], 4 * b + 4)
                pe.wait_ge(s["mult_done"], 4 * (b + after) + 4)
                for f in range(FC):
                    for i in range(NT):
                        last = nc.tensor.transpose(bank[:, 2 + f, i * P:(i + 1) * P],
                                                   ln[:, i, f * P:(f + 1) * P], t["ident"][:, :])
                    last.then_inc(s["lnt_ready"], 1)

            def step(b, par, last):
                self_features(b)
                if not (isinstance(b, int) and b == 1):
                    ln_t(b - 2, 1)
                attention(b - 1)
                scores(b, par, 0, 1)
                back(b - 1)
                scores(b, par, 1, NT)

            pe.wait_ge(s["set_up"], 4)
            self_features(0)
            scores(0, 0, 0, NT)
            steps(pe, step)
            ln_t(B - 2, 1)
            attention(B - 1)
            back(B - 1)
            pe.wait_ge(s["lnt_done"], 4 * B - 4)
            ln_t(B - 1, 0)


def split_weights(nc, t, d):
    with ExitStack() as ctx:
        raw = ctx.enter_context(nc.sbuf_tensor("w_raw", [P, 4, FC, D], F32))
        s = sems(nc, ctx, "w_in0 w_in1 w_in2 w_in3 w_hi w_lo")
        w_in = (s["w_in0"], s["w_in1"], s["w_in2"], s["w_in3"])
        block = ctx.enter_context(nc.Block())
        dst = [(t["wqkh"][:, :, 0:D], t["wqkl"][:, :, 0:D]), (t["wqkh"][:, :, D:2 * D], t["wqkl"][:, :, D:2 * D]),
               (t["wvh"][:, :, :], t["wvl"][:, :, :]), (t["wph"][:, :, :], t["wpl"][:, :, :])]

        @block.sync
        def _(sp):
            for k in range(4):
                src = d["wqkv_t"][:, k, :] if k < 3 else d["wp_t"]
                sp.dma_start(raw[:, k], src.rearrange("(c p) o -> p c o", p=P)).then_inc(w_in[k], 16)

        @block.vector
        def _(dve):
            for k in range(4):
                dve.wait_ge(w_in[k], 16)
                nc.vector.tensor_copy(dst[k][0], raw[:, k]).then_inc(s["w_hi"], 1)
                dve.wait_ge(s["w_hi"], k + 1)
                nc.vector.tensor_tensor(dst[k][1], raw[:, k], dst[k][0].bitcast(F32), ALU.subtract).then_inc(s["w_lo"], 1)


def attention(nc, t, d):
    with ExitStack() as ctx:
        def sb(name, shape, dt=F32):
            return ctx.enter_context(nc.sbuf_tensor(name, shape, dt))

        traw = sb("traw", [P, FC, N])
        hh, hl = sb("hh", [P, FC, N], F32R), sb("hl", [P, FC, N], F32R)
        h = sb("h", [P, NT, D])
        qh, ql, kh, kl = (sb(n, [P, N], F32R) for n in ("qh", "ql", "kh", "kl"))
        sq, sk = sb("sq_stack", [P, 2, HC, N], F32R), sb("sk_stack", [P, 2, HC, N], F32R)
        v = sb("v", [P, 2, NT, D])
        pt = sb("pt", [P, NT, 2, N])
        oraw, den, rden, o = (sb(n, [P, N]) for n in ("oraw", "den", "rden", "o"))
        oh, ol = sb("oh", [P, FC, N], F32R), sb("ol", [P, FC, N], F32R)
        rows = sb("rows", [P, 2, D])
        bp = sb("bp", [P, D])
        bcol3, bvs = sb("bcol3", [P, 3, FC]), sb("bvs", [P, FC])
        ln = sb("ln2", [P, NT, D])
        ones32 = sb("ones32", [P, DH])
        mx = sb("mx2", [P, 2, NT, 2])
        shift = sb("shift", [P, NT, 2, 2], F32R)
        st, mv = sb("st2", [P, NT, 6]), sb("mv2", [P, NT, 2])
        ve, rstd, nmr, mhalf = (sb(n, [P, NT]) for n in ("ve2", "rstd2", "nmr2", "mhalf2"))
        bank = ctx.enter_context(nc.psum_tensor("a_bank", [P, 8, 512], F32))

        s = sems(nc, ctx, "ld_c t_in h_in rows_in stk00 stk01 stk10 stk11 set_up bv_done hh_done hl_done q_ready "
                          "k_ready qh_done ql_done kh_done kl_done e_ready emax_done sh_hi sh_lo sh_ready shrow_done "
                          "et_ready exp_done pv_done den_done oraw_done rden_done o_done oh_done ol_done v_ready v_done "
                          "pj_ready hb_done h1_done st_done mv_done ve_done rstd_done nmr_done ln_done mulg_done "
                          "addb_done y_done y_out")
        stk = ((s["stk00"], s["stk01"]), (s["stk10"], s["stk11"]))
        STK = 16 * 12
        PAIRS = H // 2
        block = ctx.enter_context(nc.Block())

        def ahead(b, c, k):
            return (b, c + k) if c + k < FC else (b + 1, c + k - FC)

        def next_pair(b, p, more):
            if p + 1 < PAIRS:
                return b, p + 1
            return (b + 1, 0) if more else None

        def use(b, c):
            return 2 * b + c // 2

        def first(b):
            return isinstance(b, int) and b == 0

        def batches(eng, batch):
            batch(0, 0, True)
            with eng.Fori(0, B // 2 - 1) as k:
                batch(2 * k + 1, 1, True)
                batch(2 * k + 2, 0, True)
            batch(B - 1, 1, False)

        @block.sync
        def _(sp):
            sp.dma_start(bcol3[:, :, :], d["bqkc"]).then_inc(s["ld_c"], 16)
            sp.dma_start(bp[:, :], d["bp"].partition_broadcast(P)).then_inc(s["ld_c"], 16)

            def load_t(b):
                sp.dma_start(traw[:, :, :], d["t_rows"][ds(b, 1)].rearrange("o p c n -> (o p) c n")).then_inc(s["t_in"], 16)

            def load_h(b):
                sp.dma_start(h[:, :, :], d["h_rows"][ds(b, 1)].rearrange("o p t f -> (o p) t f")).then_inc(s["h_in"], 16)
                sp.dma_start(rows[:, :, :], d["gb_rows"][ds(b, 1)].rearrange("o k f -> (o k f)").partition_broadcast(P)
                             .rearrange("p (k f) -> p k f", k=2)).then_inc(s["rows_in"], 16)

            def store_y(b):
                sp.dma_start(d["out"][ds(b, 1)].rearrange("o (t p) f -> (o p) t f", p=P), ln[:, :, :]).then_inc(s["y_out"], 16)

            def stacks(c, n):
                par = c % 2
                for half in range(2):
                    for ready, src, dst, at in ((s["qh_done"], qh, sq, (0, 2 * DH)), (s["ql_done"], ql, sq, (DH,)),
                                                (s["kh_done"], kh, sk, (0, DH)), (s["kl_done"], kl, sk, (2 * DH,))):
                        if half == 0:
                            sp.wait_ge(ready, n)
                        for r in at:
                            for j in (2 * half, 2 * half + 1):
                                sp.dma_start(dst[r:r + DH, par, j, :].bitcast(F32),
                                             src[DH * j:DH * j + DH, :].bitcast(F32)).then_inc(stk[par][half], 16)

            def batch(b, bpar, more):
                for p in range(PAIRS):
                    c = p // 2
                    if p % 2 == 0 and (c < 3 or more):
                        stacks((c + 1) % FC, 4 * b + c + 2)
                    if p == 1 and more:
                        sp.wait_ge(s["hl_done"], 4 * b + 4)
                        load_t(b + 1)
                    if p == 7:
                        if first(b):
                            load_h(b)
                        else:
                            sp.wait_ge(s["y_done"], 4 * b)
                            store_y(b - 1)
                            load_h(b)

            load_t(0)
            sp.wait_ge(s["set_up"], 4)
            stacks(0, 1)
            batches(sp, batch)
            sp.wait_ge(s["y_done"], 4 * B)
            store_y(B - 1)
            sp.wait_ge(s["y_out"], 16 * B)

        @block.gpsimd
        def _(pool):
            nc.gpsimd.memset(sk[3 * DH:, :, :, :].bitcast(F32), 1.0).then_inc(s["set_up"], 1)
            pool.wait_ge(s["set_up"], 1)
            nc.gpsimd.memset(sq[3 * DH:, :, :, :].bitcast(F32), 0.0).then_inc(s["set_up"], 1)
            pool.wait_ge(s["set_up"], 2)
            nc.gpsimd.memset(ones32[:, :], 1.0).then_inc(s["set_up"], 1)
            nc.gpsimd.memset(mhalf[:, :], -0.5).then_inc(s["set_up"], 1)

            def split_h(b):
                for f in range(FC):
                    pool.wait_ge(s["hh_done"], 4 * b + f + 1)
                    nc.gpsimd.tensor_tensor(hl[:, f, :], traw[:, f, :], hh[:, f, :].bitcast(F32),
                                            ALU.subtract).then_inc(s["hl_done"], 1)

            def add_bp(b):
                pool.wait_ge(s["h_in"], 16 * b + 16)
                nc.gpsimd.tensor_tensor(h[:, :, :], h[:, :, :], bp[:, :].unsqueeze(1).broadcast_to([P, NT, D]),
                                        ALU.add).then_inc(s["hb_done"], 1)

            def rsqrt(b):
                pool.wait_ge(s["ve_done"], 2 * b + 2)
                nc.gpsimd.tensor_tensor(rstd[:, :], ve[:, :], mhalf[:, :], ALU.pow).then_inc(s["rstd_done"], 1)

            def result(b, i):
                if i == 0:
                    pool.wait_ge(s["rows_in"], 16 * b + 16)
                pool.wait_ge(s["ln_done"], 4 * b + i + 1)
                nc.gpsimd.tensor_tensor(ln[:, i, :], ln[:, i, :], rows[:, 0, :], ALU.mult).then_inc(s["mulg_done"], 1)
                nc.gpsimd.tensor_tensor(h[:, i, :], h[:, i, :], rows[:, 1, :], ALU.add).then_inc(s["addb_done"], 1)
                pool.wait_ge(s["mulg_done"], 4 * b + i + 1)
                pool.wait_ge(s["addb_done"], 4 * b + i + 1)
                nc.gpsimd.tensor_tensor(ln[:, i, :], ln[:, i, :], h[:, i, :], ALU.add).then_inc(s["y_done"], 1)

            def batch(b, bpar, more):
                for p in range(PAIRS):
                    if not first(b):
                        if p == 0:
                            add_bp(b - 1)
                        if p == 3:
                            rsqrt(b - 1)
                        if p == 5:
                            result(b - 1, 0)
                            result(b - 1, 1)
                        if p == 6:
                            result(b - 1, 2)
                            result(b - 1, 3)
                    if p == 4 and more:
                        split_h(b + 1)

            pool.wait_ge(s["set_up"], 4)
            pool.wait_ge(s["ld_c"], 32)
            split_h(0)
            batches(pool, batch)
            add_bp(B - 1)
            rsqrt(B - 1)
            for i in range(NT):
                result(B - 1, i)

        @block.scalar
        def _(act):
            def split_h(b, f):
                if f == 0:
                    act.wait_ge(s["t_in"], 16 * b + 16)
                    act.wait_ge(s["k_ready"], 4 * b)
                nc.scalar.activation(hh[:, f, :], traw[:, f, :], ACT.Copy).then_inc(s["hh_done"], 1)

            def project(b, c):
                g = 4 * b + c
                if not (isinstance(b, int) and g == 0):
                    prev = (b, c - 1) if c else (b - 1, FC - 1)
                    for half in range(2):
                        act.wait_ge(stk[prev[1] % 2][half], STK * (use(*prev) + 1))
                act.wait_ge(s["q_ready"], g + 1)
                nc.scalar.activation(qh[:, :], bank[:, 6, :], ACT.Identity, bias=bcol3[:, 0, c:c + 1]).then_inc(s["qh_done"], 1)
                act.wait_ge(s["k_ready"], g + 1)
                nc.scalar.activation(kh[:, :], bank[:, 7, :], ACT.Identity, bias=bcol3[:, 1, c:c + 1]).then_inc(s["kh_done"], 1)

            def values(b, vpar, i):
                if i == 0 and not first(b):
                    act.wait_ge(s["pv_done"], 32 * b - 32)
                act.wait_ge(s["v_ready"], 4 * b + i + 1)
                nc.scalar.activation(v[:, vpar, i, :], bank[:, 6 + i % 2, :], ACT.Copy).then_inc(s["v_done"], 1)

            def shift_rows(b, p):
                for k in range(2):
                    act.wait_ge(s["sh_ready"], 2 * (PAIRS * b + p) + k + 1)
                    nc.scalar.activation(sq[3 * DH:3 * DH + 2, (p // 2) % 2, 2 * (p % 2) + k, :],
                                         bank[3 * DH:3 * DH + 2, 2 + k, :], ACT.Copy).then_inc(s["shrow_done"], 1)

            def exps(b, p, i):
                G = PAIRS * b + p
                if not (isinstance(b, int) and G == 0):
                    act.wait_ge(s["pv_done"], 4 * G + i - 3)
                for k in range(2):
                    act.wait_ge(s["et_ready"], 8 * G + 2 * i + k + 1)
                    nc.scalar.activation(pt[:, i, k, :], bank[:, k, :], ACT.Exp).then_inc(s["exp_done"], 1)

            def outputs(b, p):
                G = PAIRS * b + p
                a, r = slice(64 * (p % 2), 64 * (p % 2) + 64), slice(64 - 64 * (p % 2), 128 - 64 * (p % 2))
                act.wait_ge(s["pv_done"], 4 * G + 4)
                if not (isinstance(b, int) and G < 2):
                    act.wait_ge(s["o_done"], 4 * b + p // 2)
                nc.scalar.activation(den[a, :], bank[r, 4 + p % 2, :], ACT.Copy).then_inc(s["den_done"], 1)
                nc.scalar.activation(oraw[a, :], bank[a, 4 + p % 2, :], ACT.Copy).then_inc(s["oraw_done"], 1)

            def output_hi(b, c):
                g = 4 * b + c
                act.wait_ge(s["o_done"], g + 1)
                act.wait_ge(s["pj_ready"], 4 * b)
                nc.scalar.activation(oh[:, c, :], o[:, :], ACT.Identity, bias=bvs[:, c:c + 1]).then_inc(s["oh_done"], 1)

            def normalise(b):
                act.wait_ge(s["y_out"], 16 * b)
                act.wait_ge(s["rstd_done"], b + 1)
                act.wait_ge(s["nmr_done"], b + 1)
                for i in range(NT):
                    nc.scalar.activation(ln[:, i, :], h[:, i, :], ACT.Identity, bias=nmr[:, i:i + 1],
                                         scale=rstd[:, i:i + 1]).then_inc(s["ln_done"], 1)

            def batch(b, bpar, more):
                for p in range(PAIRS):
                    if p:
                        outputs(b, p - 1)
                    elif not first(b):
                        outputs(b - 1, PAIRS - 1)
                    exps(b, p, 0)
                    if p % 2 and p > 1:
                        output_hi(b, p // 2 - 1)
                    elif p == 1 and not first(b):
                        output_hi(b - 1, FC - 1)
                    exps(b, p, 1)
                    exps(b, p, 2)
                    exps(b, p, 3)
                    if p == 4 and not first(b):
                        normalise(b - 1)
                    if p % 2 and (p < 4 or more):
                        project(*ahead(b, p // 2, 2))
                    if p in (4, 6) and more:
                        values(b + 1, 1 - bpar, p - 4)
                        values(b + 1, 1 - bpar, p - 3)
                    if next_pair(b, p, more):
                        shift_rows(*next_pair(b, p, more))
                    if p == 3 and more:
                        for f in range(FC):
                            split_h(b + 1, f)

            act.wait_ge(s["ld_c"], 32)
            act.wait_ge(s["set_up"], 4)
            for f in range(FC):
                split_h(0, f)
            project(0, 0)
            project(0, 1)
            for i in range(NT):
                values(0, 0, i)
            shift_rows(0, 0)
            act.wait_ge(s["bv_done"], 1)
            batches(act, batch)
            outputs(B - 1, PAIRS - 1)
            output_hi(B - 1, FC - 1)
            normalise(B - 1)

        @block.vector
        def _(dve):
            def lo_parts(b, c):
                for src, col, hi, lo, hi_done, lo_done in ((6, 0, qh, ql, s["qh_done"], s["ql_done"]),
                                                           (7, 1, kh, kl, s["kh_done"], s["kl_done"])):
                    dve.wait_ge(hi_done, 4 * b + c + 1)
                    nc.vector.scalar_tensor_tensor(lo[:, :], bank[:, src, :], bcol3[:, col, c:c + 1],
                                                   hi[:, :].bitcast(F32), ALU.add, ALU.subtract).then_inc(lo_done, 1)

            def maximum(b, p, i):
                dve.wait_ge(s["e_ready"], 8 * (PAIRS * b + p) + i + 1)
                k, n = divmod(i, NT)
                nc.vector.reduce_max(mx[:, p % 2, n, k:k + 1], bank[:, 2 + i % 2, :], AX).then_inc(s["emax_done"], 1)

            def shift_parts(b, p):
                G = PAIRS * b + p
                dve.wait_ge(s["emax_done"], 8 * G + 8)
                if not (isinstance(b, int) and G == 0):
                    dve.wait_ge(s["sh_ready"], 2 * G)
                nc.vector.tensor_scalar(shift[:, :, :, 0], mx[:, p % 2], -1.0, None, ALU.mult).then_inc(s["sh_hi"], 1)
                dve.wait_ge(s["sh_hi"], G + 1)
                nc.vector.scalar_tensor_tensor(shift[:, :, :, 1], mx[:, p % 2], -1.0, shift[:, :, :, 0].bitcast(F32),
                                               ALU.mult, ALU.subtract).then_inc(s["sh_lo"], 1)

            def quotients(b, c):
                g = 4 * b + c
                dve.wait_ge(s["den_done"], 2 * g + 2)
                nc.vector.reciprocal(rden[:, :], den[:, :]).then_inc(s["rden_done"], 1)
                dve.wait_ge(s["oraw_done"], 2 * g + 2)
                dve.wait_ge(s["rden_done"], g + 1)
                if not (isinstance(b, int) and g == 0):
                    dve.wait_ge(s["ol_done"], g)
                nc.vector.scalar_tensor_tensor(o[:, :], oraw[:, :], float(D) ** -0.5, rden[:, :],
                                               ALU.mult, ALU.mult).then_inc(s["o_done"], 1)

            def output_lo(b, c):
                dve.wait_ge(s["oh_done"], 4 * b + c + 1)
                nc.vector.scalar_tensor_tensor(ol[:, c, :], o[:, :], bvs[:, c:c + 1], oh[:, c, :].bitcast(F32),
                                               ALU.add, ALU.subtract).then_inc(s["ol_done"], 1)

            def residual(b, i):
                dve.wait_ge(s["hb_done"], b + 1)
                for i in (i, i + 1):
                    dve.wait_ge(s["pj_ready"], 4 * b + i + 1)
                    nc.vector.tensor_tensor(h[:, i, :], bank[:, 6 + i % 2, :], h[:, i, :], ALU.add).then_inc(s["h1_done"], 1)

            def statistics(b):
                dve.wait_ge(s["set_up"], 1)
                for i in range(NT):
                    dve.wait_ge(s["h1_done"], 4 * b + i + 1)
                    if i:
                        dve.wait_ge(s["st_done"], 4 * b + i)
                    nc.vector.bn_stats(st[:, i, :], h[:, i, :]).then_inc(s["st_done"], 1)
                    if i:
                        nc.vector.bn_aggr(mv[:, i - 1, :], st[:, i - 1, :]).then_inc(s["mv_done"], 1)
                dve.wait_ge(s["st_done"], 4 * b + NT)
                dve.wait_ge(s["mv_done"], 4 * b + NT - 1)
                nc.vector.tensor_scalar(ve[:, 0:NT - 1], mv[:, 0:NT - 1, 1], EPS, None, ALU.add).then_inc(s["ve_done"], 1)
                nc.vector.bn_aggr(mv[:, NT - 1, :], st[:, NT - 1, :]).then_inc(s["mv_done"], 1)
                dve.wait_ge(s["mv_done"], 4 * b + NT)
                nc.vector.tensor_scalar(ve[:, NT - 1:NT], mv[:, NT - 1:NT, 1], EPS, None, ALU.add).then_inc(s["ve_done"], 1)

            def mean_term(b):
                dve.wait_ge(s["rstd_done"], b + 1)
                nc.vector.scalar_tensor_tensor(nmr[:, :], mv[:, :, 0], -1.0, rstd[:, :],
                                               ALU.mult, ALU.mult).then_inc(s["nmr_done"], 1)

            def batch(b, bpar, more):
                for p in range(PAIRS):
                    nxt = next_pair(b, p, more)
                    if nxt:
                        for i in range(8):
                            maximum(*nxt, i)
                        shift_parts(*nxt)
                    if p % 2 == 0 and p:
                        quotients(b, p // 2 - 1)
                    elif p == 0 and not first(b):
                        quotients(b - 1, FC - 1)
                    if p % 2 and p > 1:
                        output_lo(b, p // 2 - 1)
                    elif p == 1 and not first(b):
                        output_lo(b - 1, FC - 1)
                    if p % 2 and (p < 4 or more):
                        lo_parts(*ahead(b, p // 2, 2))
                    if not first(b):
                        if p in (1, 2):
                            residual(b - 1, 2 * p - 2)
                        if p == 3:
                            statistics(b - 1)
                        if p == 4:
                            mean_term(b - 1)

            dve.wait_ge(s["ld_c"], 32)
            nc.vector.tensor_scalar(bvs[:, :], bcol3[:, 2, :], float(D) ** -0.5, None, ALU.mult).then_inc(s["bv_done"], 1)
            dve.wait_ge(s["bv_done"], 1)
            lo_parts(0, 0)
            lo_parts(0, 1)
            for i in range(8):
                maximum(0, 0, i)
            shift_parts(0, 0)
            batches(dve, batch)
            quotients(B - 1, FC - 1)
            output_lo(B - 1, FC - 1)
            residual(B - 1, 0)
            residual(B - 1, 2)
            statistics(B - 1)
            mean_term(B - 1)

        @block.tensor
        def _(pe):
            def project(b, c):
                g = 4 * b + c
                if isinstance(b, int) and b == 0 and c < 2:
                    pe.wait_ge(s["hl_done"], FC)
                    if c == 1:
                        pe.wait_ge(s["ql_done"], 1)
                        pe.wait_ge(s["kl_done"], 1)
                elif c < 2:
                    pe.wait_ge(s["hl_done"], 4 * b + 4)
                    pe.wait_ge(s["v_done"], 4 * b + 2 * c + 2)
                elif c == 3 and not first(b):
                    pe.wait_ge(s["h1_done"], 4 * b)
                else:
                    pe.wait_ge(s["ql_done"], g)
                    pe.wait_ge(s["kl_done"], g)
                for which in range(2):
                    col = slice(which * D + c * P, which * D + (c + 1) * P)
                    for f in range(FC):
                        last = mm3(nc, bank[:, 6 + which, :], t["wqkh"][:, f, col], t["wqkl"][:, f, col],
                                   hh[:, f, :], hl[:, f, :], f == 0, f == FC - 1)
                    last.then_inc((s["q_ready"], s["k_ready"])[which], 1)

            def values(b, i, chunks):
                pe.wait_ge(s["ql_done"], chunks)
                pe.wait_ge(s["kl_done"], chunks)
                pe.wait_ge(s["hl_done"], 4 * b + 4)
                if isinstance(b, int) and b == 0 and i == 2:
                    pe.wait_ge(s["v_done"], 2)
                for i in (i, i + 1):
                    r = slice(i * P, (i + 1) * P)
                    for f in range(FC):
                        last = mm3(nc, bank[:, 6 + i % 2, :], hh[:, f, r], hl[:, f, r],
                                   t["wvh"][:, f, :], t["wvl"][:, f, :], f == 0, f == FC - 1)
                    last.then_inc(s["v_ready"], 1)

            def scores(b, p, i):
                G = PAIRS * b + p
                c = p // 2
                if i == 0:
                    pe.wait_ge(stk[c % 2][p % 2], STK * (use(b, c) + 1))
                    if not (isinstance(b, int) and G == 0):
                        pe.wait_ge(s["shrow_done"], 2 * G)
                if i < 2:
                    pe.wait_ge(s["emax_done"], 8 * G)
                else:
                    pe.wait_ge(s["emax_done"], 8 * G + i - 1)
                k, n = divmod(i, NT)
                j = 2 * (p % 2) + k
                nc.tensor.matmul(bank[:, 2 + i % 2, :], sq[0:3 * DH, c % 2, j, n * P:(n + 1) * P],
                                 sk[0:3 * DH, c % 2, j, :], start=True, stop=True).then_inc(s["e_ready"], 1)

            def shift_t(b, p):
                pe.wait_ge(s["sh_lo"], PAIRS * b + p + 1)
                for k in range(2):
                    for n in range(NT):
                        last = nc.tensor.matmul(bank[3 * DH:3 * DH + 2, 2 + k, n * P:(n + 1) * P],
                                                shift[:, n, k, :].bitcast(F32), t["ident"][:, :],
                                                start=True, stop=True)
                    last.then_inc(s["sh_ready"], 1)

            def scores_t(b, p, i):
                G = PAIRS * b + p
                c = p // 2
                for k in range(2):
                    if i == 0:
                        pe.wait_ge(s["shrow_done"], 2 * G + k + 1)
                        pe.wait_ge(s["exp_done"], 8 * G)
                    else:
                        pe.wait_ge(s["exp_done"], 8 * G + 2 * i + k - 1)
                    j = 2 * (p % 2) + k
                    nc.tensor.matmul(bank[:, k, :], sk[0:3 * DH + 2, c % 2, j, i * P:(i + 1) * P],
                                     sq[0:3 * DH + 2, c % 2, j, :], start=True, stop=True).then_inc(s["et_ready"], 1)

            def weighted(b, bpar, p, i):
                G = PAIRS * b + p
                if i == 0:
                    if not (isinstance(b, int) and G < 2):
                        pe.wait_ge(s["oraw_done"], G - 1)
                    pe.wait_ge(s["v_done"], 4 * b + 4)
                pe.wait_ge(s["exp_done"], 8 * G + 2 * i + 2)
                for k in range(2):
                    w = pt[:, i, k, :]
                    a, r = 64 * (p % 2) + DH * k, 64 - 64 * (p % 2) + DH * k
                    nc.tensor.matmul(bank[a:a + DH, 4 + p % 2, :], v[:, bpar, i, (2 * p + k) * DH:(2 * p + k + 1) * DH],
                                     w, start=i == 0, stop=i == NT - 1)
                    last = nc.tensor.matmul(bank[r:r + DH, 4 + p % 2, :], ones32[:, :], w,
                                            start=i == 0, stop=i == NT - 1)
                last.then_inc(s["pv_done"], 1)

            def output_projection(b, i, chunks):
                if i == 0:
                    pe.wait_ge(s["ol_done"], 4 * b + 4)
                    pe.wait_ge(s["ql_done"], chunks)
                    pe.wait_ge(s["kl_done"], chunks)
                for i in (i, i + 1):
                    if i >= 2:
                        pe.wait_ge(s["h1_done"], 4 * b + i - 1)
                    r = slice(i * P, (i + 1) * P)
                    for c in range(FC):
                        last = mm3(nc, bank[:, 6 + i % 2, :], oh[:, c, r], ol[:, c, r],
                                   t["wph"][:, c, :], t["wpl"][:, c, :], c == 0, c == FC - 1)
                    last.then_inc(s["pj_ready"], 1)

            E_AT = (3, 3, 2, 0)

            def batch(b, bpar, more):
                for p in range(PAIRS):
                    nxt = next_pair(b, p, more)
                    scores_t(b, p, 0)
                    e = 0
                    for i in range(NT):
                        if nxt:
                            for _ in range(E_AT[i]):
                                scores(*nxt, e)
                                e += 1
                        if i < NT - 1:
                            scores_t(b, p, i + 1)
                        else:
                            if p % 2 and (p < 4 or more):
                                project(*ahead(b, p // 2, 2))
                            if p in (1, 2) and not first(b):
                                output_projection(b - 1, 2 * p - 2, 4 * b + 3)
                            if p in (4, 6) and more:
                                values(b + 1, p - 4, 4 * b + p // 2 + 2)
                            if nxt:
                                shift_t(*nxt)
                        weighted(b, bpar, p, i)

            pe.wait_ge(s["set_up"], 4)
            project(0, 0)
            project(0, 1)
            values(0, 0, 2)
            values(0, 2, 2)
            for i in range(8):
                scores(0, 0, i)
            shift_t(0, 0)
            batches(pe, batch)
            output_projection(B - 1, 0, 4 * B)
            output_projection(B - 1, 2, 4 * B)


def program(nc, d):
    d["gb_rows"] = nc.dram_tensor("gb_rows", [B, 2, D], F32, kind="Internal").ap()
    d["v_rows"] = nc.dram_tensor("v_rows", [2, 2, B * MP, D], F32, kind="Internal").ap()
    d["m_rows"] = nc.dram_tensor("m_rows", [B, P, FC, 2, HK], F32, kind="Internal").ap()
    d["h_rows"] = nc.dram_tensor("h_rows", [B, P, NT, D], F32, kind="Internal").ap()
    d["t_rows"] = nc.dram_tensor("t_rows", [B, P, FC, N], F32, kind="Internal").ap()
    t = {}
    with ExitStack() as outer:
        t["ident"] = outer.enter_context(nc.sbuf_tensor("ident", [P, P], F32))
        with ExitStack() as ctx:
            def sb(name, shape, dt=F32):
                return ctx.enter_context(nc.sbuf_tensor(name, shape, dt))

            t["w1h"], t["w1l"] = sb("w1h", [P, FC, D], F32R), sb("w1l", [P, FC, D], F32R)
            t["sq"] = sb("sq", [64, D], F32R)
            t["hot"] = sb("hot", [64, B])
            t["bself"], t["boutc"] = sb("bself", [P, FC]), sb("boutc", [P, FC])
            t["wbias"], t["bbias"] = sb("wbias", [P, L]), sb("bbias", [P, 1])
            t["bias_rows"] = sb("bias_rows", [64, B, 2, HK], F32R)
            prologue(nc, t, d)
            graph(nc, t, d)
        with ExitStack() as ctx:
            def wt(name, width):
                return ctx.enter_context(nc.sbuf_tensor(name, [P, FC, width], F32R))

            t["wqkh"], t["wqkl"] = wt("wqkh", 2 * D), wt("wqkl", 2 * D)
            t["wvh"], t["wvl"], t["wph"], t["wpl"] = wt("wvh", D), wt("wvl", D), wt("wph", D), wt("wpl", D)
            split_weights(nc, t, d)
            attention(nc, t, d)


def kernel(**inputs):
    import numpy as np
    import concourse.bacc as bacc
    from concourse import mybir as mb
    from concourse.bass_utils import run_bass_kernel_spmd

    a = {k: np.asarray(v) for k, v in inputs.items()}

    def g(k):
        return a["L0_cond_" + k]

    def f(k):
        return a["L1_cond_" + k]

    adj = a["mask_BxSxSx11_ik0"]
    x = a["x"]
    bqkv = f("bqkv").reshape(D, 3).T

    def columns(v):
        v = v.reshape(v.shape[:-1] + (FC, P))
        return np.moveaxis(v, -1, 0)

    def twice(v):
        out = np.zeros(v.shape[:-1] + (64,), v.dtype)
        out[..., 0:v.shape[-1]] = v
        out[..., 32:32 + v.shape[-1]] = v
        return out

    adj2 = np.stack([adj[:, :, :NK, :], adj[:, :NK, :, :].transpose(0, 2, 1, 3)], axis=2)
    hot = np.zeros((64, B), np.float32)
    for b in range(B):
        hot[b, b] = hot[32 + b, b] = 1.0
    hot20 = np.repeat(hot[:, :, None], MP, axis=2).reshape(64, B * MP)
    wqkv = f("Wqkv").reshape(D, 3, D)
    arrays = {
        "x": x,
        "x_t": x.transpose(0, 2, 1).reshape(B, FC, P, N).transpose(0, 2, 1, 3),
        "adj": adj2.reshape(B, NT, P, 2 * NK, L).transpose(0, 2, 1, 3, 4).reshape(B, P, NT * 2 * NK, L),
        "cond64": twice(a["cond_1024"].T.reshape(FC, P, B).transpose(1, 0, 2)),
        "wself_t": g("W_self").T,
        "b_self": columns(g("b_self")),
        "w_bias": g("w_bias"),
        "b_bias": g("b_bias").reshape(1),
        "wq": g("Wq"),
        "bq64": twice(columns(g("bq"))[..., None]),
        "wk_t": g("Wk").transpose(0, 2, 1),
        "bk": columns(g("bk")),
        "wout_t": g("Wout").reshape(2, D, D).transpose(0, 2, 1),
        "bout": columns(g("bout")),
        "ln_g": f("ln_g"), "ln_b": f("ln_b"), "bg": f("bg"), "bb": f("bb"),
        "wg_t": f("Wg").T, "wb_t": f("Wb").T,
        "wqkv_t": wqkv.transpose(2, 1, 0),
        "bqkc": columns(bqkv),
        "wp_t": f("Wp").T,
        "bp": f("bp"),
        "ident": np.eye(P, dtype=np.float32),
        "hot": hot,
        "hot20": hot20,
    }
    nc = bacc.Bacc("TRN2", target_bir_lowering=False, num_devices=1)
    feed, drams = {}, {}
    for name, v in arrays.items():
        v = np.ascontiguousarray(v)
        feed["in_" + name] = v
        drams[name] = nc.dram_tensor("in_" + name, v.shape, mb.dt.from_np(v.dtype), kind="ExternalInput").ap()
    d = dict(drams)
    d["out"] = nc.dram_tensor("out_y", (B, N, D), mb.dt.float32, kind="ExternalOutput").ap()
    program(nc, d)
    r = run_bass_kernel_spmd(nc, [feed], core_ids=[0])
    return r.results[0]["out_y"]
```

```python
from contextlib import ExitStack

import concourse.bass as bass
from concourse import mybir

F32 = mybir.dt.float32
F32R = mybir.dt.float32r
I32 = mybir.dt.int32
ALU = mybir.AluOpType
ACT = mybir.ActivationFunctionType
AX = mybir.AxisListType.X

P = 128
B, N, D = 8, 512, 512
H = 16
DH = D // H
L = 11
NK = 20
MP = 32
FC = D // P
NT = N // P
HC = P // DH
HK = H * NK
CK = HC * NK
NEG = -9000000000000000.0
EPS = 1e-5
ds = bass.ds


def sems(nc, ctx, names):
    return {n: ctx.enter_context(nc.semaphore(n)) for n in names.split()}


def mm3(nc, out, ah, al, bh, bl, start, stop):
    nc.tensor.matmul(out, ah, bh, start=start, stop=False)
    nc.tensor.matmul(out, ah, bl, start=False, stop=False)
    return nc.tensor.matmul(out, al, bh, start=False, stop=stop)


def prologue(nc, t, d):
    with ExitStack() as ctx:
        def sb(name, shape, dt=F32):
            return ctx.enter_context(nc.sbuf_tensor(name, shape, dt))

        cond64 = sb("cond64", [P, FC, 64])
        wself_raw = sb("wself_raw", [P, 2 * FC, D])
        wg = sb("wg", [P, FC, D])
        wb = sb("wb", [P, FC, D])
        x20 = sb("x20", [P, FC, B * MP])
        bg8, bb8, lng8, lnb8 = (sb(n, [B, D]) for n in ("bg8", "bb8", "lng8", "lnb8"))
        gam8, gs8, bt8, bs8 = (sb(n, [B, D]) for n in ("gam8", "gs8", "bt8", "bs8"))
        wk = sb("wk", [P, 2, FC, D])
        wq = sb("wq", [P, 2, FC, D])
        wout = sb("wout", [P, 2, FC, D])
        bk = sb("bk", [P, 2, FC])
        bout2 = sb("bout2", [P, 2, FC])
        bq64 = sb("bq64", [P, 2, FC, 64])
        hot20 = sb("hot20", [64, B * MP])
        ones64 = sb("ones64", [P, 64])
        z20 = sb("z20", [64, B * MP], F32R)
        sf20 = sb("sf20", [P, FC, B * MP])
        kdiag = sb("kdiag", [P, FC, B, CK])
        mout = sb("mout", [P, 2, B, HK])
        vparts = sb("vparts", [P, 2, 2, D], F32R)
        bank = ctx.enter_context(nc.psum_tensor("p_bank", [P, 8, 512], F32))

        s = sems(nc, ctx, "ld_small ld_const bout_done ld_wself ld_x20 ld_gb ld_wk ld_wq ld_wout ld_hot zeroed cond_in bq_in "
                          "sq_ready sq_hi sq_split rs_ready z_ready gb_ready gb_step sf_ready sf_done "
                          "kh_ready kdiag_done v_ready v_hi v_done m_ready m_done_dve m_done_act "
                          "bias_ready bias_hi bias_done w1_hi w1_split st_gb st_v st_m0 st_m1")
        block = ctx.enter_context(nc.Block())

        @block.sync
        def _(sp):
            sp.wait_ge(s["zeroed"], 1)
            sp.dma_start(cond64[:, :, :], d["cond64"]).then_inc(s["cond_in"], 16)
            sp.dma_start(wself_raw[:, :, :], d["wself_t"].rearrange("(c p) o -> p c o", p=P)).then_inc(s["ld_wself"], 16)
            for c in range(FC):
                sp.dma_start(x20[:, c, :].rearrange("p (b m) -> p b m", b=B)[:, :, 0:NK],
                             d["x_t"][:, :, c, 0:NK].rearrange("b p m -> p b m")).then_inc(s["ld_x20"], 16)
            sp.dma_start(hot20[:, :], d["hot20"]).then_inc(s["ld_hot"], 16)
            sp.dma_start(wk[:, :, :, :], d["wk_t"].rearrange("e (c p) o -> p e c o", p=P)).then_inc(s["ld_wk"], 16)
            sp.dma_start(wout[:, :, :, :], d["wout_t"].rearrange("e (c p) o -> p e c o", p=P)).then_inc(s["ld_wout"], 16)
            sp.dma_start(wq[:, :, :, :], d["wq"].rearrange("e (c p) o -> p e c o", p=P)).then_inc(s["ld_wq"], 16)
            sp.dma_start(wg[:, :, :], d["wg_t"].rearrange("(c p) o -> p c o", p=P)).then_inc(s["ld_gb"], 16)
            sp.dma_start(wb[:, :, :], d["wb_t"].rearrange("(c p) o -> p c o", p=P)).then_inc(s["ld_gb"], 16)
            sp.dma_start(t["xraw"][:, :, :], d["x_t"][0]).then_inc(t["x_t_in"], 16)
            for e in range(2):
                for g in range(2):
                    sp.wait_ge(s["v_done"], 2 * e + g + 1)
                    for part in range(2):
                        sp.dma_start(d["v_rows"][part, e, g * P:(g + 1) * P, :],
                                     vparts[:, g, part, :].bitcast(F32)).then_inc(s["st_v"], 16)
                for f in range(FC):
                    i = FC * e + f
                    sp.wait_ge(s["m_done_dve"], FC * (i + 1))
                    sp.wait_ge(s["m_done_act"], FC * (i + 1))
                    sp.dma_start(d["m_rows"][:, :, f, e, :].rearrange("b p k -> p b k"),
                                 mout[:, i % 2, :, :]).then_inc((s["st_m0"], s["st_m1"])[i % 2], 16)
            sp.wait_ge(s["gb_step"], 6)
            sp.dma_start(d["gb_rows"][:, 0, :], gs8[:, :]).then_inc(s["st_gb"], 16)
            sp.dma_start(d["gb_rows"][:, 1, :], bs8[:, :]).then_inc(s["st_gb"], 16)
            sp.wait_ge(s["st_gb"], 32)
            sp.wait_ge(s["st_v"], 16 * 8)
            sp.wait_ge(s["st_m0"], 16 * FC)
            sp.wait_ge(s["st_m1"], 16 * FC)

        @block.gpsimd
        def _(pool):
            nc.gpsimd.memset(x20[:, :, :], 0.0).then_inc(s["zeroed"], 1)
            nc.gpsimd.memset(ones64[:, :], 1.0).then_inc(s["zeroed"], 1)
            nc.gpsimd.memset(kdiag[:, :, :, :], 0.0).then_inc(s["zeroed"], 1)
            pool.wait_ge(s["w1_hi"], 1)
            nc.gpsimd.tensor_tensor(t["w1l"][:, :, :], wself_raw[:, 0:FC, :], t["w1h"][:, :, :].bitcast(F32),
                                    ALU.subtract).then_inc(s["w1_split"], 1)

        @block.scalar
        def _(act):
            act.dma_start(bq64[:, :, :, :], d["bq64"]).then_inc(s["bq_in"], 16)
            act.dma_start(t["bself"][:, :], d["b_self"]).then_inc(s["ld_const"], 16)
            act.dma_start(bout2[:, :, :], d["bout"]).then_inc(s["ld_const"], 16)
            act.dma_start(t["ident"][:, :], d["ident"]).then_inc(s["ld_const"], 16)
            act.dma_start(t["hot"][:, :], d["hot"]).then_inc(s["ld_const"], 16)
            act.dma_start(t["wbias"][:, :], d["w_bias"].partition_broadcast(P)).then_inc(s["ld_const"], 16)
            act.dma_start(t["bbias"][:, :], d["b_bias"].partition_broadcast(P)).then_inc(s["ld_const"], 16)
            act.dma_start(bk[:, :, :], d["bk"]).then_inc(s["ld_small"], 16)
            for row, src in ((bg8, d["bg"]), (bb8, d["bb"]), (lng8, d["ln_g"]), (lnb8, d["ln_b"])):
                act.dma_start(row[:, :], src.partition_broadcast(B)).then_inc(s["ld_small"], 16)
            act.wait_ge(s["ld_const"], 16 * 6)
            for o in range(FC):
                act.wait_ge(s["sf_ready"], o + 1)
                nc.scalar.activation(sf20[:, o, :], bank[:, 4 + o, 0:B * MP], ACT.Identity,
                                     bias=t["bself"][:, o:o + 1]).then_inc(s["sf_done"], 1)
            for i in range(2 * FC):
                if i >= 2:
                    act.wait_ge((s["st_m0"], s["st_m1"])[i % 2], 16 * (i // 2))
                for h in range(FC):
                    act.wait_ge(s["m_ready"], 2 * (FC * i + h) + 2)
                    nc.scalar.activation(mout[:, i % 2, 4:8, h * CK:(h + 1) * CK],
                                         bank[:, 2 * (h % 2) + 1, 0:4 * CK].rearrange("p (b k) -> p b k", b=4),
                                         ACT.Copy).then_inc(s["m_done_act"], 1)
                if i % FC == FC - 1:
                    for n in range(2 * (i - FC + 1), 2 * (i + 1)):
                        act.wait_ge(s["bias_ready"], n + 1)
                        e, h, half = n // (2 * FC), n % (2 * FC) // 2, n % 2
                        nc.scalar.activation(t["bias_rows"][:, 4 * half:4 * half + 4, e, h * CK:(h + 1) * CK],
                                             bank[0:64, 4 + n % 4, 0:4 * CK].rearrange("p (b k) -> p b k", b=4),
                                             ACT.Copy).then_inc(s["bias_hi"], 1)

        @block.vector
        def _(dve):
            def gamma_beta():
                dve.wait_ge(s["gb_ready"], 2)
                nc.vector.tensor_tensor(gam8[:, :], bank[0:B, 2, :], bg8[:, :], ALU.add).then_inc(s["gb_step"], 1)
                nc.vector.tensor_tensor(bt8[:, :], bank[0:B, 3, :], bb8[:, :], ALU.add).then_inc(s["gb_step"], 1)
                dve.wait_ge(s["gb_step"], 2)
                nc.vector.tensor_tensor(gs8[:, :], gam8[:, :], lng8[:, :], ALU.mult).then_inc(s["gb_step"], 1)
                dve.wait_ge(s["gb_step"], 3)
                nc.vector.tensor_tensor(gam8[:, :], gam8[:, :], lnb8[:, :], ALU.mult).then_inc(s["gb_step"], 1)
                dve.wait_ge(s["gb_step"], 4)
                nc.vector.tensor_tensor(bs8[:, :], gam8[:, :], bt8[:, :], ALU.add).then_inc(s["gb_step"], 2)

            dve.wait_ge(s["sq_ready"], 1)
            nc.vector.tensor_copy(t["sq"][:, :], bank[0:64, 0, :]).then_inc(s["sq_hi"], 1)
            dve.wait_ge(s["sq_hi"], 1)
            nc.vector.tensor_tensor(t["sq"][32:64, :], bank[32:64, 0, :], t["sq"][32:64, :].bitcast(F32),
                                    ALU.subtract).then_inc(s["sq_split"], 1)
            dve.wait_ge(s["rs_ready"], 1)
            dve.wait_ge(s["ld_hot"], 16)
            nc.vector.scalar_tensor_tensor(z20[:, :], bank[0:64, 1, 0:B * MP], 0.0, hot20[:, :],
                                           ALU.not_equal, ALU.mult).then_inc(s["z_ready"], 1)
            dve.wait_ge(s["ld_wself"], 16)
            nc.vector.tensor_copy(t["w1h"][:, :, :], wself_raw[:, 0:FC, :]).then_inc(s["w1_hi"], 1)
            dve.wait_ge(s["ld_const"], 16 * 6)
            nc.vector.tensor_tensor(t["boutc"][:, :], bout2[:, 0, :], bout2[:, 1, :], ALU.add).then_inc(s["bout_done"], 1)
            dve.wait_ge(s["ld_small"], 16 * 5)
            for e in range(2):
                if e == 1:
                    dve.wait_ge(s["bias_ready"], 2 * FC)
                for h in range(FC):
                    dve.wait_ge(s["kh_ready"], FC * e + h + 1)
                    dve.wait_ge(s["zeroed"], 3)
                    src = bank[:, h % 2 + 4, 0:B * MP].rearrange("p (b m) -> p b m", b=B)
                    for j in range(HC):
                        r = slice(DH * j, DH * j + DH)
                        nc.vector.tensor_scalar(kdiag[r, h, :, NK * j:NK * j + NK], src[r, :, 0:NK],
                                                bk[r, e, h:h + 1], float(DH) ** -0.5,
                                                ALU.add, ALU.mult).then_inc(s["kdiag_done"], 1)
                for g in range(2):
                    n = 2 * e + g
                    dve.wait_ge(s["v_ready"], n + 1)
                    if e == 1:
                        dve.wait_ge(s["st_v"], 16 * 2 * 2)
                    nc.vector.tensor_copy(vparts[:, g, 0, :], bank[:, 6 + g, :]).then_inc(s["v_hi"], 1)
                    dve.wait_ge(s["v_hi"], n + 1)
                    nc.vector.tensor_tensor(vparts[:, g, 1, :], bank[:, 6 + g, :],
                                            vparts[:, g, 0, :].bitcast(F32), ALU.subtract).then_inc(s["v_done"], 1)
                for f in range(FC):
                    i = FC * e + f
                    if i >= 2:
                        dve.wait_ge((s["st_m0"], s["st_m1"])[i % 2], 16 * (i // 2))
                    for h in range(FC):
                        dve.wait_ge(s["m_ready"], 2 * (FC * i + h) + 1)
                        nc.vector.tensor_copy(mout[:, i % 2, 0:4, h * CK:(h + 1) * CK],
                                              bank[:, 2 * (h % 2), 0:4 * CK].rearrange("p (b k) -> p b k", b=4)
                                              ).then_inc(s["m_done_dve"], 1)
                if e == 1:
                    gamma_beta()
                for h in range(FC):
                    for half in range(2):
                        n = 2 * (FC * e + h) + half
                        src = bank[:, 4 + n % 4, 0:4 * CK].rearrange("p (b k) -> p b k", b=4)
                        dst = t["bias_rows"][:, 4 * half:4 * half + 4, e, h * CK:(h + 1) * CK]
                        dve.wait_ge(s["bias_hi"], n + 1)
                        nc.vector.tensor_tensor(dst[32:64], src[32:64], dst[32:64].bitcast(F32),
                                                ALU.subtract).then_inc(s["bias_done"], 1)

        @block.tensor
        def _(pe):
            def gamma_beta():
                pe.wait_ge(s["m_done_dve"], 2 * FC * FC)
                pe.wait_ge(s["m_done_act"], 2 * FC * FC)
                pe.wait_ge(s["ld_gb"], 32)
                for k, w in enumerate((wg, wb)):
                    for f in range(FC):
                        last = nc.tensor.matmul(bank[0:B, 2 + k, :], cond64[:, f, 0:B], w[:, f, :],
                                                start=f == 0, stop=f == FC - 1)
                    last.then_inc(s["gb_ready"], 1)

            pe.wait_ge(s["cond_in"], 16)
            pe.wait_ge(s["ld_wself"], 16)
            for f in range(FC):
                last = nc.tensor.matmul(bank[0:64, 0, :], cond64[:, f, :], wself_raw[:, FC + f, :],
                                        start=f == 0, stop=f == FC - 1)
            last.then_inc(s["sq_ready"], 1)
            pe.wait_ge(s["ld_x20"], 16 * FC)
            pe.wait_ge(s["zeroed"], 2)
            for f in range(FC):
                last = nc.tensor.matmul(bank[0:64, 1, 0:B * MP], ones64[:, :], x20[:, f, :],
                                        start=f == 0, stop=f == FC - 1)
            last.then_inc(s["rs_ready"], 1)
            pe.wait_ge(s["z_ready"], 1)
            pe.wait_ge(s["sq_split"], 1)
            for o in range(FC):
                out = bank[:, 4 + o, 0:B * MP]
                nc.tensor.matmul(out, t["sq"][:, o * P:(o + 1) * P], z20[:, :], start=True, stop=False)
                for f in range(FC):
                    last = nc.tensor.matmul(out, wself_raw[:, f, o * P:(o + 1) * P], x20[:, f, :],
                                            start=False, stop=f == FC - 1)
                last.then_inc(s["sf_ready"], 1)
            pe.wait_ge(s["ld_wk"], 16)
            pe.wait_ge(s["sf_done"], FC)
            for e in range(2):
                if e == 1:
                    pe.wait_ge(s["bias_done"], 2 * FC)
                for h in range(FC):
                    if h >= 2:
                        pe.wait_ge(s["kdiag_done"], HC * (FC * e + h - 1))
                    for f in range(FC):
                        last = nc.tensor.matmul(bank[:, 4 + h % 2, 0:B * MP], wk[:, e, f, h * P:(h + 1) * P],
                                                sf20[:, f, :], start=f == 0, stop=f == FC - 1)
                    last.then_inc(s["kh_ready"], 1)
                pe.wait_ge(s["ld_wout"], 16)
                for g in range(2):
                    if e == 1:
                        pe.wait_ge(s["v_done"], g + 1)
                    for f in range(FC):
                        last = nc.tensor.matmul(bank[:, 6 + g, :], sf20[:, f, g * P:(g + 1) * P], wout[:, e, f, :],
                                                start=f == 0, stop=f == FC - 1)
                    last.then_inc(s["v_ready"], 1)
                pe.wait_ge(s["kdiag_done"], HC * FC * (e + 1))
                pe.wait_ge(s["ld_wq"], 16)
                pe.wait_ge(s["bq_in"], 16)
                for f in range(FC):
                    for h in range(FC):
                        k = FC * (FC * e + f) + h
                        if k == 0:
                            pe.wait_ge(s["z_ready"], 1)
                        if k >= 2:
                            pe.wait_ge(s["m_done_dve"], k - 1)
                            pe.wait_ge(s["m_done_act"], k - 1)
                        for half in range(2):
                            nc.tensor.matmul(bank[:, 2 * (h % 2) + half, 0:4 * CK], wq[:, e, h, f * P:(f + 1) * P],
                                             kdiag[:, h, 4 * half:4 * half + 4, :], start=True, stop=True
                                             ).then_inc(s["m_ready"], 1)
                if e == 1:
                    gamma_beta()
                for h in range(FC):
                    for half in range(2):
                        n = 2 * (FC * e + h) + half
                        if n % 8 == 2:
                            pe.wait_ge(s["v_done"], 2 * e + 2)
                        if n % 8 >= 4:
                            pe.wait_ge(s["bias_done"], n - 3)
                        last = nc.tensor.matmul(bank[0:64, 4 + n % 4, 0:4 * CK], bq64[:, e, h, :],
                                                kdiag[:, h, 4 * half:4 * half + 4, :], start=True, stop=True)
                        last.then_inc(s["bias_ready"], 1)


def graph(nc, t, d):
    with ExitStack() as ctx:
        def sb(name, shape, dt=F32):
            return ctx.enter_context(nc.sbuf_tensor(name, shape, dt))

        xraw = t["xraw"]
        xh, xl = sb("xh", [P, FC, N], F32R), sb("xl", [P, FC, N], F32R)
        xn = sb("xn", [P, NT, D])
        adj = sb("adj", [P, NT * 2 * NK, L], I32)
        adjw = sb("adjw", [P, NT * 2 * NK, L])
        cnt, vb, mask, blocked, cadd = (sb(n, [P, NT, 2, NK]) for n in ("cnt", "vb", "mask", "blocked", "cadd"))
        m = sb("m", [P, FC, 2, HK])
        vdiag = sb("vdiag", [CK, 2, 2, FC, P], F32R)
        z = sb("z", [64, N], F32R)
        sf2 = sb("sf", [P, 2, FC, N])
        ot = sb("ot", [P, FC, N])
        e = sb("e", [P, NT, 2, H, NK])
        mx, sm, rc = (sb(n, [P, NT, 2 * H]) for n in ("mx", "sm", "rc"))
        wth, wtl = sb("wth", [CK, 2, N], F32R), sb("wtl", [CK, 2, N], F32R)
        st = sb("st", [P, NT, 6])
        mv = sb("mv", [P, NT, 2])
        ve, rstd, nmr, mhalf = (sb(n, [P, NT]) for n in ("ve", "rstd", "nmr", "mhalf"))
        ln = sb("ln", [P, NT, D])
        hout = sb("hout", [P, FC, N])
        gcol, bcol = sb("gcol", [P, FC, B]), sb("bcol", [P, FC, B])
        onesr = sb("onesr", [64, P], F32R)
        ones64 = sb("g_ones64", [P, 64], F32R)
        bank = ctx.enter_context(nc.psum_tensor("g_bank", [P, 8, 512], F32))

        SFB = (0, 6, 7, 1)

        s = sems(nc, ctx, "x_in adj_in m_in v_in gb_in set_up xh_done xl_done rs_ready z_done adjf_done adjw_done nmr_done sf_ready "
                          "sf_done adj_step sc_ready mult_done add_done mx_done sub_done exp_done sum_done "
                          "rc_done w_done wtr_ready wh_done wl_done att_mm att_done back_ready h_done "
                          "st_done mv_done ve_done rstd_done ln_done lnt_ready lnt_done h_stored t_stored")
        block = ctx.enter_context(nc.Block())

        def steps(eng, step):
            step(1, 1, False)
            step(2, 0, False)
            with eng.Fori(1, B // 2 - 1) as k:
                step(2 * k + 1, 1, False)
                step(2 * k + 2, 0, False)
            step(B - 1, 1, True)

        def heads(x):
            return x.unsqueeze(2).broadcast_to([P, 2, H, NK])

        def keys(x):
            return x.unsqueeze(2).broadcast_to([P, 2 * H, NK])

        @block.sync
        def _(sp):

            def load_first(b):
                sp.dma_start(xraw[:, :, :], d["x_t"][ds(b, 1)].rearrange("o p c n -> (o p) c n")).then_inc(t["x_t_in"], 16)

            def load_adj(b):
                sp.dma_start(adj[:, :, :], d["adj"][ds(b, 1)].rearrange("o p k l -> (o p) k l")).then_inc(s["adj_in"], 16)

            def load_m(b):
                sp.dma_start(m[:, :, :, :], d["m_rows"][ds(b, 1)].rearrange("o p c e k -> (o p) c e k")).then_inc(s["m_in"], 16)

            def load_v(b):
                for part in range(2):
                    for dr in range(2):
                        for j in range(HC):
                            sp.dma_start(
                                vdiag[NK * j:NK * j + NK, part, dr, :, DH * j:DH * j + DH].bitcast(F32),
                                d["v_rows"][part, dr, ds(b * MP, NK), :].rearrange(
                                    "m (c j g) -> m c j g", c=FC, j=HC)[:, :, j, :]).then_inc(s["v_in"], 16)

            def load_x(b):
                sp.dma_start(xn[:, :, :], d["x"][ds(b, 1)].rearrange("o (t p) f -> (o p) t f", p=P)).then_inc(s["x_in"], 16)

            def store_h(b, four):
                sp.wait_ge(s["h_done"], four)
                sp.dma_start(d["h_rows"][ds(b, 1)].rearrange("o p t f -> (o p) t f"), xn[:, :, :]).then_inc(s["h_stored"], 16)

            def store_t(b, four):
                sp.wait_ge(s["lnt_done"], four)
                sp.dma_start(d["t_rows"][ds(b, 1)].rearrange("o p c n -> (o p) c n"), hout[:, :, :]).then_inc(s["t_stored"], 16)

            def step(b, par, last):
                if not last:
                    sp.wait_ge(s["xl_done"], 4 * b + 4)
                    load_first(b + 1)
                    sp.wait_ge(s["adj_step"], 5 * b + 5)
                    load_adj(b + 1)
                if not (isinstance(b, int) and b == 1):
                    store_t(b - 2, 4 * b - 4)
                sp.wait_ge(s["att_mm"], 8 * b)
                load_v(b)
                store_h(b - 1, 4 * b)
                sp.wait_ge(s["h_stored"], 16 * b)
                sp.wait_ge(s["ln_done"], 4 * b)
                load_x(b)
                if not last:
                    sp.wait_ge(s["sc_ready"], 4 * b + 4)
                    load_m(b + 1)

            load_adj(0)
            load_m(0)
            for c in range(FC):
                for k, dst in enumerate((gcol, bcol)):
                    sp.dma_start(dst[:, c, :], d["gb_rows"][:, k, c * P:(c + 1) * P].rearrange("b p -> p b"),
                                 allow_slow_non_contiguous=True).then_inc(s["gb_in"], 16)
            sp.wait_ge(s["set_up"], 4)
            load_v(0)
            load_x(0)
            sp.wait_ge(s["xl_done"], 4)
            load_first(1)
            sp.wait_ge(s["adj_step"], 5)
            load_adj(1)
            sp.wait_ge(s["sc_ready"], 4)
            load_m(1)
            steps(sp, step)
            store_t(B - 2, 4 * B - 4)
            store_h(B - 1, 4 * B)
            store_t(B - 1, 4 * B)
            sp.wait_ge(s["h_stored"], 16 * B)
            sp.wait_ge(s["t_stored"], 16 * B)

        @block.gpsimd
        def _(pool):
            nc.gpsimd.memset(onesr[:, :].bitcast(F32), 1.0).then_inc(s["set_up"], 1)
            nc.gpsimd.memset(ones64[:, :].bitcast(F32), 1.0).then_inc(s["set_up"], 1)
            nc.gpsimd.memset(mhalf[:, :], -0.5).then_inc(s["set_up"], 1)

            def front(b):
                pool.wait_ge(s["sf_ready"], 4 * b)
                for f in range(FC):
                    pool.wait_ge(s["xh_done"], 4 * b + f + 1)
                    nc.gpsimd.tensor_tensor(xl[:, f, :], xraw[:, f, :], xh[:, f, :].bitcast(F32),
                                            ALU.subtract).then_inc(s["xl_done"], 1)

            def label_products(b):
                pool.wait_ge(s["adjf_done"], b + 1)
                nc.gpsimd.tensor_tensor(adjw[:, :, :], adjw[:, :, :], t["wbias"][:, :].unsqueeze(1).broadcast_to(
                    [P, NT * 2 * NK, L]), ALU.mult).then_inc(s["adjw_done"], 1)

            def softmax(b, has_former):
                for i in range(NT + 2):
                    if i == 1 and has_former:
                        back(b - 1)
                    if i < NT:
                        pool.wait_ge(s["mult_done"], 4 * b + i + 1)
                        nc.gpsimd.tensor_tensor(e[:, i], e[:, i], heads(cadd[:, i]), ALU.add).then_inc(s["add_done"], 1)
                    if i >= 2:
                        pool.wait_ge(s["rc_done"], 4 * b + i - 1)
                        pool.wait_ge(s["exp_done"], 4 * b + i - 1)
                        v = e[:, i - 2].rearrange("p e h k -> p (e h) k")
                        nc.gpsimd.tensor_tensor(v, v, keys(rc[:, i - 2]), ALU.mult).then_inc(s["w_done"], 1)

            def back(b):
                pool.wait_ge(s["ve_done"], 2 * b + 2)
                nc.gpsimd.tensor_tensor(rstd[:, :], ve[:, :], mhalf[:, :], ALU.pow).then_inc(s["rstd_done"], 1)

            def step(b, par, last):
                if not last:
                    front(b + 1)
                softmax(b, True)
                if not last:
                    label_products(b + 1)

            pool.wait_ge(s["set_up"], 3)
            front(0)
            nc.gpsimd.memset(vdiag[:, :, :, :, :].bitcast(F32), 0.0).then_inc(s["set_up"], 1)
            label_products(0)
            front(1)
            softmax(0, False)
            label_products(1)
            steps(pool, step)
            back(B - 1)

        @block.scalar
        def _(act):
            def hi_chunk(b, f):
                if f == 0:
                    act.wait_ge(t["x_t_in"], 16 * b + 16)
                    act.wait_ge(s["sf_ready"], 4 * b)
                nc.scalar.activation(xh[:, f, :], xraw[:, f, :], ACT.Copy).then_inc(s["xh_done"], 1)

            def self_features(b, par):
                act.wait_ge(s["att_done"], 4 * b - 4 if not isinstance(b, int) else max(4 * b - 4, 0))
                for o in range(FC):
                    act.wait_ge(s["sf_ready"], 4 * b + o + 1)
                    nc.scalar.activation(sf2[:, par, o, :], bank[:, SFB[o], :], ACT.Identity,
                                         bias=t["bself"][:, o:o + 1]).then_inc(s["sf_done"], 1)

            def normalise(b):
                act.wait_ge(s["lnt_ready"], 4 * b)
                act.wait_ge(s["rstd_done"], b + 1)
                act.wait_ge(s["nmr_done"], b + 1)
                for i in range(NT):
                    nc.scalar.activation(ln[:, i, :], xn[:, i, :], ACT.Identity, bias=nmr[:, i:i + 1],
                                         scale=rstd[:, i:i + 1]).then_inc(s["ln_done"], 1)

            def labels_float(b):
                act.wait_ge(s["adj_in"], 16 * b + 16)
                act.wait_ge(s["adj_step"], 5 * b)
                nc.scalar.activation(adjw[:, :, :], adj[:, :, :], ACT.Copy).then_inc(s["adjf_done"], 1)

            def exps(b):
                for i in range(NT):
                    act.wait_ge(s["sub_done"], 4 * b + i + 1)
                    nc.scalar.activation(e[:, i], e[:, i], ACT.Exp).then_inc(s["exp_done"], 1)

            def hi_weights(b, i):
                act.wait_ge(s["wtr_ready"], 8 * b + i + 1)
                if i >= 1:
                    act.wait_ge(s["att_mm"], 8 * b + i - 1)
                nc.scalar.activation(wth[:, i % 2, :], bank[0:CK, 6 + i % 2, :], ACT.Copy).then_inc(s["wh_done"], 1)

            def scale_ln(b, f):
                if f == 0:
                    act.wait_ge(s["gb_in"], 16 * 2 * FC)
                    act.wait_ge(s["t_stored"], 16 * b)
                act.wait_ge(s["lnt_ready"], 4 * b + f + 1)
                nc.scalar.activation(hout[:, f, :], bank[:, 2 + f, :], ACT.Identity,
                                     bias=bcol[:, f, ds(b, 1)], scale=gcol[:, f, ds(b, 1)]).then_inc(s["lnt_done"], 1)

            def step(b, par, last):
                self_features(b, par)
                for i in range(2 * FC):
                    hi_weights(b - 1, i)
                    if i < FC:
                        if not last:
                            hi_chunk(b + 1, i)
                    elif not (isinstance(b, int) and b == 1):
                        scale_ln(b - 2, i - FC)
                normalise(b - 1)
                exps(b)
                if not last:
                    labels_float(b + 1)

            for f in range(FC):
                hi_chunk(0, f)
            labels_float(0)
            self_features(0, 0)
            for f in range(FC):
                hi_chunk(1, f)
            exps(0)
            labels_float(1)
            steps(act, step)
            for i in range(2 * FC):
                hi_weights(B - 1, i)
                if i >= FC:
                    scale_ln(B - 2, i - FC)
            normalise(B - 1)
            for f in range(FC):
                scale_ln(B - 1, f)

        @block.vector
        def _(dve):
            def nonzero_rows(b):
                dve.wait_ge(s["rs_ready"], b + 1)
                dve.wait_ge(s["sf_ready"], 4 * b)
                nc.vector.tensor_scalar(z[:, :], bank[0:64, 1, :], 0.0, t["hot"][:, ds(b, 1)],
                                        ALU.not_equal, ALU.mult).then_inc(s["z_done"], 1)

            def labels(b):
                dve.wait_ge(s["adj_in"], 16 * b + 16)
                dve.wait_ge(s["w_done"], 4 * b)
                flat = "p t e k -> p (t e k)"
                nc.vector.tensor_reduce(cnt[:].rearrange(flat), adj[:, :, :], AX, ALU.add).then_inc(s["adj_step"], 1)
                dve.wait_ge(s["adjw_done"], b + 1)
                nc.vector.tensor_reduce(vb[:].rearrange(flat), adjw[:, :, :], AX, ALU.add).then_inc(s["adj_step"], 1)
                dve.wait_ge(s["adj_step"], 5 * b + 1)
                nc.vector.tensor_scalar(mask[:].rearrange(flat), cnt[:].rearrange(flat), 0.0, None,
                                        ALU.is_gt).then_inc(s["adj_step"], 1)
                nc.vector.tensor_scalar(blocked[:].rearrange(flat), cnt[:].rearrange(flat), 0.0, NEG,
                                        ALU.is_le, ALU.mult).then_inc(s["adj_step"], 1)
                dve.wait_ge(s["adj_step"], 5 * b + 4)
                nc.vector.scalar_tensor_tensor(cadd[:].rearrange(flat), vb[:].rearrange(flat), t["bbias"][:, 0:1],
                                               blocked[:].rearrange(flat), ALU.add, ALU.add).then_inc(s["adj_step"], 1)

            def softmax(b, has_former):
                dve.wait_ge(s["adj_step"], 5 * b + 5)
                dve.wait_ge(s["wtr_ready"], 8 * b)
                for i in range(NT + 2):
                    if i < NT:
                        dve.wait_ge(s["sc_ready"], 4 * b + i + 1)
                        sc = bank[:, 2 + 2 * (i % 2):4 + 2 * (i % 2), 0:HK].rearrange("p e (h k) -> p e h k", h=H)
                        nc.vector.tensor_tensor(e[:, i], sc, heads(mask[:, i]), ALU.mult).then_inc(s["mult_done"], 1)
                    if i == 0 and has_former:
                        residual_ln(b - 1)
                    if 1 <= i <= NT:
                        v = e[:, i - 1].rearrange("p e h k -> p (e h) k")
                        dve.wait_ge(s["add_done"], 4 * b + i)
                        nc.vector.tensor_reduce(mx[:, i - 1], v, AX, ALU.max).then_inc(s["mx_done"], 1)
                        dve.wait_ge(s["mx_done"], 4 * b + i)
                        nc.vector.tensor_tensor(v, v, keys(mx[:, i - 1]), ALU.subtract).then_inc(s["sub_done"], 1)
                    if i >= 2:
                        v = e[:, i - 2].rearrange("p e h k -> p (e h) k")
                        dve.wait_ge(s["exp_done"], 4 * b + i - 1)
                        nc.vector.tensor_reduce(sm[:, i - 2], v, AX, ALU.add).then_inc(s["sum_done"], 1)
                        dve.wait_ge(s["sum_done"], 4 * b + i - 1)
                        nc.vector.reciprocal(rc[:, i - 2], sm[:, i - 2]).then_inc(s["rc_done"], 1)

            def attention(b, par):
                dve.wait_ge(s["sf_done"], 4 * b + 4)
                dve.wait_ge(s["back_ready"], 4 * b)
                for i in range(2 * FC + 1):
                    if i < 2 * FC:
                        dve.wait_ge(s["wh_done"], 8 * b + i + 1)
                        nc.vector.tensor_tensor(wtl[:, i % 2, :], bank[0:CK, 6 + i % 2, :],
                                                wth[:, i % 2, :].bitcast(F32), ALU.subtract).then_inc(s["wl_done"], 1)
                    if i >= 2 and i % 2 == 0:
                        c = i // 2 - 1
                        dve.wait_ge(s["att_mm"], 8 * b + 2 * c + 2)
                        nc.vector.scalar_tensor_tensor(ot[:, c, :], bank[:, (c + 1) % 2, :], t["boutc"][:, c:c + 1],
                                                       sf2[:, par, c, :], ALU.add, ALU.add).then_inc(s["att_done"], 1)

            def residual_ln(b):
                dve.wait_ge(s["x_in"], 16 * b + 16)
                for i in range(NT):
                    dve.wait_ge(s["back_ready"], 4 * b + i + 1)
                    nc.vector.scalar_tensor_tensor(xn[:, i, :], bank[:, 6 + i % 2, :], 0.0, xn[:, i, :],
                                                   ALU.max, ALU.add).then_inc(s["h_done"], 1)
                for i in range(NT):
                    dve.wait_ge(s["h_done"], 4 * b + i + 1)
                    if i:
                        dve.wait_ge(s["st_done"], 4 * b + i)
                    nc.vector.bn_stats(st[:, i, :], xn[:, i, :]).then_inc(s["st_done"], 1)
                    if i:
                        nc.vector.bn_aggr(mv[:, i - 1, :], st[:, i - 1, :]).then_inc(s["mv_done"], 1)
                dve.wait_ge(s["st_done"], 4 * b + NT)
                dve.wait_ge(s["mv_done"], 4 * b + NT - 1)
                nc.vector.tensor_scalar(ve[:, 0:NT - 1], mv[:, 0:NT - 1, 1], EPS, None, ALU.add).then_inc(s["ve_done"], 1)
                nc.vector.bn_aggr(mv[:, NT - 1, :], st[:, NT - 1, :]).then_inc(s["mv_done"], 1)
                dve.wait_ge(s["mv_done"], 4 * b + NT)
                nc.vector.tensor_scalar(ve[:, NT - 1:NT], mv[:, NT - 1:NT, 1], EPS, None, ALU.add).then_inc(s["ve_done"], 1)
                dve.wait_ge(s["rstd_done"], b + 1)
                nc.vector.scalar_tensor_tensor(nmr[:, :], mv[:, :, 0], -1.0, rstd[:, :],
                                               ALU.mult, ALU.mult).then_inc(s["nmr_done"], 1)

            def step(b, par, last):
                attention(b - 1, 1 - par)
                softmax(b, True)
                if not last:
                    nonzero_rows(b + 1)
                    labels(b + 1)

            nonzero_rows(0)
            labels(0)
            softmax(0, False)
            nonzero_rows(1)
            labels(1)
            steps(dve, step)
            attention(B - 1, 1)
            residual_ln(B - 1)

        @block.tensor
        def _(pe):
            def self_features(b):
                if not (isinstance(b, int) and b == 0):
                    pe.wait_ge(s["att_done"], 4 * b - 4)
                    pe.wait_ge(s["h_done"], 4 * b - 4)
                pe.wait_ge(s["xh_done"], 4 * b + 4)
                pe.wait_ge(s["xl_done"], 4 * b + 4)
                for f in range(FC):
                    nc.tensor.matmul(bank[0:64, 1, :], ones64[:, :], xh[:, f, :], start=f == 0, stop=False)
                    last = nc.tensor.matmul(bank[0:64, 1, :], ones64[:, :], xl[:, f, :],
                                            start=False, stop=f == FC - 1)
                last.then_inc(s["rs_ready"], 1)
                for o in range(FC):
                    if o == FC - 1:
                        pe.wait_ge(s["z_done"], b + 1)
                    out, col = bank[:, SFB[o], :], slice(o * P, (o + 1) * P)
                    for f in range(FC):
                        mm3(nc, out, t["w1h"][:, f, col], t["w1l"][:, f, col], xh[:, f, :], xl[:, f, :], f == 0, False)
                for o in range(FC):
                    nc.tensor.matmul(bank[:, SFB[o], :], t["sq"][:, o * P:(o + 1) * P], z[:, :],
                                     start=False, stop=True).then_inc(s["sf_ready"], 1)

            def scores(b, par, first, end):
                if first == 0:
                    pe.wait_ge(s["m_in"], 16 * b + 16)
                    pe.wait_ge(s["sf_done"], 4 * b + 4)
                    if not isinstance(b, int) or b >= 2:
                        pe.wait_ge(s["lnt_done"], 4 * b - 4)
                for i in range(first, end):
                    pe.wait_ge(s["mult_done"], 4 * b + max(i - 1, 0))
                    for dr in range(2):
                        out = bank[:, 2 + 2 * (i % 2) + dr, 0:HK]
                        for f in range(FC):
                            nc.tensor.matmul(out, sf2[:, par, f, i * P:(i + 1) * P], m[:, f, dr, :],
                                             start=f == 0, stop=False)
                        last = nc.tensor.matmul(out, onesr[:, :],
                                                t["bias_rows"][:, ds(b, 1), dr, :].rearrange("p o k -> p (o k)"),
                                                start=False, stop=True)
                    last.then_inc(s["sc_ready"], 1)

            def attention(b):
                pe.wait_ge(s["w_done"], 4 * b + 4)
                pe.wait_ge(s["v_in"], 16 * 16 * b + 16 * 16)
                pe.wait_ge(s["sf_done"], (4 * b + 8) if not isinstance(b, int) else min(4 * b + 8, 4 * B))
                for i in range(2 * FC + 1):
                    if i < 2 * FC:
                        c, dr = divmod(i, 2)
                        if i >= 2:
                            pe.wait_ge(s["wl_done"], 8 * b + i - 1)
                        for n in range(NT):
                            last = nc.tensor.transpose(
                                bank[0:CK, 6 + i % 2, n * P:(n + 1) * P],
                                e[:, n, dr, HC * c:HC * c + HC, :].rearrange("p h k -> p (h k)"), t["ident"][:, :])
                        last.then_inc(s["wtr_ready"], 1)
                    if i >= 1:
                        k = i - 1
                        c, dr = divmod(k, 2)
                        pe.wait_ge(s["wl_done"], 8 * b + k + 1)
                        if dr == 0 and c >= 2:
                            pe.wait_ge(s["att_done"], 4 * b + c - 1)
                        last = mm3(nc, bank[:, (c + 1) % 2, :], vdiag[:, 0, dr, c, :], vdiag[:, 1, dr, c, :],
                                   wth[:, k % 2, :], wtl[:, k % 2, :], dr == 0, dr == 1)
                        last.then_inc(s["att_mm"], 1)

            def back(b):
                pe.wait_ge(s["att_done"], 4 * b + 4)
                pe.wait_ge(s["wl_done"], 8 * b + 8)
                for i in range(NT):
                    if i >= 2:
                        pe.wait_ge(s["h_done"], 4 * b + i - 1)
                    for f in range(FC):
                        last = nc.tensor.transpose(bank[:, 6 + i % 2, f * P:(f + 1) * P],
                                                   ot[:, f, i * P:(i + 1) * P], t["ident"][:, :])
                    last.then_inc(s["back_ready"], 1)

            def ln_t(b, after):
                pe.wait_ge(s["ln_done"], 4 * b + 4)
                pe.wait_ge(s["mult_done"], 4 * (b + after) + 4)
                for f in range(FC):
                    for i in range(NT):
                        last = nc.tensor.transpose(bank[:, 2 + f, i * P:(i + 1) * P],
                                                   ln[:, i, f * P:(f + 1) * P], t["ident"][:, :])
                    last.then_inc(s["lnt_ready"], 1)

            def step(b, par, last):
                self_features(b)
                if not (isinstance(b, int) and b == 1):
                    ln_t(b - 2, 1)
                attention(b - 1)
                scores(b, par, 0, 1)
                back(b - 1)
                scores(b, par, 1, NT)

            pe.wait_ge(s["set_up"], 3)
            self_features(0)
            scores(0, 0, 0, NT)
            steps(pe, step)
            ln_t(B - 2, 1)
            attention(B - 1)
            back(B - 1)
            pe.wait_ge(s["lnt_done"], 4 * B - 4)
            ln_t(B - 1, 0)


def attention(nc, t, d):
    with ExitStack() as ctx:
        def sb(name, shape, dt=F32):
            return ctx.enter_context(nc.sbuf_tensor(name, shape, dt))

        traw = sb("traw", [P, FC, N])
        hh, hl = sb("hh", [P, FC, N], F32R), sb("hl", [P, FC, N], F32R)
        h = sb("h", [P, NT, D])
        qh, ql, kh, kl = (sb(n, [P, N], F32R) for n in ("qh", "ql", "kh", "kl"))
        sq, sk = sb("sq_stack", [P, 2, HC, N], F32R), sb("sk_stack", [P, 2, HC, N], F32R)
        v = sb("v", [P, 2, NT, D])
        pt = sb("pt", [P, NT, 2, N])
        oraw, den, rden, o = (sb(n, [P, N]) for n in ("oraw", "den", "rden", "o"))
        oh, ol = sb("oh", [P, FC, N], F32R), sb("ol", [P, FC, N], F32R)
        rows = sb("rows", [P, 2, D])
        bp = sb("bp", [P, D])
        bcol3, bvs = sb("bcol3", [P, 3, FC]), sb("bvs", [P, FC])
        ln = sb("ln2", [P, NT, D])
        ones32 = sb("ones32", [P, DH])
        mx = sb("mx2", [P, 2, NT, 2])
        shift = sb("shift", [P, NT, 2, 2], F32R)
        st, mv = sb("st2", [P, NT, 6]), sb("mv2", [P, NT, 2])
        ve, rstd, nmr, mhalf = (sb(n, [P, NT]) for n in ("ve2", "rstd2", "nmr2", "mhalf2"))
        bank = ctx.enter_context(nc.psum_tensor("a_bank", [P, 8, 512], F32))

        s = sems(nc, ctx, "w_in0 w_in1 w_in2 w_in3 w_hi w_lo w_lo_pool ld_c t_in h_in rows_in stq00 stq01 stq10 stq11 stk00 stk01 stk10 stk11 set_up bv_done hh_done hl_done q_ready "
                          "k_ready qh_done ql_done kh_done kl_done e_ready emax_done sh_hi sh_lo sh_ready shrow_done "
                          "et_ready exp_done pv_done den_done oraw_done rden_done o_done oh_done ol_done v_ready v_done "
                          "pj_ready hb_done h1_done st_done mv_done ve_done rstd_done nmr_done ln_done mulg_done "
                          "addb_done y_done y_out")
        stq = ((s["stq00"], s["stq01"]), (s["stq10"], s["stq11"]))
        stk = ((s["stk00"], s["stk01"]), (s["stk10"], s["stk11"]))
        STK = 16 * 6
        PAIRS = H // 2
        w_in = tuple(s["w_in%d" % k] for k in range(4))
        raw = (v[:, 0], pt[:, 0:2].rearrange("p i k n -> p (i k) n"), pt[:, 2:4].rearrange("p i k n -> p (i k) n"), v[:, 1])
        hi_lo = ((t["wqkh"][:, :, 0:D], t["wqkl"][:, :, 0:D]), (t["wqkh"][:, :, D:2 * D], t["wqkl"][:, :, D:2 * D]),
                 (t["wvh"][:, :, :], t["wvl"][:, :, :]), (t["wph"][:, :, :], t["wpl"][:, :, :]))
        block = ctx.enter_context(nc.Block())

        def ahead(b, c, k):
            return (b, c + k) if c + k < FC else (b + 1, c + k - FC)

        def next_pair(b, p, more):
            if p + 1 < PAIRS:
                return b, p + 1
            return (b + 1, 0) if more else None

        def use(b, c):
            return 2 * b + c // 2

        def first(b):
            return isinstance(b, int) and b == 0

        def batches(eng, batch):
            for b in range(3):
                batch(b, b % 2, True)
            with eng.Fori(1, B // 2 - 1) as k:
                batch(2 * k + 1, 1, True)
                batch(2 * k + 2, 0, True)
            batch(B - 1, 1, False)

        @block.sync
        def _(sp):
            sp.dma_start(bcol3[:, :, :], d["bqkc"]).then_inc(s["ld_c"], 16)
            sp.dma_start(bp[:, :], d["bp"].partition_broadcast(P)).then_inc(s["ld_c"], 16)

            def load_t(b):
                sp.dma_start(traw[:, :, :], d["t_rows"][ds(b, 1)].rearrange("o p c n -> (o p) c n")).then_inc(s["t_in"], 16)

            def load_h(b):
                sp.dma_start(h[:, :, :], d["h_rows"][ds(b, 1)].rearrange("o p t f -> (o p) t f")).then_inc(s["h_in"], 16)
                sp.dma_start(rows[:, :, :], d["gb_rows"][ds(b, 1)].rearrange("o k f -> (o k f)").partition_broadcast(P)
                             .rearrange("p (k f) -> p k f", k=2)).then_inc(s["rows_in"], 16)

            def store_y(b):
                sp.dma_start(d["out"][ds(b, 1)].rearrange("o (t p) f -> (o p) t f", p=P), ln[:, :, :]).then_inc(s["y_out"], 16)

            def stacks(c, n):
                par = c % 2
                for half in range(2):
                    for ready, src, dst, at, done in (
                            (s["qh_done"], qh, sq, (0, 2 * DH), stq), (s["ql_done"], ql, sq, (DH,), stq),
                            (s["kh_done"], kh, sk, (0, DH), stk), (s["kl_done"], kl, sk, (2 * DH,), stk)):
                        if half == 0:
                            sp.wait_ge(ready, n)
                        for r in at:
                            for j in (2 * half, 2 * half + 1):
                                sp.dma_start(dst[r:r + DH, par, j, :].bitcast(F32),
                                             src[DH * j:DH * j + DH, :].bitcast(F32)).then_inc(done[par][half], 16)

            def batch(b, bpar, more):
                for p in range(PAIRS):
                    c = p // 2
                    if p % 2 == 0 and (c < 3 or more):
                        stacks((c + 1) % FC, 4 * b + c + 2)
                    if p == 1 and more:
                        sp.wait_ge(s["hl_done"], 4 * b + 4)
                        load_t(b + 1)
                    if p == 7:
                        if first(b):
                            load_h(b)
                        else:
                            sp.wait_ge(s["y_done"], 4 * b)
                            store_y(b - 1)
                            load_h(b)

            for k in range(4):
                src = d["wqkv_t"][:, k, :] if k < 3 else d["wp_t"]
                sp.dma_start(raw[k], src.rearrange("(c p) o -> p c o", p=P)).then_inc(w_in[k], 16)
                if k == 0:
                    load_t(0)
            sp.wait_ge(s["set_up"], 4)
            stacks(0, 1)
            batches(sp, batch)
            for i in range(NT):
                sp.wait_ge(s["y_done"], 4 * (B - 1) + i + 1)
                sp.dma_start(d["out"][B - 1, i * P:(i + 1) * P, :], ln[:, i, :]).then_inc(s["y_out"], 16)
            sp.wait_ge(s["y_out"], 16 * (B - 1 + NT))

        @block.gpsimd
        def _(pool):
            def split_h(b):
                for f in range(FC):
                    pool.wait_ge(s["hh_done"], 4 * b + f + 1)
                    nc.gpsimd.tensor_tensor(hl[:, f, :], traw[:, f, :], hh[:, f, :].bitcast(F32),
                                            ALU.subtract).then_inc(s["hl_done"], 1)

            def add_bp(b):
                pool.wait_ge(s["h_in"], 16 * b + 16)
                nc.gpsimd.tensor_tensor(h[:, :, :], h[:, :, :], bp[:, :].unsqueeze(1).broadcast_to([P, NT, D]),
                                        ALU.add).then_inc(s["hb_done"], 1)

            def rsqrt(b):
                pool.wait_ge(s["ve_done"], 2 * b + 2)
                nc.gpsimd.tensor_tensor(rstd[:, :], ve[:, :], mhalf[:, :], ALU.pow).then_inc(s["rstd_done"], 1)

            def result(b, i):
                if i == 0:
                    pool.wait_ge(s["rows_in"], 16 * b + 16)
                pool.wait_ge(s["ln_done"], 4 * b + i + 1)
                nc.gpsimd.tensor_tensor(ln[:, i, :], ln[:, i, :], rows[:, 0, :], ALU.mult).then_inc(s["mulg_done"], 1)
                nc.gpsimd.tensor_tensor(h[:, i, :], h[:, i, :], rows[:, 1, :], ALU.add).then_inc(s["addb_done"], 1)
                pool.wait_ge(s["mulg_done"], 4 * b + i + 1)
                pool.wait_ge(s["addb_done"], 4 * b + i + 1)
                nc.gpsimd.tensor_tensor(ln[:, i, :], ln[:, i, :], h[:, i, :], ALU.add).then_inc(s["y_done"], 1)

            def batch(b, bpar, more):
                for p in range(PAIRS):
                    if not first(b):
                        if p == 0:
                            add_bp(b - 1)
                        if p == 3:
                            rsqrt(b - 1)
                        if p == 6:
                            result(b - 1, 0)
                            result(b - 1, 1)
                        if p == 7:
                            result(b - 1, 2)
                            result(b - 1, 3)
                    if p == 4 and more:
                        split_h(b + 1)

            split_h(0)
            pool.wait_ge(s["hl_done"], FC)
            nc.gpsimd.memset(sk[3 * DH:, :, :, :].bitcast(F32), 1.0).then_inc(s["set_up"], 1)
            pool.wait_ge(s["set_up"], 1)
            nc.gpsimd.memset(sq[3 * DH:, :, :, :].bitcast(F32), 0.0).then_inc(s["set_up"], 1)
            pool.wait_ge(s["set_up"], 2)
            nc.gpsimd.memset(ones32[:, :], 1.0).then_inc(s["set_up"], 1)
            nc.gpsimd.memset(mhalf[:, :], -0.5).then_inc(s["set_up"], 1)
            pool.wait_ge(s["set_up"], 4)
            pool.wait_ge(s["ld_c"], 32)
            pool.wait_ge(s["w_hi"], 4)
            nc.gpsimd.tensor_tensor(hi_lo[3][1], raw[3], hi_lo[3][0].bitcast(F32), ALU.subtract).then_inc(s["w_lo_pool"], 1)
            batches(pool, batch)
            add_bp(B - 1)
            rsqrt(B - 1)
            pool.wait_ge(s["rows_in"], 16 * B)
            for i in range(NT):
                pool.wait_ge(s["ln_done"], 4 * (B - 1) + i + 1)
                nc.gpsimd.tensor_tensor(h[:, i, :], h[:, i, :], rows[:, 1, :], ALU.add).then_inc(s["addb_done"], 1)

        @block.scalar
        def _(act):
            def split_h(b, f):
                if f == 0:
                    act.wait_ge(s["t_in"], 16 * b + 16)
                    act.wait_ge(s["k_ready"], 4 * b)
                nc.scalar.activation(hh[:, f, :], traw[:, f, :], ACT.Copy).then_inc(s["hh_done"], 1)

            def project(b, c, which):
                g = 4 * b + c
                if not (isinstance(b, int) and g == 0):
                    prev = (b, c - 1) if c else (b - 1, FC - 1)
                    for half in range(2):
                        act.wait_ge((stq, stk)[which][prev[1] % 2][half], STK * (use(*prev) + 1))
                act.wait_ge((s["q_ready"], s["k_ready"])[which], g + 1)
                nc.scalar.activation((qh, kh)[which][:, :], bank[:, 6 + which, :], ACT.Identity,
                                     bias=bcol3[:, which, c:c + 1]).then_inc((s["qh_done"], s["kh_done"])[which], 1)

            def values(b, vpar, i):
                if i == 0 and not first(b):
                    act.wait_ge(s["pv_done"], 32 * b - 32)
                act.wait_ge(s["v_ready"], 4 * b + i + 1)
                nc.scalar.activation(v[:, vpar, i, :], bank[:, 6 + i % 2, :], ACT.Copy).then_inc(s["v_done"], 1)

            def shift_rows(b, p):
                for k in range(2):
                    act.wait_ge(s["sh_ready"], 2 * (PAIRS * b + p) + k + 1)
                    nc.scalar.activation(sq[3 * DH:3 * DH + 2, (p // 2) % 2, 2 * (p % 2) + k, :],
                                         bank[3 * DH:3 * DH + 2, 2 + k, :], ACT.Copy).then_inc(s["shrow_done"], 1)

            def exps(b, p, i):
                G = PAIRS * b + p
                if not (isinstance(b, int) and G == 0):
                    act.wait_ge(s["pv_done"], 4 * G + i - 3)
                for k in range(2):
                    act.wait_ge(s["et_ready"], 8 * G + 2 * i + k + 1)
                    nc.scalar.activation(pt[:, i, k, :], bank[:, k, :], ACT.Exp).then_inc(s["exp_done"], 1)

            def outputs(b, p):
                G = PAIRS * b + p
                a, r = slice(64 * (p % 2), 64 * (p % 2) + 64), slice(64 - 64 * (p % 2), 128 - 64 * (p % 2))
                act.wait_ge(s["pv_done"], 4 * G + 4)
                if not (isinstance(b, int) and G < 2):
                    act.wait_ge(s["o_done"], 4 * b + p // 2)
                nc.scalar.activation(den[a, :], bank[r, 4 + p % 2, :], ACT.Copy).then_inc(s["den_done"], 1)
                nc.scalar.activation(oraw[a, :], bank[a, 4 + p % 2, :], ACT.Copy).then_inc(s["oraw_done"], 1)

            def output_hi(b, c):
                g = 4 * b + c
                act.wait_ge(s["o_done"], g + 1)
                act.wait_ge(s["pj_ready"], 4 * b)
                nc.scalar.activation(oh[:, c, :], o[:, :], ACT.Identity, bias=bvs[:, c:c + 1]).then_inc(s["oh_done"], 1)

            def normalise(b, i):
                if i == 0:
                    act.wait_ge(s["y_out"], 16 * b)
                    act.wait_ge(s["rstd_done"], b + 1)
                    act.wait_ge(s["nmr_done"], b + 1)
                nc.scalar.activation(ln[:, i, :], h[:, i, :], ACT.Identity, bias=nmr[:, i:i + 1],
                                     scale=rstd[:, i:i + 1]).then_inc(s["ln_done"], 1)

            def batch(b, bpar, more):
                for p in range(PAIRS):
                    exps(b, p, 0)
                    if p == 4 and more:
                        split_h(b + 1, 0)
                        split_h(b + 1, 1)
                    if p % 2 and p > 1:
                        output_hi(b, p // 2 - 1)
                    elif p == 1 and not first(b):
                        output_hi(b - 1, FC - 1)
                    exps(b, p, 1)
                    if p == 4 and more:
                        split_h(b + 1, 2)
                    if p:
                        outputs(b, p - 1)
                    elif not first(b):
                        outputs(b - 1, PAIRS - 1)
                    if p % 2 and (p < 4 or more):
                        project(*ahead(b, p // 2, 2), 0)
                    if p == 6 and more:
                        values(b + 1, 1 - bpar, 2)
                    exps(b, p, 2)
                    if p == 4 and more:
                        split_h(b + 1, 3)
                    if p in (5, 6) and not first(b):
                        normalise(b - 1, 2 * p - 10)
                    exps(b, p, 3)
                    if p in (5, 6) and not first(b):
                        normalise(b - 1, 2 * p - 9)
                    if next_pair(b, p, more):
                        shift_rows(*next_pair(b, p, more))
                    if p % 2 and (p < 4 or more):
                        project(*ahead(b, p // 2, 2), 1)
                    if p in (4, 6) and more:
                        for i in ((0, 1) if p == 4 else (3,)):
                            values(b + 1, 1 - bpar, i)

            act.wait_ge(s["ld_c"], 32)
            for k in range(4):
                act.wait_ge(w_in[k], 16)
                nc.scalar.activation(hi_lo[k][0], raw[k], ACT.Copy).then_inc(s["w_hi"], 1)
                if k == 0:
                    for f in range(FC):
                        split_h(0, f)
            project(0, 0, 0)
            project(0, 0, 1)
            for i in range(NT):
                values(0, 0, i)
            project(0, 1, 0)
            project(0, 1, 1)
            act.wait_ge(s["set_up"], 4)
            shift_rows(0, 0)
            act.wait_ge(s["bv_done"], 1)
            batches(act, batch)
            outputs(B - 1, PAIRS - 1)
            output_hi(B - 1, FC - 1)
            for i in range(NT):
                normalise(B - 1, i)

        @block.vector
        def _(dve):
            def lo_part(b, c, which):
                hi, lo = ((qh, ql), (kh, kl))[which]
                dve.wait_ge((s["qh_done"], s["kh_done"])[which], 4 * b + c + 1)
                nc.vector.scalar_tensor_tensor(lo[:, :], bank[:, 6 + which, :], bcol3[:, which, c:c + 1],
                                               hi[:, :].bitcast(F32), ALU.add, ALU.subtract
                                               ).then_inc((s["ql_done"], s["kl_done"])[which], 1)

            def maximum(b, p, i):
                dve.wait_ge(s["e_ready"], 8 * (PAIRS * b + p) + i + 1)
                k, n = divmod(i, NT)
                nc.vector.reduce_max(mx[:, p % 2, n, k:k + 1], bank[:, 2 + i % 2, :], AX).then_inc(s["emax_done"], 1)

            def shift_parts(b, p):
                G = PAIRS * b + p
                dve.wait_ge(s["emax_done"], 8 * G + 8)
                if not (isinstance(b, int) and G == 0):
                    dve.wait_ge(s["sh_ready"], 2 * G)
                nc.vector.tensor_scalar(shift[:, :, :, 0], mx[:, p % 2], -1.0, None, ALU.mult).then_inc(s["sh_hi"], 1)
                dve.wait_ge(s["sh_hi"], G + 1)
                nc.vector.scalar_tensor_tensor(shift[:, :, :, 1], mx[:, p % 2], -1.0, shift[:, :, :, 0].bitcast(F32),
                                               ALU.mult, ALU.subtract).then_inc(s["sh_lo"], 1)

            def quotients(b, c):
                g = 4 * b + c
                dve.wait_ge(s["den_done"], 2 * g + 2)
                nc.vector.reciprocal(rden[:, :], den[:, :]).then_inc(s["rden_done"], 1)
                dve.wait_ge(s["oraw_done"], 2 * g + 2)
                dve.wait_ge(s["rden_done"], g + 1)
                if not (isinstance(b, int) and g == 0):
                    dve.wait_ge(s["ol_done"], g)
                nc.vector.scalar_tensor_tensor(o[:, :], oraw[:, :], float(D) ** -0.5, rden[:, :],
                                               ALU.mult, ALU.mult).then_inc(s["o_done"], 1)

            def output_lo(b, c):
                dve.wait_ge(s["oh_done"], 4 * b + c + 1)
                nc.vector.scalar_tensor_tensor(ol[:, c, :], o[:, :], bvs[:, c:c + 1], oh[:, c, :].bitcast(F32),
                                               ALU.add, ALU.subtract).then_inc(s["ol_done"], 1)

            def residual(b, tiles):
                dve.wait_ge(s["hb_done"], b + 1)
                for i in tiles:
                    dve.wait_ge(s["pj_ready"], 4 * b + i + 1)
                    nc.vector.tensor_tensor(h[:, i, :], bank[:, 6 + i % 2, :], h[:, i, :], ALU.add).then_inc(s["h1_done"], 1)

            def statistics(b, tiles):
                for i in tiles:
                    dve.wait_ge(s["h1_done"], 4 * b + i + 1)
                    if i:
                        dve.wait_ge(s["st_done"], 4 * b + i)
                    nc.vector.bn_stats(st[:, i, :], h[:, i, :]).then_inc(s["st_done"], 1)
                    if i:
                        nc.vector.bn_aggr(mv[:, i - 1, :], st[:, i - 1, :]).then_inc(s["mv_done"], 1)
                if NT - 1 not in tiles:
                    return
                dve.wait_ge(s["st_done"], 4 * b + NT)
                dve.wait_ge(s["mv_done"], 4 * b + NT - 1)
                nc.vector.tensor_scalar(ve[:, 0:NT - 1], mv[:, 0:NT - 1, 1], EPS, None, ALU.add).then_inc(s["ve_done"], 1)
                nc.vector.bn_aggr(mv[:, NT - 1, :], st[:, NT - 1, :]).then_inc(s["mv_done"], 1)
                dve.wait_ge(s["mv_done"], 4 * b + NT)
                nc.vector.tensor_scalar(ve[:, NT - 1:NT], mv[:, NT - 1:NT, 1], EPS, None, ALU.add).then_inc(s["ve_done"], 1)

            def mean_term(b):
                dve.wait_ge(s["rstd_done"], b + 1)
                nc.vector.scalar_tensor_tensor(nmr[:, :], mv[:, :, 0], -1.0, rstd[:, :],
                                               ALU.mult, ALU.mult).then_inc(s["nmr_done"], 1)

            def batch(b, bpar, more):
                for p in range(PAIRS):
                    nxt = next_pair(b, p, more)
                    if nxt:
                        for i in range(5):
                            maximum(*nxt, i)
                    if p % 2 and (p < 4 or more):
                        lo_part(*ahead(b, p // 2, 2), 0)
                    if p == 2 and not first(b):
                        residual(b - 1, (2,))
                    if nxt:
                        for i in range(5, 8):
                            maximum(*nxt, i)
                        shift_parts(*nxt)
                    if p % 2 == 0 and p:
                        quotients(b, p // 2 - 1)
                    elif p == 0 and not first(b):
                        quotients(b - 1, FC - 1)
                    if p % 2 and p > 1:
                        output_lo(b, p // 2 - 1)
                    elif p == 1 and not first(b):
                        output_lo(b - 1, FC - 1)
                    if p == 3 and not first(b):
                        statistics(b - 1, (2, 3))
                    if p % 2 and (p < 4 or more):
                        lo_part(*ahead(b, p // 2, 2), 1)
                    if not first(b):
                        if p in (1, 2):
                            residual(b - 1, ((0, 1), (3,))[p - 1])
                        if p == 1:
                            statistics(b - 1, (0, 1))
                        if p == 4:
                            mean_term(b - 1)

            dve.wait_ge(s["ld_c"], 32)
            nc.vector.tensor_scalar(bvs[:, :], bcol3[:, 2, :], float(D) ** -0.5, None, ALU.mult).then_inc(s["bv_done"], 1)
            dve.wait_ge(s["bv_done"], 1)
            for k in range(3):
                dve.wait_ge(s["w_hi"], k + 1)
                nc.vector.tensor_tensor(hi_lo[k][1], raw[k], hi_lo[k][0].bitcast(F32), ALU.subtract).then_inc(s["w_lo"], 1)
            for c in range(2):
                lo_part(0, c, 0)
                lo_part(0, c, 1)
            for i in range(8):
                maximum(0, 0, i)
            shift_parts(0, 0)
            batches(dve, batch)
            quotients(B - 1, FC - 1)
            output_lo(B - 1, FC - 1)
            for i in range(NT):
                residual(B - 1, (i,))
                statistics(B - 1, (i,))
            mean_term(B - 1)
            dve.wait_ge(s["rows_in"], 16 * B)
            for i in range(NT):
                n = 4 * (B - 1) + i + 1
                dve.wait_ge(s["ln_done"], n)
                nc.vector.tensor_tensor(ln[:, i, :], ln[:, i, :], rows[:, 0, :], ALU.mult).then_inc(s["mulg_done"], 1)
                dve.wait_ge(s["mulg_done"], n)
                dve.wait_ge(s["addb_done"], n)
                nc.vector.tensor_tensor(ln[:, i, :], ln[:, i, :], h[:, i, :], ALU.add).then_inc(s["y_done"], 1)

        @block.tensor
        def _(pe):
            ALL, PART1, PART2 = range(FC), range(FC // 2), range(FC // 2, FC)

            def project_wait(b, c, which):
                g = 4 * b + c
                if isinstance(b, int) and b == 0 and c < 2:
                    pe.wait_ge(s["hl_done"], FC)
                    if c == 1:
                        pe.wait_ge(s["v_done"], 4)
                elif c < 2:
                    pe.wait_ge(s["hl_done"], 4 * b + 4)
                    pe.wait_ge(s["v_done"], 4 * b + 2 * c + 2)
                elif c == 3 and not first(b):
                    pe.wait_ge(s["h1_done"], 4 * b)
                else:
                    pe.wait_ge((s["ql_done"], s["kl_done"])[which], g)

            def project(b, c, which, part=ALL):
                if part[0] == 0:
                    project_wait(b, c, which)
                col = slice(which * D + c * P, which * D + (c + 1) * P)
                for f in part:
                    last = mm3(nc, bank[:, 6 + which, :], t["wqkh"][:, f, col], t["wqkl"][:, f, col],
                               hh[:, f, :], hl[:, f, :], f == 0, f == FC - 1)
                if part[-1] == FC - 1:
                    last.then_inc((s["q_ready"], s["k_ready"])[which], 1)

            def values(b, tiles, chunks, part=ALL):
                if part[0] == 0:
                    pe.wait_ge(s["ql_done"], chunks)
                    pe.wait_ge(s["kl_done"], chunks)
                    pe.wait_ge(s["hl_done"], 4 * b + 4)
                for i in tiles:
                    if i >= 2 and part[0] == 0:
                        pe.wait_ge(s["v_done"], 4 * b + i - 1)
                    r = slice(i * P, (i + 1) * P)
                    for f in part:
                        last = mm3(nc, bank[:, 6 + i % 2, :], hh[:, f, r], hl[:, f, r],
                                   t["wvh"][:, f, :], t["wvl"][:, f, :], f == 0, f == FC - 1)
                    if part[-1] == FC - 1:
                        last.then_inc(s["v_ready"], 1)

            def scores(b, p, i):
                G = PAIRS * b + p
                c = p // 2
                if i == 0:
                    pe.wait_ge(stq[c % 2][p % 2], STK * (use(b, c) + 1))
                    pe.wait_ge(stk[c % 2][p % 2], STK * (use(b, c) + 1))
                    if not (isinstance(b, int) and G == 0):
                        pe.wait_ge(s["shrow_done"], 2 * G)
                if i < 2:
                    pe.wait_ge(s["emax_done"], 8 * G)
                else:
                    pe.wait_ge(s["emax_done"], 8 * G + i - 1)
                k, n = divmod(i, NT)
                j = 2 * (p % 2) + k
                nc.tensor.matmul(bank[:, 2 + i % 2, :], sq[0:3 * DH, c % 2, j, n * P:(n + 1) * P],
                                 sk[0:3 * DH, c % 2, j, :], start=True, stop=True).then_inc(s["e_ready"], 1)

            def shift_t(b, p):
                pe.wait_ge(s["sh_lo"], PAIRS * b + p + 1)
                for k in range(2):
                    for n in range(NT):
                        last = nc.tensor.matmul(bank[3 * DH:3 * DH + 2, 2 + k, n * P:(n + 1) * P],
                                                shift[:, n, k, :].bitcast(F32), t["ident"][:, :],
                                                start=True, stop=True)
                    last.then_inc(s["sh_ready"], 1)

            def scores_t(b, p, i):
                G = PAIRS * b + p
                c = p // 2
                for k in range(2):
                    if i == 0:
                        pe.wait_ge(s["shrow_done"], 2 * G + k + 1)
                        pe.wait_ge(s["exp_done"], 8 * G)
                    else:
                        pe.wait_ge(s["exp_done"], 8 * G + 2 * i + k - 1)
                    j = 2 * (p % 2) + k
                    nc.tensor.matmul(bank[:, k, :], sk[0:3 * DH + 2, c % 2, j, i * P:(i + 1) * P],
                                     sq[0:3 * DH + 2, c % 2, j, :], start=True, stop=True).then_inc(s["et_ready"], 1)

            def weighted(b, bpar, p, i):
                G = PAIRS * b + p
                if i == 0:
                    if not (isinstance(b, int) and G < 2):
                        pe.wait_ge(s["oraw_done"], G - 1)
                    pe.wait_ge(s["v_done"], 4 * b + 4)
                pe.wait_ge(s["exp_done"], 8 * G + 2 * i + 2)
                for k in range(2):
                    w = pt[:, i, k, :]
                    a, r = 64 * (p % 2) + DH * k, 64 - 64 * (p % 2) + DH * k
                    nc.tensor.matmul(bank[a:a + DH, 4 + p % 2, :], v[:, bpar, i, (2 * p + k) * DH:(2 * p + k + 1) * DH],
                                     w, start=i == 0, stop=i == NT - 1)
                    last = nc.tensor.matmul(bank[r:r + DH, 4 + p % 2, :], ones32[:, :], w,
                                            start=i == 0, stop=i == NT - 1)
                last.then_inc(s["pv_done"], 1)

            def output_projection(b, tiles, chunks, part=ALL):
                if part[0] == 0:
                    pe.wait_ge(s["ol_done"], 4 * b + 4)
                for i in tiles:
                    if part[0] == 0:
                        if i < 2:
                            pe.wait_ge((s["ql_done"], s["kl_done"])[i], chunks)
                        else:
                            pe.wait_ge(s["h1_done"], 4 * b + i - 1)
                    r = slice(i * P, (i + 1) * P)
                    for c in part:
                        last = mm3(nc, bank[:, 6 + i % 2, :], oh[:, c, r], ol[:, c, r],
                                   t["wph"][:, c, :], t["wpl"][:, c, :], c == 0, c == FC - 1)
                    if part[-1] == FC - 1:
                        last.then_inc(s["pj_ready"], 1)

            def held(b, p, more):
                if p % 2:
                    return p < 4 or more
                return (p == 2 and not first(b)) or (p in (4, 6) and more)

            def batch(b, bpar, more):
                for p in range(PAIRS):
                    nxt = next_pair(b, p, more)
                    qk = p % 2 and (p < 4 or more)

                    def maxima(*tiles):
                        for i in tiles:
                            if nxt:
                                scores(*nxt, i)

                    scores_t(b, p, 0)
                    if p and held(b, p - 1, more):
                        weighted(b, bpar, p - 1, 3)
                    if p == 0 and not first(b):
                        weighted(b - 1, 1 - bpar, PAIRS - 1, 3)
                    maxima(0, 1)
                    scores_t(b, p, 1)
                    weighted(b, bpar, p, 0)
                    if p == 1:
                        project(*ahead(b, 0, 2), 0)
                    maxima(2, 3)
                    if qk and p > 1:
                        project(*ahead(b, p // 2, 2), 0)
                        maxima(4)
                    if p == 2 and not first(b):
                        output_projection(b - 1, (2,), 4 * b + 3)
                        maxima(4)
                    if p == 6 and more:
                        values(b + 1, (2,), 4 * b + 5)
                        maxima(4)
                    spread = not ((qk and p > 1) or (p == 2 and not first(b)) or (p == 6 and more))
                    scores_t(b, p, 2)
                    maxima(4 if spread else 5)
                    weighted(b, bpar, p, 1)
                    maxima(5 if spread else 6)
                    scores_t(b, p, 3)
                    maxima(6 if spread else 7)
                    if spread and not held(b, p, more):
                        maxima(7)
                    weighted(b, bpar, p, 2)
                    if spread and held(b, p, more):
                        maxima(7)
                    for part in (PART1, PART2):
                        if qk:
                            project(*ahead(b, p // 2, 2), 1, part)
                        if p == 2 and not first(b):
                            output_projection(b - 1, (3,), 4 * b + 3, part)
                        if p in (4, 6) and more:
                            values(b + 1, (0 if p == 4 else 3,), 4 * b + p // 2 + 2, part)
                        if part == PART1 and nxt:
                            shift_t(*nxt)
                    if p == 1 and not first(b):
                        output_projection(b - 1, (0, 1), 4 * b + 3)
                    if p == 4 and more:
                        values(b + 1, (1,), 4 * b + 4)
                    if not held(b, p, more):
                        weighted(b, bpar, p, 3)

            pe.wait_ge(s["w_lo"], 1)
            project(0, 0, 0)
            pe.wait_ge(s["w_lo"], 2)
            project(0, 0, 1)
            pe.wait_ge(s["w_lo"], 3)
            values(0, range(NT), 1)
            project(0, 1, 0)
            project(0, 1, 1)
            pe.wait_ge(s["set_up"], 4)
            for i in range(8):
                scores(0, 0, i)
            shift_t(0, 0)
            pe.wait_ge(s["w_lo_pool"], 1)
            batches(pe, batch)
            output_projection(B - 1, range(NT), 4 * B)


def program(nc, d):
    d["gb_rows"] = nc.dram_tensor("gb_rows", [B, 2, D], F32, kind="Internal").ap()
    d["v_rows"] = nc.dram_tensor("v_rows", [2, 2, B * MP, D], F32, kind="Internal").ap()
    d["m_rows"] = nc.dram_tensor("m_rows", [B, P, FC, 2, HK], F32, kind="Internal").ap()
    d["h_rows"] = nc.dram_tensor("h_rows", [B, P, NT, D], F32, kind="Internal").ap()
    d["t_rows"] = nc.dram_tensor("t_rows", [B, P, FC, N], F32, kind="Internal").ap()
    t = {}
    with ExitStack() as outer:
        t["ident"] = outer.enter_context(nc.sbuf_tensor("ident", [P, P], F32))
        with ExitStack() as ctx:
            def sb(name, shape, dt=F32):
                return ctx.enter_context(nc.sbuf_tensor(name, shape, dt))

            t["w1h"], t["w1l"] = sb("w1h", [P, FC, D], F32R), sb("w1l", [P, FC, D], F32R)
            t["sq"] = sb("sq", [64, D], F32R)
            t["hot"] = sb("hot", [64, B])
            t["bself"], t["boutc"] = sb("bself", [P, FC]), sb("boutc", [P, FC])
            t["wbias"], t["bbias"] = sb("wbias", [P, L]), sb("bbias", [P, 1])
            t["xraw"] = sb("xraw", [P, FC, N])
            t["x_t_in"] = outer.enter_context(nc.semaphore("x_t_in"))
            t["bias_rows"] = sb("bias_rows", [64, B, 2, HK], F32R)
            prologue(nc, t, d)
            graph(nc, t, d)
        with ExitStack() as ctx:
            def wt(name, width):
                return ctx.enter_context(nc.sbuf_tensor(name, [P, FC, width], F32R))

            t["wqkh"], t["wqkl"] = wt("wqkh", 2 * D), wt("wqkl", 2 * D)
            t["wvh"], t["wvl"], t["wph"], t["wpl"] = wt("wvh", D), wt("wvl", D), wt("wph", D), wt("wpl", D)
            attention(nc, t, d)


def kernel(**inputs):
    import numpy as np
    import concourse.bacc as bacc
    from concourse import mybir as mb
    from concourse.bass_utils import run_bass_kernel_spmd

    a = {k: np.asarray(v) for k, v in inputs.items()}

    def g(k):
        return a["L0_cond_" + k]

    def f(k):
        return a["L1_cond_" + k]

    adj = a["mask_BxSxSx11_ik0"]
    x = a["x"]
    bqkv = f("bqkv").reshape(D, 3).T

    def columns(v):
        v = v.reshape(v.shape[:-1] + (FC, P))
        return np.moveaxis(v, -1, 0)

    def twice(v):
        out = np.zeros(v.shape[:-1] + (64,), v.dtype)
        out[..., 0:v.shape[-1]] = v
        out[..., 32:32 + v.shape[-1]] = v
        return out

    adj2 = np.stack([adj[:, :, :NK, :], adj[:, :NK, :, :].transpose(0, 2, 1, 3)], axis=2)
    hot = np.zeros((64, B), np.float32)
    for b in range(B):
        hot[b, b] = hot[32 + b, b] = 1.0
    hot20 = np.repeat(hot[:, :, None], MP, axis=2).reshape(64, B * MP)
    wqkv = f("Wqkv").reshape(D, 3, D)
    arrays = {
        "x": x,
        "x_t": x.transpose(0, 2, 1).reshape(B, FC, P, N).transpose(0, 2, 1, 3),
        "adj": adj2.reshape(B, NT, P, 2 * NK, L).transpose(0, 2, 1, 3, 4).reshape(B, P, NT * 2 * NK, L),
        "cond64": twice(a["cond_1024"].T.reshape(FC, P, B).transpose(1, 0, 2)),
        "wself_t": g("W_self").T,
        "b_self": columns(g("b_self")),
        "w_bias": g("w_bias"),
        "b_bias": g("b_bias").reshape(1),
        "wq": g("Wq"),
        "bq64": twice(columns(g("bq"))[..., None]),
        "wk_t": g("Wk").transpose(0, 2, 1),
        "bk": columns(g("bk")),
        "wout_t": g("Wout").reshape(2, D, D).transpose(0, 2, 1),
        "bout": columns(g("bout")),
        "ln_g": f("ln_g"), "ln_b": f("ln_b"), "bg": f("bg"), "bb": f("bb"),
        "wg_t": f("Wg").T, "wb_t": f("Wb").T,
        "wqkv_t": wqkv.transpose(2, 1, 0),
        "bqkc": columns(bqkv),
        "wp_t": f("Wp").T,
        "bp": f("bp"),
        "ident": np.eye(P, dtype=np.float32),
        "hot": hot,
        "hot20": hot20,
    }
    nc = bacc.Bacc("TRN2", target_bir_lowering=False, num_devices=1)
    feed, drams = {}, {}
    for name, v in arrays.items():
        v = np.ascontiguousarray(v)
        feed["in_" + name] = v
        drams[name] = nc.dram_tensor("in_" + name, v.shape, mb.dt.from_np(v.dtype), kind="ExternalInput").ap()
    d = dict(drams)
    d["out"] = nc.dram_tensor("out_y", (B, N, D), mb.dt.float32, kind="ExternalOutput").ap()
    program(nc, d)
    r = run_bass_kernel_spmd(nc, [feed], core_ids=[0])
    return r.results[0]["out_y"]
```
